# Optimizing a Trainium2 kernel written in Bass

```python
import numpy as np
import jax
import jax.numpy as jnp

def _softmax(x, axis=-1):
    return jax.nn.softmax(x, axis=axis)

def _gelu(x):
    return jax.nn.gelu(x, approximate=True)

def _silu(x):
    return jax.nn.silu(x)

def _sigmoid(x):
    return jax.nn.sigmoid(x)

def _layernorm(x, axis=-1, eps=1e-05):
    m = jnp.mean(x, axis=axis, keepdims=True)
    v = jnp.var(x, axis=axis, keepdims=True)
    return (x - m) / jnp.sqrt(v + eps)

def _scatter_add(tgt, idx, src, axis=0):
    return tgt.at[idx].add(src)

def _segment_sum(src, seg, n):
    return jax.ops.segment_sum(src, seg, n)
kernel_name = 'mk_xattn_ffn_d2_seqx_r8_e5431f'

def setup_inputs(seed: int=0):
    np.random.seed(seed)
    _w = jnp.asarray

    def _rec_inputs():
        import jax
        import jax.numpy as jnp
        _rk = jax.random.key(seed)
        x = -0.000125 + 0.9999 * jax.random.normal(jax.random.fold_in(_rk, 1), (4, 256, 256), jnp.float32)
        _lenS = 256 - jax.random.randint(jax.random.fold_in(_rk, 7), (4,), 0, max(1, 256 // 4) + 1, jnp.int32)
        _lenS2 = 256 - jax.random.randint(jax.random.fold_in(_rk, 8), (4,), 0, max(1, 256 // 4) + 1, jnp.int32)
        _ctx_2048P = jax.random.normal(jax.random.fold_in(_rk, 11), (4, 16, 256), jnp.float32)
        _ctx_2048c = jax.random.dirichlet(jax.random.fold_in(_rk, 511), 0.3 * jnp.ones((16,), jnp.float32), (4, 256))
        _ctx_2048t = jnp.einsum('bsk,bkd->bsd', _ctx_2048c, _ctx_2048P)
        _ctx_2048t = _ctx_2048t * jax.lax.rsqrt(jnp.mean(jnp.square(_ctx_2048t)) + 1e-12) * 0.953939
        ctx_2048 = -1.52775e-05 + 0.999936 * (_ctx_2048t + 0.3 * jax.random.normal(jax.random.fold_in(_rk, 611), (4, 256, 256), jnp.float32))
        return (x, ctx_2048)
    x, ctx_2048 = _rec_inputs()

    def _L0_xattn_setup():
        import jax, jax.numpy as jnp
        import numpy as np
        B, S, D, H = (4, 512, 256, 16)
        HD = D // H
        key = jax.random.key(seed)
        ks = jax.random.split(key, 12)
        sc = 1.0 / np.sqrt(D)
        inp = {'q': jax.random.normal(ks[0], (B, S, D), jnp.float32), 'k': jax.random.normal(ks[1], (B, S, D), jnp.float32), 'v': jax.random.normal(ks[2], (B, S, D), jnp.float32), 'Wq': jax.random.normal(ks[3], (D, D), jnp.float32) * sc, 'bq': jnp.zeros((D,), jnp.float32), 'Wk': jax.random.normal(ks[4], (D, D), jnp.float32) * sc, 'bk': jnp.zeros((D,), jnp.float32), 'Wv': jax.random.normal(ks[5], (D, D), jnp.float32) * sc, 'bv': jnp.zeros((D,), jnp.float32), 'Wo': jax.random.normal(ks[6], (D, D), jnp.float32) * sc, 'bo': jnp.zeros((D,), jnp.float32)}
        return inp
    _L0_xattn_all = _L0_xattn_setup()
    _L0_xattn_in = {k: v for k, v in _L0_xattn_all.items() if k in ('Wq', 'bq', 'Wk', 'bk', 'Wv', 'bv', 'Wo', 'bo')}
    del _L0_xattn_all

    def _L0_ffn_setup():
        import jax, jax.numpy as jnp
        import numpy as np
        H = 256
        NH = 16
        NOPE = 128
        ROPE = 64
        VD = 128
        QHD = NOPE + ROPE
        E = 16
        I = 176
        TOPK = 4
        NSH = 2
        SHI = I * NSH
        EPS = 1e-06
        B, S = (2, 128)

        def rmsnorm(x, w):
            return x * jax.lax.rsqrt(jnp.mean(x * x, axis=-1, keepdims=True) + EPS) * w
        key = jax.random.key(seed)
        ks = jax.random.split(key, 12)
        sd = lambda fan_in: 1.0 / np.sqrt(fan_in)
        return {'hidden_states': jax.random.normal(ks[0], (B, S, H), jnp.float32), 'positions': jnp.broadcast_to(jnp.arange(S, dtype=jnp.int32), (B, S)), 'ln1_w': jnp.ones((H,), jnp.float32), 'ln2_w': jnp.ones((H,), jnp.float32), 'q_w': jax.random.normal(ks[1], (NH * QHD, H), jnp.float32) * sd(H), 'kv_w': jax.random.normal(ks[2], (NH * (NOPE + VD) + ROPE, H), jnp.float32) * sd(H), 'o_w': jax.random.normal(ks[3], (H, NH * VD), jnp.float32) * sd(NH * VD), 'gate_w': jax.random.normal(ks[4], (E, H), jnp.float32) * sd(H), 'w1': jax.random.normal(ks[5], (E, 2 * I, H), jnp.float32) * sd(H), 'w2': jax.random.normal(ks[6], (E, H, I), jnp.float32) * sd(I), 'sh_gu_w': jax.random.normal(ks[7], (2 * SHI, H), jnp.float32) * sd(H), 'sh_down_w': jax.random.normal(ks[8], (H, SHI), jnp.float32) * sd(SHI)}
    _L0_ffn_all = _L0_ffn_setup()
    _L0_ffn_in = {k: v for k, v in _L0_ffn_all.items() if k in ('positions', 'ln1_w', 'ln2_w', 'q_w', 'kv_w', 'o_w', 'gate_w', 'w1', 'w2', 'sh_gu_w', 'sh_down_w')}
    del _L0_ffn_all

    def _L1_xattn_setup():
        import jax, jax.numpy as jnp
        import numpy as np
        D_MODEL = 256
        NUM_HEADS = 16
        HEAD_DIM = D_MODEL // NUM_HEADS

        def _fq_sym(x, axis):
            s = jnp.max(jnp.abs(x), axis=axis, keepdims=True) / 127.0
            s = jnp.maximum(s, 1e-08)
            q = jnp.clip(jnp.round(x / s), -127.0, 127.0) * s
            return x + jax.lax.stop_gradient(q - x)

        def _fq_unsigned(x, axis):
            s = jnp.max(x, axis=axis, keepdims=True) / 255.0
            s = jnp.maximum(s, 1e-08)
            q = jnp.clip(jnp.round(x / s), 0.0, 255.0) * s
            return x + jax.lax.stop_gradient(q - x)
        key = jax.random.key(seed)
        ks = jax.random.split(key, 8)
        B, N, M, C = (2, 256, 64, D_MODEL)
        return {'x': jax.random.normal(ks[0], (B, N, C), jnp.float32), 'cond': jax.random.normal(ks[1], (B, M, C), jnp.float32), 'Wq': jax.random.normal(ks[2], (C, C), jnp.float32) * 0.02, 'bq': jnp.zeros((C,), jnp.float32), 'Wkv': jax.random.normal(ks[3], (C, 2 * C), jnp.float32) * 0.02, 'bkv': jnp.zeros((2 * C,), jnp.float32), 'Wp': jax.random.normal(ks[4], (C, C), jnp.float32) * 0.02, 'bp': jnp.zeros((C,), jnp.float32)}
    _L1_xattn_all = _L1_xattn_setup()
    _L1_xattn_in = {k: v for k, v in _L1_xattn_all.items() if k in ('Wq', 'bq', 'Wkv', 'bkv', 'Wp', 'bp')}
    del _L1_xattn_all

    def _L1_ffn_setup():
        import jax, jax.numpy as jnp
        import numpy as np
        NUM_EXPERTS = 32
        TOP_K = 8
        THRESHOLD = 0.8
        HIDDEN = 256
        INTER = 96
        key = jax.random.key(seed)
        k1, k2, k3, k4 = jax.random.split(key, 4)
        hidden_states = jax.random.normal(k1, (2, 128, HIDDEN), jnp.float32)
        gate_weight = jax.random.normal(k2, (NUM_EXPERTS, HIDDEN), jnp.float32) * 0.02
        gate_up_proj = jax.random.normal(k3, (NUM_EXPERTS, 2 * INTER, HIDDEN), jnp.float32) * 0.02
        down_proj = jax.random.normal(k4, (NUM_EXPERTS, HIDDEN, INTER), jnp.float32) * 0.02
        return {'hidden_states': hidden_states, 'gate_weight': gate_weight, 'gate_up_proj': gate_up_proj, 'down_proj': down_proj}
    _L1_ffn_all = _L1_ffn_setup()
    _L1_ffn_in = {k: v for k, v in _L1_ffn_all.items() if k in ('gate_weight', 'gate_up_proj', 'down_proj')}
    del _L1_ffn_all
    return {'x': x, 'ctx_2048': ctx_2048, 'L0_xattn_Wq': _L0_xattn_in['Wq'], 'L0_xattn_bq': _L0_xattn_in['bq'], 'L0_xattn_Wk': _L0_xattn_in['Wk'], 'L0_xattn_bk': _L0_xattn_in['bk'], 'L0_xattn_Wv': _L0_xattn_in['Wv'], 'L0_xattn_bv': _L0_xattn_in['bv'], 'L0_xattn_Wo': _L0_xattn_in['Wo'], 'L0_xattn_bo': _L0_xattn_in['bo'], 'L0_ffn_positions': _L0_ffn_in['positions'], 'L0_ffn_ln1_w': _L0_ffn_in['ln1_w'], 'L0_ffn_ln2_w': _L0_ffn_in['ln2_w'], 'L0_ffn_q_w': _L0_ffn_in['q_w'], 'L0_ffn_kv_w': _L0_ffn_in['kv_w'], 'L0_ffn_o_w': _L0_ffn_in['o_w'], 'L0_ffn_gate_w': _L0_ffn_in['gate_w'], 'L0_ffn_w1': _L0_ffn_in['w1'], 'L0_ffn_w2': _L0_ffn_in['w2'], 'L0_ffn_sh_gu_w': _L0_ffn_in['sh_gu_w'], 'L0_ffn_sh_down_w': _L0_ffn_in['sh_down_w'], 'L1_xattn_Wq': _L1_xattn_in['Wq'], 'L1_xattn_bq': _L1_xattn_in['bq'], 'L1_xattn_Wkv': _L1_xattn_in['Wkv'], 'L1_xattn_bkv': _L1_xattn_in['bkv'], 'L1_xattn_Wp': _L1_xattn_in['Wp'], 'L1_xattn_bp': _L1_xattn_in['bp'], 'L1_ffn_gate_weight': _L1_ffn_in['gate_weight'], 'L1_ffn_gate_up_proj': _L1_ffn_in['gate_up_proj'], 'L1_ffn_down_proj': _L1_ffn_in['down_proj']}

def reference(x, ctx_2048, L0_xattn_Wq, L0_xattn_bq, L0_xattn_Wk, L0_xattn_bk, L0_xattn_Wv, L0_xattn_bv, L0_xattn_Wo, L0_xattn_bo, L0_ffn_positions, L0_ffn_ln1_w, L0_ffn_ln2_w, L0_ffn_q_w, L0_ffn_kv_w, L0_ffn_o_w, L0_ffn_gate_w, L0_ffn_w1, L0_ffn_w2, L0_ffn_sh_gu_w, L0_ffn_sh_down_w, L1_xattn_Wq, L1_xattn_bq, L1_xattn_Wkv, L1_xattn_bkv, L1_xattn_Wp, L1_xattn_bp, L1_ffn_gate_weight, L1_ffn_gate_up_proj, L1_ffn_down_proj):
    import jax
    import jax.numpy as jnp

    def _L0_xattn_ref(q, k, v, Wq, bq, Wk, bk, Wv, bv, Wo, bo):
        import jax, jax.numpy as jnp
        import numpy as np
        B, S, D, H = (4, 512, 256, 16)
        HD = D // H
        bs, sl, nf = q.shape
        Q = (q @ Wq.T + bq).reshape(bs, sl, H, HD)
        K = (k @ Wk.T + bk).reshape(bs, sl, H, HD)
        V = (v @ Wv.T + bv).reshape(bs, sl, H, HD)
        score = jnp.einsum('bshd,bsgd->bshg', Q, K)
        weight = jax.nn.softmax(score, axis=-1)
        attn = jnp.einsum('bshg,bsgd->bshd', weight, V).reshape(bs, sl, nf)
        return attn @ Wo.T + bo

    def _L0_ffn_ref(hidden_states, positions, ln1_w, ln2_w, q_w, kv_w, o_w, gate_w, w1, w2, sh_gu_w, sh_down_w):
        import jax, jax.numpy as jnp
        import numpy as np
        H = 256
        NH = 16
        NOPE = 128
        ROPE = 64
        VD = 128
        QHD = NOPE + ROPE
        E = 16
        I = 176
        TOPK = 4
        NSH = 2
        SHI = I * NSH
        EPS = 1e-06
        B, S = (2, 128)

        def rmsnorm(x, w):
            return x * jax.lax.rsqrt(jnp.mean(x * x, axis=-1, keepdims=True) + EPS) * w
        b, s, h = hidden_states.shape
        x = rmsnorm(hidden_states, ln1_w)
        q = jnp.einsum('bsh,dh->bsd', x, q_w).reshape(b, s, NH, QHD)[..., :NOPE]
        kv = jnp.einsum('bsh,dh->bsd', x, kv_w)
        k = kv[..., :NH * NOPE].reshape(b, s, NH, NOPE)
        v = kv[..., NH * NOPE:NH * (NOPE + VD)].reshape(b, s, NH, VD)
        scale = QHD ** (-0.5)
        scores = jnp.einsum('bqnd,bknd->bnqk', q, k) * scale
        causal = jnp.tril(jnp.ones((s, s), bool))
        scores = jnp.where(causal, scores, -1000000000.0)
        p = jax.nn.softmax(scores, axis=-1)
        attn = jnp.einsum('bnqk,bknd->bqnd', p, v).reshape(b, s, NH * VD)
        attn_out = jnp.einsum('bsd,hd->bsh', attn, o_w)
        hid = hidden_states + attn_out
        x2 = rmsnorm(hid, ln2_w).reshape(-1, h)
        logits = x2 @ gate_w.T
        probs = jax.nn.softmax(logits, axis=-1)
        top_w, top_i = jax.lax.top_k(probs, TOPK)
        top_w = top_w / jnp.sum(top_w, axis=-1, keepdims=True)
        wfull = jnp.sum(jax.nn.one_hot(top_i, E, dtype=x2.dtype) * top_w[..., None], axis=1)
        gu = jnp.einsum('th,eih->tei', x2, w1)
        g, u = (gu[..., :I], gu[..., I:])
        act = jax.nn.silu(g) * u
        down = jnp.einsum('tei,ehi->teh', act, w2)
        routed = jnp.einsum('te,teh->th', wfull, down)
        sgu = x2 @ sh_gu_w.T
        sg, su = (sgu[..., :SHI], sgu[..., SHI:])
        shared = jax.nn.silu(sg) * su @ sh_down_w.T
        return hid + (routed + shared).reshape(b, s, h)

    def _L1_xattn_ref(x, cond, Wq, bq, Wkv, bkv, Wp, bp):
        import jax, jax.numpy as jnp
        import numpy as np
        D_MODEL = 256
        NUM_HEADS = 16
        HEAD_DIM = D_MODEL // NUM_HEADS

        def _fq_sym(x, axis):
            s = jnp.max(jnp.abs(x), axis=axis, keepdims=True) / 127.0
            s = jnp.maximum(s, 1e-08)
            q = jnp.clip(jnp.round(x / s), -127.0, 127.0) * s
            return x + jax.lax.stop_gradient(q - x)

        def _fq_unsigned(x, axis):
            s = jnp.max(x, axis=axis, keepdims=True) / 255.0
            s = jnp.maximum(s, 1e-08)
            q = jnp.clip(jnp.round(x / s), 0.0, 255.0) * s
            return x + jax.lax.stop_gradient(q - x)
        B, N, C = x.shape
        H, hd = (NUM_HEADS, HEAD_DIM)
        q = (x @ Wq + bq).reshape(1, B * N, H, hd)
        kv = (cond @ Wkv + bkv).reshape(1, -1, 2, H, hd)
        k, v = (kv[:, :, 0], kv[:, :, 1])
        scale = 1.0 / np.sqrt(hd).astype(np.float32)
        q = jnp.transpose(q * scale, (0, 2, 1, 3))
        k = jnp.transpose(k, (0, 2, 1, 3))
        v = jnp.transpose(v, (0, 2, 1, 3))
        q = _fq_sym(q, axis=-1)
        k = _fq_sym(k, axis=-1)
        v = _fq_sym(v, axis=2)
        attn = jnp.einsum('bhqd,bhkd->bhqk', q, k)
        attn = jax.nn.softmax(attn.astype(jnp.float32), axis=-1)
        attn = _fq_unsigned(attn, axis=-1)
        out = jnp.einsum('bhqk,bhkd->bhqd', attn, v)
        out = jnp.transpose(out, (0, 2, 1, 3)).reshape(B, N, C)
        return out @ Wp + bp

    def _L1_ffn_ref(hidden_states, gate_weight, gate_up_proj, down_proj):
        import jax, jax.numpy as jnp
        import numpy as np
        NUM_EXPERTS = 32
        TOP_K = 8
        THRESHOLD = 0.8
        HIDDEN = 256
        INTER = 96
        B, S, H = hidden_states.shape
        x = hidden_states.reshape(-1, H)
        logits = x @ gate_weight.T
        probs = jax.nn.softmax(logits.astype(jnp.float32), axis=-1).astype(logits.dtype)
        top_vals, top_idx = jax.lax.top_k(probs, TOP_K)
        renorm = top_vals / jnp.clip(jnp.sum(top_vals, axis=-1, keepdims=True), 1e-12)
        cum = jnp.cumsum(renorm, axis=-1)
        num_keep = jnp.minimum(jnp.sum((cum < THRESHOLD).astype(jnp.int32), axis=-1) + 1, TOP_K)
        active = jnp.arange(TOP_K)[None, :] < num_keep[:, None]
        rw = top_vals * active.astype(top_vals.dtype)
        rw = rw / jnp.clip(jnp.sum(rw, axis=-1, keepdims=True), 1e-12)
        combine = jnp.sum(jax.nn.one_hot(top_idx, NUM_EXPERTS, dtype=rw.dtype) * rw[..., None], axis=1)

        def body(acc, params):
            w_gu, w_d, ce = params
            gu = x @ w_gu.T
            g, u = jnp.split(gu, 2, axis=-1)
            h = jax.nn.silu(g) * u
            return (acc + h @ w_d.T * ce[:, None], None)
        out, _ = jax.lax.scan(body, jnp.zeros_like(x), (gate_up_proj, down_proj, combine.T))
        return out.reshape(B, S, H)
    x = x + _L0_xattn_ref(_layernorm(x, axis=-1), ctx_2048, ctx_2048, L0_xattn_Wq, L0_xattn_bq, L0_xattn_Wk, L0_xattn_bk, L0_xattn_Wv, L0_xattn_bv, L0_xattn_Wo, L0_xattn_bo)
    x = x + _L0_ffn_ref(_layernorm(x, axis=-1), L0_ffn_positions, L0_ffn_ln1_w, L0_ffn_ln2_w, L0_ffn_q_w, L0_ffn_kv_w, L0_ffn_o_w, L0_ffn_gate_w, L0_ffn_w1, L0_ffn_w2, L0_ffn_sh_gu_w, L0_ffn_sh_down_w)
    x = x + _L1_xattn_ref(_layernorm(x, axis=-1), ctx_2048, L1_xattn_Wq, L1_xattn_bq, L1_xattn_Wkv, L1_xattn_bkv, L1_xattn_Wp, L1_xattn_bp)
    x = x + _L1_ffn_ref(_layernorm(x, axis=-1), L1_ffn_gate_weight, L1_ffn_gate_up_proj, L1_ffn_down_proj)
    return x

_drawn_inputs = setup_inputs


def setup_inputs(seed=0):
    import zlib

    import numpy as np

    out = dict(_drawn_inputs(seed))
    spreads = {'L0_xattn_bq': (0.0, 0.1),
     'L0_xattn_bk': (0.0, 0.1),
     'L0_xattn_bv': (0.0, 0.1),
     'L0_xattn_bo': (0.0, 0.1),
     'L0_ffn_ln1_w': (1.0, 0.2),
     'L0_ffn_ln2_w': (1.0, 0.2),
     'L1_xattn_bq': (0.0, 0.8),
     'L1_xattn_bkv': (0.0, 0.659),
     'L1_xattn_bp': (0.0, 0.1)}
    factors = {'L1_xattn_Wq': 8.0,
     'L1_xattn_Wkv': 5.639,
     'L1_xattn_Wp': 3.264,
     'L1_ffn_gate_weight': 8.0,
     'L1_ffn_gate_up_proj': 8.0,
     'L1_ffn_down_proj': 8.0}
    for name, (base, spread) in spreads.items():
        noise = np.random.default_rng([zlib.crc32(name.encode()), seed]).standard_normal(out[name].shape)
        drawn = base * np.exp(spread * noise) if base else spread * noise
        out[name] = jnp.asarray(drawn.astype(out[name].dtype))
    for name, factor in factors.items():
        out[name] = (out[name] * factor).astype(out[name].dtype)
    return out
```

```python
from contextlib import ExitStack

import numpy as np
import concourse.bass as bass
from concourse import mybir
from concourse.alu_op_type import AluOpType as ALU

F32 = mybir.dt.float32
F32R = mybir.dt.float32r
BF16 = mybir.dt.bfloat16
I16 = mybir.dt.int16
ACT = mybir.ActivationFunctionType
AX = mybir.AxisListType

P = 128
B, S, D = 4, 256, 256
T = B * S
NT = T // P
NC = D // P
H, HD = 16, 16
HALF = 512
NHALF = T // HALF


class Counter:

    def __init__(self, engine, sem):
        self.engine, self.sem, self.n = engine, sem, 0

    def after(self, instruction):
        self.n += 1
        instruction.then_inc(self.sem, 1)
        self.engine.wait_ge(self.sem, self.n)


class Core:

    def __init__(self, nc, ctx, dram):
        self.nc, self.ctx, self.dram = nc, ctx, dram
        self.stages = {}

    def sb(self, name, shape, dtype=F32, ctx=None):
        return (ctx or self.ctx).enter_context(self.nc.sbuf_tensor(name, shape, dtype))

    def ps(self, name, shape, dtype=F32, ctx=None):
        return (ctx or self.ctx).enter_context(self.nc.psum_tensor(name, shape, dtype))

    def sem(self, name):
        return self.ctx.enter_context(self.nc.semaphore(name))

    def shared_sems(self, stage, names):
        if stage not in self.stages:
            self.stages[stage] = ([self.sem(f"{stage}_{n}") for n in names], 0)
        sems, runs = self.stages[stage]
        self.stages[stage] = (sems, runs + 1)
        return sems, runs * NT

    def column(self, tensor, t):
        return tensor[:, t:t + 1] if isinstance(t, int) else tensor[:, bass.ds(t, 1)]


def f32(ap):
    return ap.bitcast(F32)


def load_constants(c):
    nc = c.nc
    loaded = c.sem("const_loaded")
    prepared = c.sem("const_prepared")
    with nc.Block() as block:

        @block.sync
        def _(sp):
            sp.dma_start(c.x[:], c.dram["x"]).then_inc(loaded, 16)
            sp.dma_start(c.ident[:], c.dram["ident"]).then_inc(loaded, 16)
            sp.dma_start(c.vecs[:], c.dram["vecs"]).then_inc(loaded, 16)
            sp.wait_ge(loaded, 48)

        @block.vector
        def _(dve):
            dve.wait_ge(loaded, 48)
            nc.vector.tensor_copy(c.ident_bf[:], c.ident[:]).then_inc(prepared, 1)
            nc.vector.memset(c.ones[:], 1.0).then_inc(prepared, 1)
            dve.wait_ge(prepared, 2)


def row_statistics(c, name, src, eps=1e-5, second_eps=None):
    nc = c.nc
    stats_done, root_done, own = c.sem(name + "_var"), c.sem(name + "_root"), c.sem(name + "_own")

    with nc.Block() as block:

        @block.vector
        def _(dve):
            step = Counter(dve, own)
            for t in range(NT):
                ins = nc.vector.bn_stats(c.bn[:, t, :], src[:, t, :])
            step.after(ins)
            for t in range(NT):
                ins = nc.vector.bn_aggr(c.mean_var[:, t, :], c.bn[:, t, :])
            step.after(ins)
            step.after(nc.vector.tensor_scalar(c.stat[:, 0, :], c.mean_var[:, :, 1], eps, None, ALU.add))
            inverse_root(c, dve, step, stats_done, root_done, 1, c.stat[:, 0, :], c.rstd[:])
            step.after(nc.vector.scalar_tensor_tensor(out=c.shift[:], in0=c.mean_var[:, :, 0], scalar=-1.0,
                                                      in1=c.rstd[:], op0=ALU.mult, op1=ALU.mult))
            if second_eps is not None:
                step.after(nc.vector.tensor_tensor(c.stat[:, 0, :], c.mean_var[:, :, 1], c.rstd[:], ALU.mult))
                step.after(nc.vector.tensor_tensor(c.stat[:, 0, :], c.stat[:, 0, :], c.rstd[:], ALU.mult))
                step.after(nc.vector.tensor_scalar(c.stat[:, 0, :], c.stat[:, 0, :], second_eps, None, ALU.add))
                inverse_root(c, dve, step, stats_done, root_done, 2, c.stat[:, 0, :], c.rms[:])

        @block.scalar
        def _(act):
            for n in range(1 if second_eps is None else 2):
                act.wait_ge(stats_done, n + 1)
                nc.scalar.activation(c.stat[:, 1, :], c.stat[:, 0, :], ACT.Sqrt).then_inc(root_done, 1)


def inverse_root(c, dve, step, ready, root_done, n, value, out):
    nc = c.nc
    nc.vector.tensor_copy(c.stat[:, 2, :], value).then_inc(ready, 1)
    dve.wait_ge(ready, n)
    dve.wait_ge(root_done, n)
    r, u = c.stat[:, 1, :], c.stat[:, 3, :]
    step.after(nc.vector.reciprocal(r, r))
    step.after(nc.vector.tensor_tensor(u, r, r, ALU.mult))
    step.after(nc.vector.tensor_tensor(u, u, value, ALU.mult))
    step.after(nc.vector.tensor_scalar(u, u, -0.5, 1.5, ALU.mult, ALU.add))
    step.after(nc.vector.tensor_tensor(out, r, u, ALU.mult))



POOL_HEADS = 5


def head_attention(c):
    nc = c.nc
    row_statistics(c, "ha_norm", c.x)
    with ExitStack() as ctx:
        w = c.sb("ha_w", [P, NC, 4 * D], ctx=ctx)
        bias = c.sb("ha_bias", [1, 4 * D], ctx=ctx)
        xn = [c.sb(f"ha_xn{k}", [P, D], ctx=ctx) for k in range(2)]
        xT = [c.sb(f"ha_xT{k}", [P, NC, P], ctx=ctx) for k in range(2)]
        cT = [c.sb(f"ha_cT{k}", [P, NC, P], ctx=ctx) for k in range(2)]
        q = [c.sb(f"ha_q{k}", [P, H, HD], ctx=ctx) for k in range(2)]
        kk = [c.sb(f"ha_k{k}", [P, H, HD], ctx=ctx) for k in range(2)]
        vT = [c.sb(f"ha_v{k}", [P, HD, H], ctx=ctx) for k in range(2)]
        prod = c.sb("ha_prod", [P, H, H * HD], ctx=ctx)
        sc = c.sb("ha_sc", [P, H, H], ctx=ctx)
        ex = c.sb("ha_ex", [P, H, H], ctx=ctx)
        red = c.sb("ha_red", [P, H], ctx=ctx)
        at = [c.sb(f"ha_at{k}", [P, H, HD], ctx=ctx) for k in range(2)]
        aT = c.sb("ha_aT", [P, NC, P], ctx=ctx)
        psT = c.ps("ha_psT", [P, NC * P], ctx=ctx)
        psQ = c.ps("ha_psQ", [P, D], ctx=ctx)
        psKV = c.ps("ha_psKV", [P, 2 * D], ctx=ctx)
        psA = c.ps("ha_psA", [P, NC * P], ctx=ctx)
        psO = c.ps("ha_psO", [P, D], ctx=ctx)
        w_loaded = c.sem("ha_w_loaded")
        ctx_loaded = [c.sem(f"ha_ctx_loaded{k}") for k in range(2)]
        normed = c.sem("ha_normed")
        x_turned = c.sem("ha_x_turned")
        xT_ready = c.sem("ha_xT_ready")
        qkv_done = c.sem("ha_qkv_done")
        qkv_ready = c.sem("ha_qkv_ready")
        qk_pool = c.sem("ha_qk_pool")
        sub_done = c.sem("ha_sub_done")
        exp_done = c.sem("ha_exp_done")
        prob_ready = c.sem("ha_prob_ready")
        pv_pool = c.sem("ha_pv_pool")
        at_ready = c.sem("ha_at_ready")
        at_turned = c.sem("ha_at_turned")
        aT_ready = c.sem("ha_aT_ready")
        out_done = c.sem("ha_out_done")
        own = c.sem("ha_own")
        added = c.sem("ha_added")

        def tiles(engine, front, back):
            front(0, 0)
            front(1, 1)
            back(0, 0, True)
            with engine.Fori(0, (NT - 2) // 2) as i:
                for j in range(2):
                    front(i * 2 + (2 + j), j)
                    back(i * 2 + (1 + j), 1 - j, False)
            back(NT - 1, (NT - 1) % 2, False)

        with nc.Block() as block:

            @block.sync
            def _(sp):
                sp.dma_start(w[:], c.dram["ha_w"]).then_inc(w_loaded, 16)
                sp.dma_start(bias[:], c.dram["ha_bias"]).then_inc(w_loaded, 16)

                def front(t, k):
                    if not (isinstance(t, int) and t < 2):
                        sp.wait_ge(qkv_done, t - 1)
                    sp.dma_start(cT[k][:], c.dram["ctx_tiles"][t]).then_inc(ctx_loaded[k], 16)

                tiles(sp, front, lambda t, k, first: None)

            @block.scalar
            def _(act):
                def front(t, k):
                    nc.scalar.activation(xn[k][:], c.x[:, t, :], ACT.Identity, scale=c.column(c.rstd, t),
                                         bias=c.column(c.shift, t)).then_inc(normed, 1)
                    act.wait_ge(x_turned, t + 1)
                    nc.scalar.activation(xT[k][:].rearrange("p c t -> p (c t)"), psT[:],
                                         ACT.Copy).then_inc(xT_ready, 1)
                    act.wait_ge(qkv_done, t + 1)
                    if not (isinstance(t, int) and t < 2):
                        act.wait_ge(at_ready, t - 1)
                    nc.scalar.activation(q[k][:].rearrange("p h d -> p (h d)"), psQ[:], ACT.Copy)
                    nc.scalar.activation(kk[k][:].rearrange("p h d -> p (h d)"), psKV[:, 0:D], ACT.Copy)
                    nc.scalar.activation(vT[k][:].rearrange("p d g -> p g d"),
                                         psKV[:, D:2 * D].rearrange("p (g d) -> p g d", g=H),
                                         ACT.Copy).then_inc(qkv_ready, 1)

                def back(t, k, first):
                    act.wait_ge(sub_done, t + 1)
                    nc.scalar.activation(ex[:], sc[:], ACT.Exp).then_inc(exp_done, 1)
                    act.wait_ge(at_turned, t + 1)
                    nc.scalar.activation(aT[:].rearrange("p c t -> p (c t)"), psA[:],
                                         ACT.Copy).then_inc(aT_ready, 1)

                tiles(act, front, back)

            @block.tensor
            def _(pe):
                pe.wait_ge(w_loaded, 32)

                def front(t, k):
                    pe.wait_ge(normed, t + 1)
                    pe.wait_ge(xT_ready, t)
                    for n in range(NC):
                        ins = nc.tensor.transpose(psT[:, n * P:(n + 1) * P], xn[k][:, n * P:(n + 1) * P], c.ident[:])
                    ins.then_inc(x_turned, 1)
                    pe.wait_ge(xT_ready, t + 1)
                    pe.wait_ge(ctx_loaded[k], slot_loads(t, k))
                    pe.wait_ge(qkv_ready, t)
                    nc.tensor.matmul(psQ[:], c.ones[0:1, 0:P], bias[:, 0:D], start=True, stop=False)
                    for n in range(NC):
                        nc.tensor.matmul(psQ[:], xT[k][:, n, :], w[:, n, 0:D], start=False, stop=(n == NC - 1))
                    nc.tensor.matmul(psKV[:], c.ones[0:1, 0:P], bias[:, D:3 * D], start=True, stop=False)
                    for n in range(NC):
                        ins = nc.tensor.matmul(psKV[:], cT[k][:, n, :], w[:, n, D:3 * D], start=False,
                                               stop=(n == NC - 1))
                    ins.then_inc(qkv_done, 1)

                def slot_loads(t, k):
                    return (t - k) // 2 * 16 + 16 if isinstance(t, int) else (t - k) * 8 + 16

                def back(t, k, first):
                    pe.wait_ge(at_ready, t + 1)
                    for n in range(NC):
                        ins = nc.tensor.transpose(psA[:, n * P:(n + 1) * P],
                                                  at[k][:, 8 * n:8 * n + 8, :].rearrange("p h d -> p (h d)"),
                                                  c.ident[:])
                    ins.then_inc(at_turned, 1)
                    pe.wait_ge(aT_ready, t + 1)
                    nc.tensor.matmul(psO[:], c.ones[0:1, 0:P], bias[:, 3 * D:4 * D], start=True, stop=False)
                    for n in range(NC):
                        ins = nc.tensor.matmul(psO[:], aT[:, n, :], w[:, n, 3 * D:4 * D], start=False,
                                               stop=(n == NC - 1))
                    ins.then_inc(out_done, 1)

                tiles(pe, front, back)

            def products(engine, h0, h1, k, left, right):
                return engine.tensor_tensor(prod[:, h0:h1, :].rearrange("p h (x y) -> p h x y", x=HD),
                                            left, right, ALU.mult)

            def qk_operands(h0, h1, k):
                n = h1 - h0
                return (q[k][:, h0:h1, :].unsqueeze(2).to_broadcast([P, n, H, HD]),
                        kk[k][:].unsqueeze(1).to_broadcast([P, n, H, HD]))

            def pv_operands(h0, h1, k):
                n = h1 - h0
                return (ex[:, h0:h1, :].unsqueeze(2).to_broadcast([P, n, HD, H]),
                        vT[k][:].unsqueeze(1).to_broadcast([P, n, HD, H]))

            @block.gpsimd
            def _(pool):
                def back(t, k, first):
                    pool.wait_ge(qkv_ready, t + 1)
                    pool.wait_ge(at_ready, t)
                    products(nc.gpsimd, 0, POOL_HEADS, k, *qk_operands(0, POOL_HEADS, k)).then_inc(qk_pool, 1)
                    pool.wait_ge(prob_ready, t + 1)
                    products(nc.gpsimd, 0, POOL_HEADS, k, *pv_operands(0, POOL_HEADS, k)).then_inc(pv_pool, 1)

                tiles(pool, lambda t, k: None, back)

            @block.vector
            def _(dve):
                def residual(t):
                    nc.vector.tensor_tensor(c.x[:, t, :], c.x[:, t, :], psO[:], ALU.add).then_inc(added, 1)

                def back(t, k, first):
                    steps = 0

                    def after(ins):
                        nonlocal steps
                        steps += 1
                        ins.then_inc(own, 1)
                        dve.wait_ge(own, t * 6 + steps)

                    dve.wait_ge(qkv_ready, t + 1)
                    dve.wait_ge(at_ready, t)
                    products(nc.vector, POOL_HEADS, H, k, *qk_operands(POOL_HEADS, H, k)).then_inc(own, 1)
                    steps += 1
                    if not first:
                        dve.wait_ge(out_done, t)
                        residual(t - 1)
                    dve.wait_ge(own, t * 6 + steps)
                    dve.wait_ge(qk_pool, t + 1)
                    after(nc.vector.tensor_reduce(sc[:], prod[:].rearrange("p h (g d) -> p h g d", g=H), AX.X, ALU.add))
                    after(nc.vector.tensor_reduce(red[:], sc[:], AX.X, ALU.max))
                    nc.vector.tensor_tensor(sc[:], sc[:], red[:].unsqueeze(2).to_broadcast([P, H, H]),
                                            ALU.subtract).then_inc(sub_done, 1)
                    dve.wait_ge(exp_done, t + 1)
                    after(nc.vector.tensor_reduce(red[:], ex[:], AX.X, ALU.add))
                    after(nc.vector.reciprocal(red[:], red[:]))
                    nc.vector.tensor_tensor(ex[:], ex[:], red[:].unsqueeze(2).to_broadcast([P, H, H]),
                                            ALU.mult).then_inc(prob_ready, 1)
                    dve.wait_ge(prob_ready, t + 1)
                    after(products(nc.vector, POOL_HEADS, H, k, *pv_operands(POOL_HEADS, H, k)))
                    dve.wait_ge(pv_pool, t + 1)
                    nc.vector.tensor_reduce(at[k][:], prod[:].rearrange("p h (d g) -> p h d g", d=HD), AX.X,
                                            ALU.add).then_inc(at_ready, 1)

                tiles(dve, lambda t, k: None, back)
                dve.wait_ge(out_done, NT)
                residual(NT - 1)



def causal_block(c):
    nc = c.nc
    row_statistics(c, "cb_norm", c.x, second_eps=1e-6)
    scaled, tile_step = c.sem("cb_scaled"), c.sem("cb_tile_step")
    with nc.Block() as block:

        @block.vector
        def _(dve):
            nc.vector.tensor_tensor(c.scale2[:], c.rstd[:], c.rms[:], ALU.mult).then_inc(scaled, 1)
            nc.vector.tensor_tensor(c.shift2[:], c.shift[:], c.rms[:], ALU.mult).then_inc(scaled, 1)
            dve.wait_ge(scaled, 2)

    def keep_normed(pool, t):
        nc.gpsimd.tensor_scalar(c.hid[:, t, :], c.x[:, t, :], c.column(c.rstd, t), c.column(c.shift, t),
                                ALU.mult, ALU.add).then_inc(tile_step, 1)

    norm_to_feature_major(c, "cb_turn", c.x, c.scale2, c.shift2, gain=0, tile_work=keep_normed)
    causal_attention(c)
    add_feature_major(c, "cb_out", c.out_t, c.hid)


PASSES = ((0, 0), (0, 1), (1, 0))


def in_pairs(engine, n, body, peel_last=False):
    straight = n % 2 or (2 if peel_last else 0)
    body(0, 0)
    body(1, 1)
    with engine.Fori(0, (n - 2 - straight) // 2) as i:
        for j in range(2):
            body(i * 2 + (2 + j), j)
    for t in range(n - straight, n):
        body(t, t % 2)


def loads_of_slot(t, k):
    return ((t - k) // 2 + 1) * 16 if isinstance(t, int) else (t - k) * 8 + 16


def norm_to_feature_major(c, name, src, scale, shift, gain=None, tile_work=None):
    nc = c.nc
    with ExitStack() as ctx:
        z = [c.sb(f"{name}_z{k}", [P, D], ctx=ctx) for k in range(2)]
        ps = [c.ps(f"{name}_ps{k}", [P, NC, P], ctx=ctx) for k in range(2)]
        (normed, turned, hi_done, lo_done), start = c.shared_sems("norm", ("normed", "turned", "hi", "lo"))

        def token(t):
            return slice(t * P, (t + 1) * P) if isinstance(t, int) else bass.ds(t * P, P)

        with nc.Block() as block:

            @block.scalar
            def _(act):
                def split_hi(t, k):
                    act.wait_ge(turned, start + t + 1)
                    for n in range(NC):
                        g = 1.0 if gain is None else c.vecs[:, gain + n:gain + n + 1]
                        ins = nc.scalar.activation(c.fT[0][:, n, token(t)], ps[k][:, n, :], ACT.Copy, scale=g)
                    ins.then_inc(hi_done, 1)

                def body(t, k):
                    nc.scalar.activation(z[k][:], src[:, t, :], ACT.Identity, scale=c.column(scale, t),
                                         bias=0.0 if shift is None else c.column(shift, t)).then_inc(normed, 1)
                    if not (isinstance(t, int) and t == 0):
                        split_hi(t - 1, 1 - k)

                in_pairs(act, NT, body)
                split_hi(NT - 1, 1)

            @block.tensor
            def _(pe):
                def body(t, k):
                    pe.wait_ge(normed, start + t + 1)
                    if not (isinstance(t, int) and t < 2):
                        pe.wait_ge(lo_done, start + t - 1)
                    for n in range(NC):
                        ins = nc.tensor.transpose(ps[k][:, n, :], z[k][:, n * P:(n + 1) * P], c.ident[:])
                    ins.then_inc(turned, 1)

                in_pairs(pe, NT, body)

            @block.vector
            def _(dve):
                def body(t, k):
                    dve.wait_ge(hi_done, start + t + 1)
                    for n in range(NC):
                        hi, lo = f32(c.fT[0][:, n, token(t)]), c.fT[1][:, n, token(t)]
                        if gain is None:
                            ins = nc.vector.tensor_tensor(lo, ps[k][:, n, :], hi, ALU.subtract)
                        else:
                            ins = nc.vector.scalar_tensor_tensor(
                                out=lo, in0=ps[k][:, n, :], scalar=c.vecs[:, gain + n:gain + n + 1], in1=hi,
                                op0=ALU.mult, op1=ALU.subtract)
                    ins.then_inc(lo_done, 1)

                in_pairs(dve, NT, body)

            if tile_work:

                @block.gpsimd
                def _(pool):
                    for t in range(NT):
                        tile_work(pool, t)


def add_feature_major(c, name, acc, dst, extra=None):
    nc = c.nc
    with ExitStack() as ctx:
        ps = [c.ps(f"{name}_ps{k}", [P, D], ctx=ctx) for k in range(4)]
        (turned, added), start = c.shared_sems("add", ("turned", "added"))
        base = c.sem(name + "_base") if extra is not None else None
        with nc.Block() as block:

            @block.tensor
            def _(pe):
                for t in range(NT):
                    if t >= 4:
                        pe.wait_ge(added, start + t - 3)
                    for n in range(NC):
                        ins = nc.tensor.transpose(ps[t % 4][:, n * P:(n + 1) * P], acc[:, n, t * P:(t + 1) * P],
                                                  c.ident[:])
                    ins.then_inc(turned, 1)

            if extra is not None:

                @block.gpsimd
                def _(pool):
                    for t in range(NT):
                        nc.gpsimd.tensor_tensor(dst[:, t, :], dst[:, t, :], extra[:, t, :], ALU.add).then_inc(base, 1)

            @block.vector
            def _(dve):
                for t in range(NT):
                    dve.wait_ge(turned, start + t + 1)
                    if extra is not None:
                        dve.wait_ge(base, t + 1)
                    nc.vector.tensor_tensor(dst[:, t, :], dst[:, t, :], ps[t % 4][:], ALU.add).then_inc(added, 1)



NH, DH, QHD = 16, 128, 192
PAIRS = NH // 2
QSCALE = float(QHD) ** -0.5


def causal_attention(c):
    nc = c.nc
    with ExitStack() as ctx:
        raw = c.sb("ca_raw", [P, 3, NC, 2 * DH], ctx=ctx)
        w = [c.sb(f"ca_w{x}", [P, 3, NC, 2 * DH], F32R, ctx=ctx) for x in range(2)]
        raw_o = c.sb("ca_raw_o", [DH, 2, D], ctx=ctx)
        wo = [c.sb(f"ca_wo{x}", [DH, 2, D], F32R, ctx=ctx) for x in range(2)]
        qk = [[c.sb(f"ca_{m}{x}", [DH, 2, T], F32R, ctx=ctx) for x in range(2)] for m in "qk"]
        v = [c.sb(f"ca_v{x}", [P, NT, 2 * DH], F32R, ctx=ctx) for x in range(2)]
        e = [c.sb(f"ca_e{k}", [P, 3 * P], ctx=ctx) for k in range(2)]
        pT = [[c.sb(f"ca_pT{k}{x}", [P, 3 * P], F32R, ctx=ctx) for x in range(2)] for k in range(2)]
        oT = [c.sb(f"ca_oT{x}", [DH, 2, T], F32R, ctx=ctx) for x in range(2)]
        top = c.sb("ca_top", [P, 2, 2], ctx=ctx)
        total = c.sb("ca_total", [P, 2, 2], ctx=ctx)
        inv = c.sb("ca_inv", [P, 2, 2], ctx=ctx)
        dummy = c.sb("ca_dummy", [P, 1], ctx=ctx)
        starts = c.sb("ca_starts", [P, 2], ctx=ctx)
        mask = c.sb("ca_mask", [P, P], BF16, ctx=ctx)
        mask_raw = c.sb("ca_mask_raw", [P, P], ctx=ctx)
        bank = [c.ps(f"ca_proj{k}", [P, HALF], ctx=ctx) for k in range(4)]
        ps_s = [c.ps(f"ca_s{k}", [P, 3 * P], ctx=ctx) for k in range(2)]
        ps_t = c.ps("ca_t", [P, 3 * P], ctx=ctx)
        ps_o = c.ps("ca_o", [DH, 2, S], ctx=ctx)

        mask_loaded = c.sem("ca_mask_loaded")
        mask_ready = c.sem("ca_mask_ready")
        qkv_loaded, wo_loaded = c.sem("ca_qkv_loaded"), c.sem("ca_wo_loaded")
        w_hi, w_lo = c.sem("ca_w_hi"), c.sem("ca_w_lo")
        proj_done = c.sem("ca_proj_done")
        proj_hi = c.sem("ca_proj_hi")
        proj_lo = c.sem("ca_proj_lo")
        s_done = c.sem("ca_s_done")
        top_done = c.sem("ca_top_done")
        exp_done = c.sem("ca_exp_done")
        inv_done = c.sem("ca_inv_done")
        p_done = c.sem("ca_p_done")
        t_done = c.sem("ca_t_done")
        pT_hi, pT_lo = c.sem("ca_pT_hi"), c.sem("ca_pT_lo")
        pv_done = c.sem("ca_pv_done")
        oT_hi, oT_lo = c.sem("ca_oT_hi"), c.sem("ca_oT_lo")
        out_done = c.sem("ca_out_done")
        out_added = c.sem("ca_out_added")

        def bank_view(j):
            b = bank[j % 4]
            return b[:] if j < 8 else b[:].rearrange("p (t n) -> p t n", t=2)

        def projected(j, x):
            if j < 8:
                m, h, half = j // 4, j // 2 % 2, j % 2
                return qk[m][x][:, h, half * HALF:(half + 1) * HALF], QSCALE if m == 0 else 1.0
            t = 2 * (j - 8)
            return v[x][:, t:t + 2, :], 1.0

        def pairs(engine, body):
            with engine.Fori(0, PAIRS - 1) as p:
                body(p, False)
            body(PAIRS - 1, True)

        with nc.Block() as block:

            @block.sync
            def _(sp):
                sp.dma_start(mask_raw[:], c.dram["mask"]).then_inc(mask_loaded, 16)
                sp.dma_start(raw[:], c.dram["ca_w"][0]).then_inc(qkv_loaded, 16)
                sp.dma_start(raw_o[:], c.dram["ca_wo"][0]).then_inc(wo_loaded, 16)
                with sp.Fori(0, PAIRS - 1) as p:
                    sp.wait_ge(w_lo, p * 4 + 3)
                    sp.dma_start(raw[:], c.dram["ca_w"][p + 1]).then_inc(qkv_loaded, 16)
                    sp.wait_ge(w_lo, p * 4 + 4)
                    sp.dma_start(raw_o[:], c.dram["ca_wo"][p + 1]).then_inc(wo_loaded, 16)

            @block.gpsimd
            def _(pool):
                def split(part, count):
                    pool.wait_ge(w_hi, count)
                    if part == 3:
                        out, a, hi = wo[1][:], raw_o[:], f32(wo[0][:])
                    else:
                        out, a, hi = w[1][:, part], raw[:, part], f32(w[0][:, part])
                    nc.gpsimd.tensor_tensor(out, a, hi, ALU.subtract).then_inc(w_lo, 1)

                for part in range(3):
                    split(part, part + 1)

                def body(p, last):
                    for u in range(8):
                        k = u % 2
                        pool.wait_ge(inv_done, p * 8 + (u + 1))
                        nc.gpsimd.tensor_tensor(e[k][:, 0:P], e[k][:, 0:P], inv[:, k, 0:1].to_broadcast([P, P]),
                                                ALU.mult)
                        nc.gpsimd.tensor_tensor(e[k][:, P:], e[k][:, P:], inv[:, k, 1:2].to_broadcast([P, 2 * P]),
                                                ALU.mult).then_inc(p_done, 1)
                        if u == 0:
                            split(3, p * 4 + 4)
                        elif u < 4 and not last:
                            split(u - 1, p * 4 + (4 + u))

                pairs(pool, body)

            @block.scalar
            def _(act):
                nc.scalar.activation(dummy[:], c.ones[:, 0:1], ACT.Exp).then_inc(exp_done, 2)

                def split(part, p):
                    if part == 3:
                        act.wait_ge(wo_loaded, p * 16 + 16)
                        act.wait_ge(out_added, p * 4 + 4)
                        nc.scalar.activation(wo[0][:], raw_o[:], ACT.Copy).then_inc(w_hi, 1)
                    else:
                        act.wait_ge(qkv_loaded, p * 16 + 16)
                        nc.scalar.activation(w[0][:, part], raw[:, part], ACT.Copy).then_inc(w_hi, 1)

                def evacuate(p, j):
                    act.wait_ge(proj_done, p * 12 + (j + 1))
                    dst, scale = projected(j, 0)
                    nc.scalar.activation(dst, bank_view(j), ACT.Copy, scale=scale).then_inc(proj_hi, 1)

                for part in range(3):
                    split(part, 0)
                for j in range(12):
                    evacuate(0, j)

                def body(p, last):
                    for s in range(12):
                        if s < 8:
                            k = s % 2
                            act.wait_ge(top_done, p * 8 + (s + 1))
                            nc.scalar.activation(e[k][:, 0:P], ps_s[k][:, 0:P], ACT.Exp, bias=top[:, k, 0:1],
                                                 accum_out=total[:, k, 0:1])
                            nc.scalar.activation(e[k][:, P:], ps_s[k][:, P:], ACT.Exp, bias=top[:, k, 1:2],
                                                 accum_out=total[:, k, 1:2]).then_inc(exp_done, 1)
                        if s == 1:
                            split(3, p)
                        elif 2 <= s < 5 and not last:
                            split(s - 2, p + 1)
                        if 1 <= s < 9:
                            k = (s - 1) % 2
                            act.wait_ge(t_done, p * 8 + s)
                            nc.scalar.activation(pT[k][0][:], ps_t[:], ACT.Copy).then_inc(pT_hi, 1)
                        if s >= 4 and s % 2 == 0:
                            b = (s - 4) // 2
                            act.wait_ge(pv_done, p * 8 + (2 * b + 2))
                            nc.scalar.activation(oT[0][:, :, b * S:(b + 1) * S], ps_o[:], ACT.Copy).then_inc(oT_hi, 1)
                        if s in (8, 9) and not last:
                            for j in (2 * (s - 8), 2 * (s - 8) + 1):
                                evacuate(p + 1, j)
                    if not last:
                        for j in range(4, 12):
                            evacuate(p + 1, j)

                pairs(act, body)

            @block.tensor
            def _(pe):
                def project(p, j):
                    if j >= 4:
                        pe.wait_ge(proj_lo, p * 12 + (j - 3))
                    b, m = bank[j % 4], j // 4
                    if j < 8:
                        h, half = j // 2 % 2, j % 2
                        for n, (x, y) in enumerate(PASSES):
                            for ch in range(NC):
                                ins = nc.tensor.matmul(b[:], w[x][:, m, ch, h * DH:(h + 1) * DH],
                                                       c.fT[y][:, ch, half * HALF:(half + 1) * HALF],
                                                       start=(n + ch == 0), stop=(n == 2 and ch == NC - 1))
                    else:
                        for i in range(2):
                            t = 2 * (j - 8) + i
                            for n, (x, y) in enumerate(PASSES):
                                for ch in range(NC):
                                    ins = nc.tensor.matmul(b[:, i * 2 * DH:(i + 1) * 2 * DH],
                                                           c.fT[y][:, ch, t * P:(t + 1) * P], w[x][:, 2, ch, :],
                                                           start=(n + ch == 0), stop=(n == 2 and ch == NC - 1))
                    ins.then_inc(proj_done, 1)

                def scores(p, u):
                    b, h, k = u // 2, u % 2, u % 2
                    pe.wait_ge(exp_done, p * 8 + (u + 1))
                    qh, kh = qk
                    for tile, c0, n_keys in ((0, 0, P), (1, P, 2 * P)):
                        q0 = b * S + tile * P
                        for n, (x, y) in enumerate(PASSES):
                            nc.tensor.matmul(ps_s[k][:, c0:c0 + n_keys], qh[x][:, h, q0:q0 + P],
                                             kh[y][:, h, b * S:b * S + n_keys], start=(n == 0), stop=False)
                        ins = nc.tensor.matmul(ps_s[k][:, c0 + n_keys - P:c0 + n_keys], c.ident_bf[:], mask[:],
                                               start=False, stop=True)
                    ins.then_inc(s_done, 1)

                def turn(p, u):
                    k = u % 2
                    pe.wait_ge(p_done, p * 8 + (u + 1))
                    pe.wait_ge(pT_lo, p * 8 + (u + 1))
                    for n in range(3):
                        ins = nc.tensor.transpose(ps_t[:, n * P:(n + 1) * P], e[k][:, n * P:(n + 1) * P], c.ident[:])
                    ins.then_inc(t_done, 1)

                def weigh(p, u):
                    b, h, k = u // 2, u % 2, u % 2
                    pe.wait_ge(pT_lo, p * 8 + (u + 2))
                    if h == 0:
                        pe.wait_ge(oT_lo, p * 4 + (b + 1))
                    for tile, q0, c0, n_q in ((0, 0, 0, 2 * P), (1, P, 2 * P, P)):
                        for n, (x, y) in enumerate(PASSES):
                            ins = nc.tensor.matmul(ps_o[:, h, q0:q0 + n_q], v[x][:, 2 * b + tile, h * DH:(h + 1) * DH],
                                                   pT[k][y][:, c0:c0 + n_q], start=(tile == 0 and n == 0),
                                                   stop=(tile == 1 and n == 2))
                    ins.then_inc(pv_done, 1)

                def output(p, last):
                    pe.wait_ge(oT_lo, p * 4 + 5)
                    pe.wait_ge(w_lo, p * 4 + 4)
                    for j in range(4):
                        if last:
                            pe.wait_ge(out_added, PAIRS * 4)
                        else:
                            pe.wait_ge(proj_lo, p * 12 + (24 - 3 + j))
                        ch, half = j // 2, j % 2
                        for n, (x, y) in enumerate(PASSES):
                            for h in range(2):
                                ins = nc.tensor.matmul(bank[j][:], wo[x][:, h, ch * P:(ch + 1) * P],
                                                       oT[y][:, h, half * HALF:(half + 1) * HALF],
                                                       start=(n + h == 0), stop=(n == 2 and h == 1))
                        ins.then_inc(out_done, 1)

                pe.wait_ge(mask_ready, 1)
                pe.wait_ge(w_lo, 3)
                for j in range(12):
                    project(0, j)

                def body(p, last):
                    pe.wait_ge(proj_lo, p * 12 + 8)
                    for s in range(11):
                        if s < 8:
                            scores(p, s)
                        if s == 3:
                            pe.wait_ge(proj_lo, p * 12 + 12)
                        if s >= 3:
                            weigh(p, s - 3)
                        if 1 <= s < 9:
                            turn(p, s - 1)
                        if s in (8, 9) and not last:
                            if s == 8:
                                pe.wait_ge(w_lo, p * 4 + 7)
                            pe.wait_ge(out_added, p * 4 + 4)
                            for j in (2 * (s - 8), 2 * (s - 8) + 1):
                                project(p + 1, j)
                    if not last:
                        for j in range(4, 12):
                            project(p + 1, j)
                    output(p, last)

                pairs(pe, body)

            @block.vector
            def _(dve):
                nc.vector.memset(c.out_t[:], 0.0).then_inc(out_added, 4)
                nc.vector.memset(starts[:, 0:1], 0.0).then_inc(pT_lo, 1)
                nc.vector.memset(starts[:, 1:2], 0.0).then_inc(oT_lo, 1)
                dve.wait_ge(mask_loaded, 16)
                nc.vector.tensor_copy(mask[:], mask_raw[:]).then_inc(mask_ready, 1)

                def evacuate(p, j):
                    dve.wait_ge(proj_hi, p * 12 + (j + 1))
                    hi, scale = projected(j, 0)
                    lo, _ = projected(j, 1)
                    if scale == 1.0:
                        ins = nc.vector.tensor_tensor(lo, bank_view(j), f32(hi), ALU.subtract)
                    else:
                        ins = nc.vector.scalar_tensor_tensor(out=lo, in0=bank_view(j), scalar=scale, in1=f32(hi),
                                                             op0=ALU.mult, op1=ALU.subtract)
                    ins.then_inc(proj_lo, 1)

                for j in range(12):
                    evacuate(0, j)

                def body(p, last):
                    for s in range(12):
                        if 1 <= s < 9:
                            k = (s - 1) % 2
                            dve.wait_ge(exp_done, p * 8 + (s + 2))
                            nc.vector.reciprocal(inv[:, k, :], total[:, k, :]).then_inc(inv_done, 1)
                        if 2 <= s < 10:
                            k = (s - 2) % 2
                            dve.wait_ge(pT_hi, p * 8 + (s - 1))
                            nc.vector.tensor_tensor(pT[k][1][:], ps_t[:], f32(pT[k][0][:]),
                                                    ALU.subtract).then_inc(pT_lo, 1)
                        if s < 8:
                            k = s % 2
                            dve.wait_ge(s_done, p * 8 + (s + 1))
                            nc.vector.tensor_reduce(top[:, k, 0:1], ps_s[k][:, 0:P], AX.X, ALU.max, negate=True)
                            nc.vector.tensor_reduce(top[:, k, 1:2], ps_s[k][:, P:], AX.X, ALU.max,
                                                    negate=True).then_inc(top_done, 1)
                        if s >= 5 and s % 2 == 1:
                            b = (s - 5) // 2
                            dve.wait_ge(oT_hi, p * 4 + (b + 1))
                            nc.vector.tensor_tensor(oT[1][:, :, b * S:(b + 1) * S], ps_o[:],
                                                    f32(oT[0][:, :, b * S:(b + 1) * S]),
                                                    ALU.subtract).then_inc(oT_lo, 1)
                        if s in (9, 10) and not last:
                            for j in (2 * (s - 9), 2 * (s - 9) + 1):
                                evacuate(p + 1, j)
                    if not last:
                        for j in range(4, 12):
                            evacuate(p + 1, j)
                    for j in range(4):
                        ch, half = j // 2, j % 2
                        dst = c.out_t[:, ch, half * HALF:(half + 1) * HALF]
                        dve.wait_ge(out_done, p * 4 + (j + 1))
                        dve.wait_ge(out_added, p * 4 + 4)
                        nc.vector.tensor_tensor(dst, dst, bank[j][:], ALU.add).then_inc(out_added, 1)

                pairs(dve, body)



ROWS = 32
WCOLS = 2 * NC * P + D + P


def top_k_mask(c, dve, step, probs, top, mask, n_experts):
    nc = c.nc
    for t in range(NT):
        ins = nc.vector.match_replace(mask[:, t, :], top[:, t, :], probs[:, t, :], -2.0)
    step.after(ins)
    step.after(nc.vector.tensor_tensor(mask[:], mask[:], probs[:], ALU.not_equal))


def route(c, name, n_experts, top_k, threshold=None, shared=False):
    nc = c.nc
    width = n_experts + 8
    with ExitStack() as ctx:
        gate = c.sb(name + "_gate", [P, NC, n_experts], ctx=ctx)
        g = [c.sb(f"{name}_g{x}", [P, NC, n_experts], F32R, ctx=ctx) for x in range(2)]
        probs = c.sb(name + "_probs", [P, NT, width], ctx=ctx)
        mask = c.sb(name + "_mask", [P, NT, width], ctx=ctx)
        top = c.sb(name + "_top", [P, NT, 8], ctx=ctx)
        kept = c.sb(name + "_kept", [P, NT, 8], ctx=ctx)
        share = c.sb(name + "_share", [P, NT, 8], ctx=ctx)
        red = c.sb(name + "_red", [P, NT], ctx=ctx)
        weights = c.sb(name + "_weights", [P, NT, ROWS], ctx=ctx)
        ps_l = c.ps(name + "_ps_l", [P, NT, n_experts], ctx=ctx)
        ps_w = [c.ps(f"{name}_ps_w{k}", [ROWS, HALF], ctx=ctx) for k in range(NHALF)]
        loaded, g_hi, g_lo = c.sem(name + "_loaded"), c.sem(name + "_g_hi"), c.sem(name + "_g_lo")
        logits, shifted, exped = c.sem(name + "_logits"), c.sem(name + "_shifted"), c.sem(name + "_exped")
        weighted, turned = c.sem(name + "_weighted"), c.sem(name + "_turned")
        hi_done, lo_done, own = c.sem(name + "_hi"), c.sem(name + "_lo"), c.sem(name + "_own")
        experts = probs[:, :, 0:n_experts]

        def spread(col, n):
            return col.unsqueeze(2).to_broadcast([P, NT, n])

        with nc.Block() as block:

            @block.sync
            def _(sp):
                sp.dma_start(gate[:], c.dram[name + "_gate"]).then_inc(loaded, 16)

            @block.scalar
            def _(act):
                act.wait_ge(loaded, 16)
                nc.scalar.activation(g[0][:], gate[:], ACT.Copy).then_inc(g_hi, 1)
                act.wait_ge(shifted, 1)
                nc.scalar.activation(experts, experts, ACT.Exp).then_inc(exped, 1)
                for k in range(NHALF):
                    act.wait_ge(turned, k + 1)
                    nc.scalar.activation(c.route_t[0:ROWS, k * HALF:(k + 1) * HALF], ps_w[k][:],
                                         ACT.Copy).then_inc(hi_done, 1)

            @block.tensor
            def _(pe):
                pe.wait_ge(g_lo, 1)
                for t in range(NT):
                    for n, (x, y) in enumerate(PASSES):
                        for ch in range(NC):
                            ins = nc.tensor.matmul(ps_l[:, t, :], c.fT[x][:, ch, t * P:(t + 1) * P], g[y][:, ch, :],
                                                   start=(n + ch == 0), stop=(n == 2 and ch == NC - 1))
                ins.then_inc(logits, 1)
                pe.wait_ge(weighted, 1)
                for t in range(NT):
                    k, c0 = t // 4, t % 4 * P
                    ins = nc.tensor.matmul(ps_w[k][:, c0:c0 + P], weights[:, t, :], c.ident[:], start=True, stop=True)
                    if t % 4 == 3:
                        ins.then_inc(turned, 1)

            @block.vector
            def _(dve):
                step = Counter(dve, own)
                dve.wait_ge(g_hi, 1)
                nc.vector.tensor_tensor(g[1][:], gate[:], f32(g[0][:]), ALU.subtract).then_inc(g_lo, 1)
                step.after(nc.vector.memset(probs[:], -1.0))
                step.after(nc.vector.memset(weights[:], 0.0))
                if shared:
                    step.after(nc.vector.memset(weights[:, :, n_experts:n_experts + 1], 1.0))
                step.after(nc.vector.memset(c.route_t[:].bitcast(F32), 0.0))
                dve.wait_ge(logits, 1)
                step.after(nc.vector.tensor_reduce(red[:], ps_l[:], AX.X, ALU.max))
                nc.vector.tensor_tensor(experts, ps_l[:], spread(red[:], n_experts), ALU.subtract).then_inc(shifted, 1)
                dve.wait_ge(exped, 1)
                step.after(nc.vector.tensor_reduce(red[:], experts, AX.X, ALU.add))
                step.after(nc.vector.reciprocal(red[:], red[:]))
                step.after(nc.vector.tensor_tensor(experts, experts, spread(red[:], n_experts), ALU.mult))
                for t in range(NT):
                    ins = nc.vector.max(out=top[:, t, :], in_=probs[:, t, :])
                step.after(ins)
                if threshold is None:
                    step.after(nc.vector.memset(top[:, :, top_k:8], -1.0))
                    step.after(nc.vector.tensor_reduce(red[:], top[:, :, 0:top_k], AX.X, ALU.add))
                else:
                    step.after(nc.vector.tensor_reduce(red[:], top[:], AX.X, ALU.add))
                    step.after(nc.vector.tensor_scalar(red[:], red[:], 1e-12, None, ALU.max))
                    step.after(nc.vector.reciprocal(red[:], red[:]))
                    step.after(nc.vector.tensor_tensor(share[:], top[:], spread(red[:], 8), ALU.mult))
                    for j in range(1, top_k):
                        step.after(nc.vector.tensor_tensor(share[:, :, j], share[:, :, j], share[:, :, j - 1], ALU.add))
                    step.after(nc.vector.memset(kept[:, :, 0:1], 1.0))
                    step.after(nc.vector.tensor_scalar(kept[:, :, 1:8], share[:, :, 0:7], threshold, None, ALU.is_lt))
                    step.after(nc.vector.tensor_tensor(top[:], top[:], kept[:], ALU.mult))
                    step.after(nc.vector.tensor_reduce(red[:], top[:], AX.X, ALU.add))
                    step.after(nc.vector.tensor_scalar(kept[:], kept[:], -1.0, None, ALU.add))
                    step.after(nc.vector.tensor_tensor(top[:], top[:], kept[:], ALU.add))
                    step.after(nc.vector.tensor_scalar(red[:], red[:], 1e-12, None, ALU.max))
                top_k_mask(c, dve, step, probs, top, mask, n_experts)
                step.after(nc.vector.reciprocal(red[:], red[:]))
                step.after(nc.vector.tensor_tensor(experts, experts, mask[:, :, 0:n_experts], ALU.mult))
                nc.vector.tensor_tensor(weights[:, :, 0:n_experts], experts, spread(red[:], n_experts),
                                        ALU.mult).then_inc(weighted, 1)
                for k in range(NHALF):
                    dve.wait_ge(hi_done, k + 1)
                    cols = slice(k * HALF, (k + 1) * HALF)
                    nc.vector.tensor_tensor(c.route_t[ROWS:2 * ROWS, cols], ps_w[k][:],
                                            f32(c.route_t[0:ROWS, cols]), ALU.subtract).then_inc(lo_done, 1)


def experts(c, name, n_chunks):
    nc = c.nc
    with ExitStack() as ctx:
        raw = [c.sb(f"{name}_raw{k}", [P, WCOLS], ctx=ctx) for k in range(2)]
        w = [[c.sb(f"{name}_w{k}{x}", [P, WCOLS], F32R, ctx=ctx) for x in range(2)] for k in range(2)]
        gated = [c.sb(f"{name}_gated{k}", [P, HALF], ctx=ctx) for k in range(2)]
        routed = [c.sb(f"{name}_routed{k}", [P, HALF], ctx=ctx) for k in range(2)]
        inner = [c.sb(f"{name}_inner{k}", [P, HALF], ctx=ctx) for k in range(2)]
        a = [[c.sb(f"{name}_a{k}{x}", [P, HALF], F32R, ctx=ctx) for x in range(2)] for k in range(2)]
        zeros = c.sb(name + "_zeros", [P, HALF], BF16, ctx=ctx)
        ps_g = [c.ps(f"{name}_ps_g{k}", [P, HALF], ctx=ctx) for k in range(2)]
        ps_u = c.ps(name + "_ps_u", [P, HALF], ctx=ctx)
        ps_r = c.ps(name + "_ps_r", [P, HALF], ctx=ctx)
        acc = [[c.ps(f"{name}_acc{ch}{h}", [P, HALF], ctx=ctx) for h in range(NHALF)] for ch in range(NC)]
        loaded = [c.sem(f"{name}_loaded{k}") for k in range(2)]
        zeroed = c.sem(name + "_zeroed")
        w_hi, w_lo = c.sem(name + "_w_hi"), c.sem(name + "_w_lo")
        gate_done = c.sem(name + "_gate_done")
        route_done = c.sem(name + "_route_done")
        up_done = c.sem(name + "_up_done")
        down_done = c.sem(name + "_down_done")
        silu_done = c.sem(name + "_silu_done")
        routed_done = c.sem(name + "_routed_done")
        inner_done = c.sem(name + "_inner_done")
        a_hi, a_lo = c.sem(name + "_a_hi"), c.sem(name + "_a_lo")
        taken = c.sem(name + "_taken")

        def gate_up(m, ch):
            c0 = (m * NC + ch) * P
            return slice(c0, c0 + P)

        def down(ch):
            c0 = 2 * NC * P + ch * P
            return slice(c0, c0 + P)

        select = slice(WCOLS - P, WCOLS)
        zero = lambda x: isinstance(x, int) and x == 0

        with nc.Block() as block:

            @block.sync
            def _(sp):
                def load(ck, k):
                    if not (isinstance(ck, int) and ck < 2):
                        sp.wait_ge(w_lo, ck - 1)
                    sp.dma_start(raw[k][:], c.dram[name + "_w"][ck]).then_inc(loaded[k], 16)

                in_pairs(sp, n_chunks, load)

            @block.gpsimd
            def _(pool):
                def split(ck, k):
                    pool.wait_ge(w_hi, ck + 1)
                    nc.gpsimd.tensor_tensor(w[k][1][:], raw[k][:], f32(w[k][0][:]), ALU.subtract).then_inc(w_lo, 1)

                in_pairs(pool, n_chunks, split)

            @block.scalar
            def _(act):
                def split(ck, k):
                    act.wait_ge(loaded[k], loads_of_slot(ck, k))
                    if not (isinstance(ck, int) and ck < 2):
                        act.wait_ge(down_done, ck * 2 - 2)
                    nc.scalar.activation(w[k][0][:], raw[k][:], ACT.Copy).then_inc(w_hi, 1)

                def take_hi(n, h):
                    act.wait_ge(inner_done, n + 1)
                    nc.scalar.activation(a[h][0][:], inner[h][:], ACT.Copy).then_inc(a_hi, 1)

                def body(ck, k):
                    for h in range(2):
                        n = ck * 2 + h
                        if not zero(n):
                            take_hi(n - 1, 1 - h)
                        act.wait_ge(gate_done, n + 1)
                        nc.scalar.activation(gated[h][:], ps_g[h][:], ACT.Silu).then_inc(silu_done, 1)
                    if not (isinstance(ck, int) and ck == n_chunks - 1):
                        split(ck + 1, 1 - k)

                split(0, 0)
                in_pairs(act, n_chunks, body, peel_last=True)
                take_hi(2 * n_chunks - 1, 1)
                act.wait_ge(down_done, 2 * n_chunks)
                for ch in range(NC):
                    for h in range(NHALF):
                        nc.scalar.activation(c.out_t[:, ch, h * HALF:(h + 1) * HALF], acc[ch][h][:],
                                             ACT.Copy).then_inc(taken, 1)

            @block.tensor
            def _(pe):
                def down_products(n, h, k):
                    pe.wait_ge(a_lo, n + 1)
                    for ch in range(NC):
                        for x, y in PASSES:
                            ins = nc.tensor.matmul(acc[ch][h][:], w[k][x][:, down(ch)], a[h][y][:], start=False,
                                                   stop=False, skip_group_check=True)
                    ins.then_inc(down_done, 1)

                def body(ck, k):
                    pe.wait_ge(w_lo, ck + 1)
                    for h in range(2):
                        n = ck * 2 + h
                        cols = slice(h * HALF, (h + 1) * HALF)
                        for i, (x, y) in enumerate(PASSES):
                            for ch in range(NC):
                                ins = nc.tensor.matmul(ps_g[h][:], w[k][x][:, gate_up(0, ch)], c.fT[y][:, ch, cols],
                                                       start=(i + ch == 0), stop=(i == 2 and ch == NC - 1))
                        ins.then_inc(gate_done, 1)
                        pe.wait_ge(routed_done, n)
                        nc.tensor.matmul(ps_r[:], w[k][0][0:2 * ROWS, select], c.route_t[:, cols], start=True,
                                         stop=True).then_inc(route_done, 1)
                        pe.wait_ge(inner_done, n)
                        for i, (x, y) in enumerate(PASSES):
                            for ch in range(NC):
                                ins = nc.tensor.matmul(ps_u[:], w[k][x][:, gate_up(1, ch)], c.fT[y][:, ch, cols],
                                                       start=(i + ch == 0), stop=(i == 2 and ch == NC - 1))
                        ins.then_inc(up_done, 1)
                        if not zero(n):
                            down_products(n - 1, 1 - h, k if h == 1 else 1 - k)

                pe.wait_ge(zeroed, 1)
                for ch in range(NC):
                    for h in range(NHALF):
                        nc.tensor.matmul(acc[ch][h][:], zeros[:, 0:P], zeros[:], start=True, stop=False,
                                         skip_group_check=True)
                in_pairs(pe, n_chunks, body)
                down_products(2 * n_chunks - 1, 1, (n_chunks - 1) % 2)

            @block.vector
            def _(dve):
                nc.vector.memset(zeros[:], 0.0).then_inc(zeroed, 1)

                def take_lo(n, h):
                    dve.wait_ge(a_hi, n + 1)
                    nc.vector.tensor_tensor(a[h][1][:], inner[h][:], f32(a[h][0][:]), ALU.subtract).then_inc(a_lo, 1)

                def body(ck, k):
                    for h in range(2):
                        n = ck * 2 + h
                        if not zero(n):
                            take_lo(n - 1, 1 - h)
                        dve.wait_ge(silu_done, n + 1)
                        dve.wait_ge(route_done, n + 1)
                        if not zero(n):
                            dve.wait_ge(inner_done, n)
                        nc.vector.tensor_tensor(routed[h][:], ps_r[:], gated[h][:], ALU.mult).then_inc(routed_done, 1)
                        dve.wait_ge(up_done, n + 1)
                        dve.wait_ge(routed_done, n + 1)
                        if not zero(n):
                            dve.wait_ge(a_lo, n - 1)
                        nc.vector.tensor_tensor(inner[h][:], ps_u[:], routed[h][:], ALU.mult).then_inc(inner_done, 1)

                in_pairs(dve, n_chunks, body)
                take_lo(2 * n_chunks - 1, 1)


def routed_block(c):
    nc = c.nc
    squared, root, own = c.sem("rb_squared"), c.sem("rb_root"), c.sem("rb_own")
    with ExitStack() as ctx:
        sq = c.sb("rb_sq", [P, NT, D], ctx=ctx)
        with nc.Block() as block:

            @block.vector
            def _(dve):
                step = Counter(dve, own)
                step.after(nc.vector.tensor_tensor(sq[:], c.hid[:], c.hid[:], ALU.mult))
                step.after(nc.vector.tensor_reduce(c.stat[:, 0, :], sq[:], AX.X, ALU.add))
                step.after(nc.vector.tensor_scalar(c.stat[:, 0, :], c.stat[:, 0, :], 1.0 / D, 1e-6, ALU.mult, ALU.add))
                inverse_root(c, dve, step, squared, root, 1, c.stat[:, 0, :], c.rms[:])

            @block.scalar
            def _(act):
                act.wait_ge(squared, 1)
                nc.scalar.activation(c.stat[:, 1, :], c.stat[:, 0, :], ACT.Sqrt).then_inc(root, 1)

    norm_to_feature_major(c, "rb_turn", c.hid, c.rms, None, gain=NC)
    route(c, "rb_route", 16, 4, shared=True)
    experts(c, "rb_moe", L0_CHUNKS)
    add_feature_major(c, "rb_out", c.out_t, c.x, extra=c.hid)



SLOT = 4 * HD
LN255 = float(np.log(255.0))
NPAIR = H // 2


def quantised_attention(c):
    row_statistics(c, "qa_norm", c.x)
    norm_to_feature_major(c, "qa_turn", c.x, c.rstd, c.shift)
    with ExitStack() as ctx:
        a = Core(c.nc, ctx, c.dram)
        a.sq = a.sb("qa_sq", [P, NT, H])
        a.sv = a.sb("qa_sv", [P, NC])
        a.q_parts = a.sb("qa_q_parts", [P, NPAIR, T], BF16)
        a.k_parts = a.sb("qa_k_parts", [P, NPAIR, T], BF16)
        a.v_int = a.sb("qa_v_int", [P, NT, D], BF16)
        a.wp = [a.sb(f"qa_wp{x}", [P, NC, D], F32R) for x in range(2)]
        quantise(c, a)
        a.aT = [a.sb(f"qa_aT{x}", [P, NC, T], F32R) for x in range(2)]
        attend(c, a)
        project_out(c, a)
    add_feature_major(c, "qa_out", c.out_t, c.x)


def quantise(c, a):
    nc = c.nc
    with ExitStack() as ctx:
        q_rows = c.sb("qa_q_rows", [P, NT, H, 4, HD], BF16, ctx=ctx)
        k_rows = c.sb("qa_k_rows", [P, NT, H, 4, HD], BF16, ctx=ctx)
        v_cols = c.sb("qa_v_cols", [P, NC, T], BF16, ctx=ctx)
        with ExitStack() as inner:
            project_in(c, a, inner, q_rows, k_rows, v_cols)
        slots = [c.ps(f"qa_ps_slot{k}", [P, T], BF16, ctx=ctx) for k in range(4)]
        turned, by_act, by_dve = c.sem("qa_turned"), c.sem("qa_turned_act"), c.sem("qa_turned_dve")
        groups = [("q", n) for n in range(NPAIR)] + [("k", n) for n in range(NPAIR)] + [("v", n) for n in range(NC)]

        def source(kind, n, t):
            if kind == "v":
                return v_cols[:, n, t * P:(t + 1) * P]
            rows = q_rows if kind == "q" else k_rows
            return rows[:, t, 2 * n:2 * n + 2].rearrange("p h s d -> p (h s d)")

        def target(kind, n):
            if kind == "v":
                return a.v_int[:, :, n * P:(n + 1) * P]
            return (a.q_parts if kind == "q" else a.k_parts)[:, n, :].rearrange("p (t n) -> p t n", t=NT)

        def slot(g):
            return slots[g % 4][:].rearrange("p (t n) -> p t n", t=NT)

        with nc.Block() as block:

            @block.tensor
            def _(pe):
                for g, (kind, n) in enumerate(groups):
                    if g >= 4:
                        pe.wait_ge(by_act if g % 2 else by_dve, (g - 4) // 2 + 1)
                    for t in range(NT):
                        ins = nc.tensor.transpose(slots[g % 4][:, t * P:(t + 1) * P], source(kind, n, t),
                                                  c.ident_bf[:])
                    ins.then_inc(turned, 1)

            @block.scalar
            def _(act):
                for g in range(1, len(groups), 2):
                    act.wait_ge(turned, g + 1)
                    nc.scalar.activation(target(*groups[g]), slot(g), ACT.Copy).then_inc(by_act, 1)

            @block.vector
            def _(dve):
                for g in range(0, len(groups), 2):
                    dve.wait_ge(turned, g + 1)
                    nc.vector.tensor_copy(target(*groups[g]), slot(g)).then_inc(by_dve, 1)


def project_in(c, a, ctx, q_rows, k_rows, v_cols):
    nc = c.nc
    w_raw = c.sb("qa_w_raw", [P, NC, 4 * D], ctx=ctx)
    w = [c.sb(f"qa_w{x}", [P, NC, 3 * D], F32R, ctx=ctx) for x in range(2)]
    ctx_raw = c.sb("qa_ctx_raw", [P, NC, T], ctx=ctx)
    cT = [c.sb(f"qa_cT{x}", [P, NC, T], F32R, ctx=ctx) for x in range(2)]
    bias = c.sb("qa_bias", [1, 2 * D], ctx=ctx)
    qf = c.sb("qa_qf", [P, NT * H, HD], ctx=ctx)
    kf = c.sb("qa_kf", [P, NT * H, HD], ctx=ctx)
    vf = c.out_t
    ints = c.sb("qa_ints", [P, NT * H, HD], I16, ctx=ctx)
    v_ints = c.sb("qa_v_ints", [P, T], I16, ctx=ctx)
    rest = c.hid[:].rearrange("p t (h d) -> p (t h) d", d=HD)
    sk = c.sb("qa_sk", [P, NT * H], ctx=ctx)
    inv = c.sb("qa_inv_scale", [P, NT * H], ctx=ctx)
    inv_v = c.sb("qa_inv_v", [P, NC], ctx=ctx)
    bank = [c.ps(f"qa_bank{k}", [P, HALF], ctx=ctx) for k in range(8)]
    loaded = c.sem("qa_loaded")
    hi_done, lo_done = c.sem("qa_hi"), c.sem("qa_lo")
    done = c.sem("qa_proj_done")
    out = c.sem("qa_proj_out")
    own = c.sem("qa_quant_own")
    sq = a.sq[:].rearrange("p t h -> p (t h)")

    with nc.Block() as block:

        @block.sync
        def _(sp):
            sp.dma_start(w_raw[:], c.dram["qa_w"]).then_inc(loaded, 16)
            sp.dma_start(ctx_raw[:], c.dram["ctx_t"]).then_inc(loaded, 16)
            sp.dma_start(bias[:], c.dram["qa_bias"]).then_inc(loaded, 16)

        @block.gpsimd
        def _(pool):
            pool.wait_ge(hi_done, 2)
            nc.gpsimd.tensor_tensor(w[1][:], w_raw[:, :, 0:3 * D], f32(w[0][:]), ALU.subtract).then_inc(lo_done, 1)
            nc.gpsimd.tensor_tensor(a.wp[1][:], w_raw[:, :, 3 * D:], f32(a.wp[0][:]), ALU.subtract).then_inc(lo_done, 1)
            pool.wait_ge(hi_done, 3)
            nc.gpsimd.tensor_tensor(cT[1][:], ctx_raw[:], f32(cT[0][:]), ALU.subtract).then_inc(lo_done, 1)

        @block.scalar
        def _(act):
            act.wait_ge(loaded, 48)
            nc.scalar.activation(w[0][:], w_raw[:, :, 0:3 * D], ACT.Copy).then_inc(hi_done, 1)
            nc.scalar.activation(a.wp[0][:], w_raw[:, :, 3 * D:], ACT.Copy).then_inc(hi_done, 1)
            nc.scalar.activation(cT[0][:], ctx_raw[:], ACT.Copy).then_inc(hi_done, 1)
            for j in range(8):
                act.wait_ge(done, j + 1)
                dst = (qf, kf)[j // 4][:, (j % 4) * 2 * H:(j % 4 + 1) * 2 * H, :]
                nc.scalar.activation(dst.rearrange("p h d -> p (h d)"), bank[j][:], ACT.Copy).then_inc(out, 1)
            for j in range(4):
                act.wait_ge(done, j + 9)
                ch, half = j // 2, j % 2
                nc.scalar.activation(vf[:, ch, half * HALF:(half + 1) * HALF], bank[j][:], ACT.Identity,
                                     bias=c.vecs[:, 4 + ch:5 + ch]).then_inc(out, 1)

        @block.tensor
        def _(pe):
            pe.wait_ge(lo_done, 1)
            for m in range(2):
                if m == 1:
                    pe.wait_ge(lo_done, 3)
                src = (c.fT, cT)[m]
                for t in range(NT):
                    dst = bank[4 * m + t // 2][:, (t % 2) * D:(t % 2 + 1) * D]
                    nc.tensor.matmul(dst, c.ones[0:1, 0:P], bias[:, m * D:(m + 1) * D], start=True, stop=False)
                    for n, (x, y) in enumerate(PASSES):
                        for ch in range(NC):
                            ins = nc.tensor.matmul(dst, src[x][:, ch, t * P:(t + 1) * P],
                                                   w[y][:, ch, m * D:(m + 1) * D], start=False,
                                                   stop=(n == 2 and ch == NC - 1))
                    if t % 2:
                        ins.then_inc(done, 1)
            for j in range(4):
                pe.wait_ge(out, j + 1)
                out_ch, half = j // 2, j % 2
                for n, (x, y) in enumerate(PASSES):
                    for ch in range(NC):
                        ins = nc.tensor.matmul(bank[j][:], w[x][:, ch, 2 * D + out_ch * P:2 * D + (out_ch + 1) * P],
                                               cT[y][:, ch, half * HALF:(half + 1) * HALF], start=(n + ch == 0),
                                               stop=(n == 2 and ch == NC - 1))
                ins.then_inc(done, 1)

        @block.vector
        def _(dve):
            step = Counter(dve, own)

            def spread(col):
                return col.unsqueeze(2).to_broadcast([P, NT * H, HD])

            def integers(values, scale, factor):
                step.after(nc.vector.tensor_reduce(scale, values[:], AX.X, ALU.max, apply_absolute_value=True))
                step.after(nc.vector.tensor_scalar(scale, scale, factor / 127.0, 1e-8, ALU.mult, ALU.max))
                step.after(nc.vector.reciprocal(inv[:], scale))
                if factor != 1.0:
                    step.after(nc.vector.tensor_scalar(inv[:], inv[:], factor, None, ALU.mult))
                step.after(nc.vector.tensor_tensor(ints[:], values[:], spread(inv[:]), ALU.mult))

            def rows(tensor, part):
                return tensor[:, :, :, part, :].rearrange("p t h d -> p (t h) d")

            step.after(nc.vector.memset(rows(q_rows, 3), 0.0))
            step.after(nc.vector.memset(rows(k_rows, 3), 0.0))
            dve.wait_ge(out, 4)
            integers(qf, sq, HD ** -0.5)
            for part in range(3):
                ins = nc.vector.tensor_scalar(rows(q_rows, part), ints[:], 127.0, -127.0, ALU.min, ALU.max)
            step.after(ins)
            dve.wait_ge(out, 8)
            integers(kf, sk[:], 1.0)
            step.after(nc.vector.tensor_scalar(kf[:], ints[:], 127.0, -127.0, ALU.min, ALU.max))
            step.after(nc.vector.tensor_tensor(rest, kf[:], spread(sk[:]), ALU.mult))
            for part in range(3):
                step.after(nc.vector.tensor_copy(rows(k_rows, part), rest))
                if part < 2:
                    step.after(nc.vector.tensor_tensor(rest, rest, rows(k_rows, part), ALU.subtract))
            dve.wait_ge(out, 12)
            step.after(nc.vector.tensor_reduce(a.sv[:], vf[:], AX.X, ALU.max, apply_absolute_value=True))
            step.after(nc.vector.tensor_scalar(a.sv[:], a.sv[:], 1.0 / 127.0, 1e-8, ALU.mult, ALU.max))
            step.after(nc.vector.reciprocal(inv_v[:], a.sv[:]))
            for ch in range(NC):
                step.after(nc.vector.tensor_scalar(v_ints[:], vf[:, ch, :], inv_v[:, ch:ch + 1], None, ALU.mult))
                step.after(nc.vector.tensor_scalar(v_cols[:, ch, :], v_ints[:], 127.0, -127.0, ALU.min, ALU.max))


def attend(c, a):
    nc = c.nc
    LAG_T, LAG_V = 2, 3
    with ExitStack() as ctx:
        q_now = c.sb("qa_q_now", [P, NPAIR, P], BF16, ctx=ctx)
        e = [c.sb(f"qa_e{k}", [P, T], I16, ctx=ctx) for k in range(4)]
        pT = [c.sb(f"qa_pT{k}", [P, T], BF16, ctx=ctx) for k in range(2)]
        top = c.sb("qa_top", [P, 4], ctx=ctx)
        shift = c.sb("qa_shift", [P, 4], ctx=ctx)
        total = c.sb("qa_total", [P, NT, H], ctx=ctx)
        inv = c.sb("qa_inv", [P, H], ctx=ctx)
        at = c.sb("qa_at", [P, H, HD], ctx=ctx)
        dummy = c.sb("qa_dummy", [P, 1], ctx=ctx)
        ps_s = [c.ps(f"qa_s{k}", [P, T], ctx=ctx) for k in range(2)]
        ps_t = [c.ps(f"qa_t{k}", [P, T], BF16, ctx=ctx) for k in range(2)]
        ps_o = c.ps("qa_o", [P, H, HD], ctx=ctx)
        ps_a = c.ps("qa_a", [P, NC, P], ctx=ctx)
        q_ready = c.sem("qa_q_ready")
        s_done = c.sem("qa_s_done")
        top_done = c.sem("qa_top_done")
        shift_done = c.sem("qa_shift_done")
        exp_done = c.sem("qa_exp_done")
        t_done = c.sem("qa_t_done")
        out_dve, out_act = c.sem("qa_out_dve"), c.sem("qa_out_act")
        pv_done = c.sem("qa_pv_done")
        inv_done = c.sem("qa_inv_done")
        at_done = c.sem("qa_at_done")
        a_turned = c.sem("qa_a_turned")
        a_hi, a_lo = c.sem("qa_a_hi"), c.sem("qa_a_lo")

        def tiles(engine, body):
            body(0, True)
            with engine.Fori(0, NT - 1) as i:
                body(i + 1, False)

        def tokens(t):
            return slice(t * P, (t + 1) * P) if isinstance(t, int) else bass.ds(t * P, P)

        with nc.Block() as block:

            @block.gpsimd
            def _(pool):
                def body(t, first):
                    pool.wait_ge(s_done, t * H)
                    nc.gpsimd.tensor_copy(q_now[:], a.q_parts[:, :, tokens(t)]).then_inc(q_ready, 1)

                tiles(pool, body)

            @block.tensor
            def _(pe):
                def scores(t, h):
                    pe.wait_ge(exp_done, t * H + h + 1)
                    r0 = (h % 2) * SLOT
                    for half in range(2):
                        ins = nc.tensor.matmul(ps_s[h % 2][:, half * HALF:(half + 1) * HALF],
                                               q_now[r0:r0 + 3 * HD, h // 2, :],
                                               a.k_parts[r0:r0 + 3 * HD, h // 2, half * HALF:(half + 1) * HALF],
                                               start=True, stop=True)
                    ins.then_inc(s_done, 1)

                def turn(t, h):
                    pe.wait_ge(exp_done, t * H + h + 3)
                    for n in range(NT):
                        ins = nc.tensor.transpose(ps_t[h % 2][:, n * P:(n + 1) * P],
                                                  e[h % 4][:, n * P:(n + 1) * P].bitcast(BF16), c.ident_bf[:])
                    ins.then_inc(t_done, 1)

                def weigh(t, h):
                    pe.wait_ge(out_act if h % 2 else out_dve, t * (H // 2) + (h // 2 + 1))
                    if h == 0:
                        pe.wait_ge(at_done, t)
                    for n in range(NT):
                        ins = nc.tensor.matmul(ps_o[:, h, :], pT[h % 2][:, n * P:(n + 1) * P],
                                               a.v_int[:, n, h * HD:(h + 1) * HD], start=(n == 0), stop=(n == NT - 1))
                    if h == H - 1:
                        ins.then_inc(pv_done, 1)

                def turn_output(t):
                    pe.wait_ge(at_done, t + 1)
                    pe.wait_ge(a_lo, t)
                    for ch in range(NC):
                        ins = nc.tensor.transpose(ps_a[:, ch, :], at[:, 8 * ch:8 * ch + 8, :].rearrange("p h d -> p (h d)"),
                                                  c.ident[:])
                    ins.then_inc(a_turned, 1)

                def lagging(t, s, lag, work):
                    if s >= lag:
                        work(t, s - lag)
                    elif not (isinstance(t, int) and t == 0):
                        work(t - 1, H + s - lag)

                def body(t, first):
                    pe.wait_ge(q_ready, t + 1)
                    for h in range(H):
                        scores(t, h)
                        lagging(t, h, LAG_T, turn)
                        lagging(t, h, LAG_V, weigh)
                        if h == 5 and not first:
                            turn_output(t - 1)

                tiles(pe, body)
                for s in range(H, H + LAG_V):
                    if s - LAG_T < H:
                        turn(NT - 1, s - LAG_T)
                    weigh(NT - 1, s - LAG_V)
                turn_output(NT - 1)

            @block.vector
            def _(dve):
                def finish(t):
                    dve.wait_ge(pv_done, t + 1)
                    nc.vector.reciprocal(inv[:], total[:, t, :]).then_inc(inv_done, 1)
                    dve.wait_ge(inv_done, t + 1)
                    nc.vector.tensor_tensor(at[:], ps_o[:], inv[:].unsqueeze(2).to_broadcast([P, H, HD]),
                                            ALU.mult).then_inc(at_done, 1)

                def split_lo(t):
                    dve.wait_ge(a_hi, t + 1)
                    for ch in range(NC):
                        ins = nc.vector.scalar_tensor_tensor(out=a.aT[1][:, ch, tokens(t)], in0=ps_a[:, ch, :],
                                                             scalar=a.sv[:, ch:ch + 1],
                                                             in1=f32(a.aT[0][:, ch, tokens(t)]), op0=ALU.mult,
                                                             op1=ALU.subtract)
                    ins.then_inc(a_lo, 1)

                def take(t, h):
                    dve.wait_ge(t_done, t * H + (h + 1))
                    nc.vector.tensor_copy(pT[h % 2][:], ps_t[h % 2][:].bitcast(I16)).then_inc(out_dve, 1)

                def body(t, first):
                    for h in range(H):
                        dve.wait_ge(s_done, t * H + (h + 1))
                        nc.vector.tensor_reduce(top[:, h % 4:h % 4 + 1], ps_s[h % 2][:], AX.X, ALU.max,
                                                negate=True).then_inc(top_done, 1)
                        if not (first and h < 2) and h % 2 == 0:
                            if h >= 2:
                                take(t, h - 2)
                            else:
                                take(t - 1, H - 2)
                        dve.wait_ge(top_done, t * H + (h + 1))
                        nc.vector.tensor_scalar(shift[:, h % 4:h % 4 + 1], top[:, h % 4:h % 4 + 1],
                                                a.sq[:, t, h:h + 1], LN255, ALU.mult, ALU.add).then_inc(shift_done, 1)
                        if h == 3 and not first:
                            finish(t - 1)
                        if h == 7 and not first:
                            split_lo(t - 1)

                tiles(dve, body)
                take(NT - 1, H - 2)
                finish(NT - 1)
                split_lo(NT - 1)

            @block.scalar
            def _(act):
                nc.scalar.activation(dummy[:], c.ones[:, 0:1], ACT.Exp).then_inc(exp_done, 2)

                def take(t, h):
                    act.wait_ge(t_done, t * H + (h + 1))
                    nc.scalar.activation(pT[h % 2][:], ps_t[h % 2][:].bitcast(I16), ACT.Copy).then_inc(out_act, 1)

                def split_hi(t):
                    act.wait_ge(a_turned, t + 1)
                    for ch in range(NC):
                        ins = nc.scalar.activation(a.aT[0][:, ch, tokens(t)], ps_a[:, ch, :], ACT.Copy,
                                                   scale=a.sv[:, ch:ch + 1])
                    ins.then_inc(a_hi, 1)

                def body(t, first):
                    for h in range(H):
                        if h % 2 == 1:
                            if h >= 2:
                                take(t, h - 2)
                            elif not first:
                                take(t - 1, H - 1)
                        act.wait_ge(shift_done, t * H + (h + 1))
                        nc.scalar.activation(e[h % 4][:], ps_s[h % 2][:], ACT.Exp, bias=shift[:, h % 4:h % 4 + 1],
                                             scale=a.sq[:, t, h:h + 1],
                                             accum_out=total[:, t, h:h + 1]).then_inc(exp_done, 1)
                        if h == 6 and not first:
                            split_hi(t - 1)

                tiles(act, body)
                take(NT - 1, H - 1)
                split_hi(NT - 1)


def project_out(c, a):
    nc = c.nc
    with ExitStack() as ctx:
        bank = [c.ps(f"qa_out{k}", [P, HALF], ctx=ctx) for k in range(4)]
        done, out = c.sem("qa_out_done"), c.sem("qa_out_out")
        with nc.Block() as block:

            @block.tensor
            def _(pe):
                for j in range(4):
                    out_ch, half = j // 2, j % 2
                    for n, (x, y) in enumerate(PASSES):
                        for ch in range(NC):
                            ins = nc.tensor.matmul(bank[j][:], a.wp[x][:, ch, out_ch * P:(out_ch + 1) * P],
                                                   a.aT[y][:, ch, half * HALF:(half + 1) * HALF],
                                                   start=(n + ch == 0), stop=(n == 2 and ch == NC - 1))
                    ins.then_inc(done, 1)

            @block.scalar
            def _(act):
                for j in range(4):
                    out_ch, half = j // 2, j % 2
                    act.wait_ge(done, j + 1)
                    nc.scalar.activation(c.out_t[:, out_ch, half * HALF:(half + 1) * HALF], bank[j][:],
                                         ACT.Identity, bias=c.vecs[:, 6 + out_ch:7 + out_ch]).then_inc(out, 1)


L0_CHUNKS = (18 * 176 + P - 1) // P
L1_CHUNKS = 32 * 96 // P


def threshold_block(c):
    row_statistics(c, "tb_norm", c.x)
    norm_to_feature_major(c, "tb_turn", c.x, c.rstd, c.shift)
    route(c, "tb_route", 32, 8, threshold=0.8)
    experts(c, "tb_moe", L1_CHUNKS)
    add_feature_major(c, "tb_out", c.out_t, c.x)


def build(nc, dram, out):
    with ExitStack() as ctx:
        c = Core(nc, ctx, dram)
        c.x = c.sb("x_res", [P, NT, D])
        c.ident = c.sb("ident_sb", [P, P])
        c.ident_bf = c.sb("ident_bf", [P, P], BF16)
        c.ones = c.sb("ones", [P, P])
        c.vecs = c.sb("vecs_sb", [P, 16])
        c.bn = c.sb("bn", [P, NT, 6])
        c.mean_var = c.sb("mean_var", [P, NT, 2])
        c.stat = c.sb("stat", [P, 4, NT])
        c.rstd = c.sb("rstd", [P, NT])
        c.shift = c.sb("shift", [P, NT])
        c.rms = c.sb("rms", [P, NT])
        c.out_t = c.sb("out_t", [P, NC, T])
        c.fT = [c.sb(f"fT{x}", [P, NC, T], F32R) for x in range(2)]
        c.hid = c.sb("hid", [P, NT, D])
        c.route_t = c.sb("route_t", [2 * ROWS, T], F32R)
        c.scale2 = c.sb("scale2", [P, NT])
        c.shift2 = c.sb("shift2", [P, NT])
        load_constants(c)
        head_attention(c)
        causal_block(c)
        routed_block(c)
        quantised_attention(c)
        threshold_block(c)
        store(c, out)


def store(c, out):
    nc = c.nc
    stored = c.sem("stored")
    with nc.Block() as block:

        @block.sync
        def _(sp):
            sp.dma_start(out, c.x[:]).then_inc(stored, 16)
            sp.wait_ge(stored, 16)



def chunks(gate, up, down, sizes, n_chunks):
    rows = n_chunks * P
    pad = lambda m: np.concatenate([m, np.zeros((rows - len(m), D), np.float32)])
    turned = lambda m: pad(m).reshape(n_chunks, P, NC, P).transpose(0, 3, 2, 1).reshape(n_chunks, P, NC * P)
    of_row = np.repeat(np.arange(len(sizes)), sizes)
    select = np.zeros((P, rows), np.float32)
    for part in range(2):
        select[ROWS * part + of_row, np.arange(len(of_row))] = 1.0
    select = select.reshape(P, n_chunks, P).transpose(1, 0, 2)
    return np.concatenate([turned(gate), turned(up), pad(down).reshape(n_chunks, P, D), select], axis=2)


def arrays_of(inputs):
    a = {k: np.asarray(v) for k, v in inputs.items()}
    out = {}
    out["x"] = a["x"].reshape(NT, P, D).transpose(1, 0, 2)
    ctx_t = a["ctx_2048"].reshape(T, D)
    out["ctx_tiles"] = ctx_t.reshape(NT, P, NC, P).transpose(0, 3, 2, 1)
    out["ident"] = np.eye(P, dtype=np.float32)
    feat = lambda m: m.reshape(NC, P, -1).transpose(1, 0, 2)
    out["ha_w"] = feat(np.concatenate([a["L0_xattn_Wq"].T, a["L0_xattn_Wk"].T, a["L0_xattn_Wv"].T,
                                       a["L0_xattn_Wo"].T], axis=1))
    out["ha_bias"] = np.concatenate([a["L0_xattn_bq"], a["L0_xattn_bk"], a["L0_xattn_bv"], a["L0_xattn_bo"]])[None]
    cols = np.concatenate([a["L0_ffn_ln1_w"].reshape(NC, P), a["L0_ffn_ln2_w"].reshape(NC, P)])
    out["vecs"] = np.concatenate([cols.T, a["L1_xattn_bkv"][D:].reshape(NC, P).T, a["L1_xattn_bp"].reshape(NC, P).T,
                                  np.zeros((P, 8), np.float32)], axis=1)
    out["ctx_t"] = feat(ctx_t.T)
    out["qa_w"] = feat(np.concatenate([a["L1_xattn_Wq"], a["L1_xattn_Wkv"], a["L1_xattn_Wp"]], axis=1))
    out["qa_bias"] = np.concatenate([a["L1_xattn_bq"], a["L1_xattn_bkv"][:D]])[None]
    head_rows = lambda m, step: m.reshape(NH, step, D)[:, :DH].reshape(PAIRS, 2 * DH, NC, P)
    kv = a["L0_ffn_kv_w"]
    qkv = np.stack([head_rows(a["L0_ffn_q_w"], QHD), head_rows(kv[:NH * DH], DH),
                    head_rows(kv[NH * DH:2 * NH * DH], DH)])
    out["ca_w"] = qkv.transpose(1, 4, 0, 3, 2)
    out["ca_wo"] = a["L0_ffn_o_w"].T.reshape(PAIRS, 2, DH, D).transpose(0, 2, 1, 3)
    out["mask"] = np.triu(np.full((P, P), -1e9, np.float32), 1)
    w1, w2, sh = a["L0_ffn_w1"], a["L0_ffn_w2"], a["L0_ffn_sh_gu_w"]
    out["rb_route_gate"] = feat(a["L0_ffn_gate_w"].T)
    out["rb_moe_w"] = chunks(np.concatenate([w1[:, :176].reshape(-1, D), sh[:352]]),
                             np.concatenate([w1[:, 176:].reshape(-1, D), sh[352:]]),
                             np.concatenate([w2.transpose(0, 2, 1).reshape(-1, D), a["L0_ffn_sh_down_w"].T]),
                             [176] * 16 + [352], L0_CHUNKS)
    gu, dn = a["L1_ffn_gate_up_proj"], a["L1_ffn_down_proj"]
    out["tb_route_gate"] = feat(a["L1_ffn_gate_weight"].T)
    out["tb_moe_w"] = chunks(gu[:, :96].reshape(-1, D), gu[:, 96:].reshape(-1, D),
                             dn.transpose(0, 2, 1).reshape(-1, D), [96] * 32, L1_CHUNKS)
    return {k: np.ascontiguousarray(v) for k, v in out.items()}


def kernel(**inputs):
    import concourse.bacc as bacc
    from concourse.bass_utils import run_bass_kernel_spmd

    nc = bacc.Bacc("TRN2", target_bir_lowering=False, num_devices=1)
    arrays = arrays_of(inputs)
    dram = {n: nc.dram_tensor("in_" + n, v.shape, mybir.dt.from_np(v.dtype), kind="ExternalInput").ap()
            for n, v in arrays.items()}
    out = nc.dram_tensor("out", (P, NT, D), F32, kind="ExternalOutput").ap()
    build(nc, dram, out)
    r = run_bass_kernel_spmd(nc, [{"in_" + n: v for n, v in arrays.items()}], core_ids=[0])
    y = r.results[0]["out"]
    return np.ascontiguousarray(y.transpose(1, 0, 2)).reshape(B, S, D)
```

```python
from contextlib import ExitStack

import numpy as np
import concourse.bass as bass
from concourse import mybir
from concourse.alu_op_type import AluOpType as ALU

F32 = mybir.dt.float32
F32R = mybir.dt.float32r
BF16 = mybir.dt.bfloat16
I16 = mybir.dt.int16
ACT = mybir.ActivationFunctionType
AX = mybir.AxisListType

P = 128
B, S, D = 4, 256, 256
T = B * S
NT = T // P
NC = D // P
H, HD = 16, 16
HALF = 512
NHALF = T // HALF


class Counter:

    def __init__(self, engine, sem):
        self.engine, self.sem, self.n = engine, sem, 0

    def after(self, instruction):
        self.n += 1
        instruction.then_inc(self.sem, 1)
        self.engine.wait_ge(self.sem, self.n)


class Core:

    def __init__(self, nc, ctx, dram):
        self.nc, self.ctx, self.dram = nc, ctx, dram
        self.stages = {}

    def sb(self, name, shape, dtype=F32, ctx=None):
        return (ctx or self.ctx).enter_context(self.nc.sbuf_tensor(name, shape, dtype))

    def ps(self, name, shape, dtype=F32, ctx=None):
        return (ctx or self.ctx).enter_context(self.nc.psum_tensor(name, shape, dtype))

    def sem(self, name):
        return self.ctx.enter_context(self.nc.semaphore(name))

    def shared_sems(self, stage, names):
        if stage not in self.stages:
            self.stages[stage] = ([self.sem(f"{stage}_{n}") for n in names], 0)
        sems, runs = self.stages[stage]
        self.stages[stage] = (sems, runs + 1)
        return sems, runs * NT

    def column(self, tensor, t):
        return tensor[:, t:t + 1] if isinstance(t, int) else tensor[:, bass.ds(t, 1)]


def f32(ap):
    return ap.bitcast(F32)


def load_constants(c):
    nc = c.nc
    loaded = c.sem("const_loaded")
    prepared = c.sem("const_prepared")
    with nc.Block() as block:

        @block.sync
        def _(sp):
            sp.dma_start(c.x[:], c.dram["x"]).then_inc(loaded, 16)
            sp.dma_start(c.ident[:], c.dram["ident"]).then_inc(loaded, 16)
            sp.dma_start(c.vecs[:], c.dram["vecs"]).then_inc(loaded, 16)
            sp.wait_ge(loaded, 48)

        @block.vector
        def _(dve):
            dve.wait_ge(loaded, 48)
            nc.vector.tensor_copy(c.ident_bf[:], c.ident[:]).then_inc(prepared, 1)
            nc.vector.memset(c.ones[:], 1.0).then_inc(prepared, 1)
            dve.wait_ge(prepared, 2)


def row_statistics(c, name, src, eps=1e-5, second_eps=None, meanwhile=None):
    nc = c.nc
    stats_done, root_done, own = c.sem(name + "_var"), c.sem(name + "_root"), c.sem(name + "_own")

    with nc.Block() as block:

        if meanwhile:
            block.sync(meanwhile)

        @block.vector
        def _(dve):
            step = Counter(dve, own)
            for t in range(NT):
                ins = nc.vector.bn_stats(c.bn[:, t, :], src[:, t, :])
            step.after(ins)
            for t in range(NT):
                ins = nc.vector.bn_aggr(c.mean_var[:, t, :], c.bn[:, t, :])
            step.after(ins)
            step.after(nc.vector.tensor_scalar(c.stat[:, 0, :], c.mean_var[:, :, 1], eps, None, ALU.add))
            inverse_root(c, dve, step, stats_done, root_done, 1, c.stat[:, 0, :], c.rstd[:])
            step.after(nc.vector.scalar_tensor_tensor(out=c.shift[:], in0=c.mean_var[:, :, 0], scalar=-1.0,
                                                      in1=c.rstd[:], op0=ALU.mult, op1=ALU.mult))
            if second_eps is not None:
                step.after(nc.vector.tensor_tensor(c.stat[:, 0, :], c.mean_var[:, :, 1], c.rstd[:], ALU.mult))
                step.after(nc.vector.tensor_tensor(c.stat[:, 0, :], c.stat[:, 0, :], c.rstd[:], ALU.mult))
                step.after(nc.vector.tensor_scalar(c.stat[:, 0, :], c.stat[:, 0, :], second_eps, None, ALU.add))
                inverse_root(c, dve, step, stats_done, root_done, 2, c.stat[:, 0, :], c.rms[:])

        @block.scalar
        def _(act):
            for n in range(1 if second_eps is None else 2):
                act.wait_ge(stats_done, n + 1)
                nc.scalar.activation(c.stat[:, 1, :], c.stat[:, 0, :], ACT.Sqrt).then_inc(root_done, 1)


def inverse_root(c, dve, step, ready, root_done, n, value, out):
    nc = c.nc
    nc.vector.tensor_copy(c.stat[:, 2, :], value).then_inc(ready, 1)
    dve.wait_ge(ready, n)
    dve.wait_ge(root_done, n)
    r, u = c.stat[:, 1, :], c.stat[:, 3, :]
    step.after(nc.vector.reciprocal(r, r))
    step.after(nc.vector.tensor_tensor(u, r, r, ALU.mult))
    step.after(nc.vector.tensor_tensor(u, u, value, ALU.mult))
    step.after(nc.vector.tensor_scalar(u, u, -0.5, 1.5, ALU.mult, ALU.add))
    step.after(nc.vector.tensor_tensor(out, r, u, ALU.mult))



POOL_HEADS = 11
FIRST_HEADS = 5


def head_attention(c):
    nc = c.nc
    with ExitStack() as ctx:
        w = c.sb("ha_w", [P, NC, 4 * D], ctx=ctx)
        bias = c.sb("ha_bias", [1, 4 * D], ctx=ctx)
        xn = [c.sb(f"ha_xn{k}", [P, D], ctx=ctx) for k in range(2)]
        xT = [c.sb(f"ha_xT{k}", [P, NC, P], ctx=ctx) for k in range(2)]
        cT = [c.sb(f"ha_cT{k}", [P, NC, P], ctx=ctx) for k in range(2)]
        q = [c.sb(f"ha_q{k}", [P, H, HD], ctx=ctx) for k in range(2)]
        kk = [c.sb(f"ha_k{k}", [P, H, HD], ctx=ctx) for k in range(2)]
        vT = [c.sb(f"ha_v{k}", [P, HD, H], ctx=ctx) for k in range(2)]
        ex = [c.sb(f"ha_ex{k}", [P, H, H], ctx=ctx) for k in range(2)]
        at = [c.sb(f"ha_at{k}", [P, H, HD], ctx=ctx) for k in range(2)]
        qk_prod = c.sb("ha_qk_prod", [P, H, H * HD], ctx=ctx)
        pv_prod = c.sb("ha_pv_prod", [P, H, HD * H], ctx=ctx)
        sc = c.sb("ha_sc", [P, H, H], ctx=ctx)
        red = c.sb("ha_red", [P, H], ctx=ctx)
        aT = c.sb("ha_aT", [P, NC, P], ctx=ctx)
        psT = c.ps("ha_psT", [P, NC * P], ctx=ctx)
        psQ = c.ps("ha_psQ", [P, D], ctx=ctx)
        psKV = c.ps("ha_psKV", [P, 2 * D], ctx=ctx)
        psA = c.ps("ha_psA", [P, NC * P], ctx=ctx)
        psO = c.ps("ha_psO", [P, D], ctx=ctx)
        w_loaded = c.sem("ha_w_loaded")
        ctx_loaded = [c.sem(f"ha_ctx_loaded{k}") for k in range(2)]
        normed = c.sem("ha_normed")
        x_turned = c.sem("ha_x_turned")
        xT_ready = c.sem("ha_xT_ready")
        qkv_done = c.sem("ha_qkv_done")
        qk_ready = c.sem("ha_qk_ready")
        v_ready = c.sem("ha_v_ready")
        qk_pool = c.sem("ha_qk_pool")
        scored = c.sem("ha_scored")
        sub_done = c.sem("ha_sub_done")
        exp_done = c.sem("ha_exp_done")
        prob_ready = c.sem("ha_prob_ready")
        pv_dve = c.sem("ha_pv_dve")
        pv_pool = c.sem("ha_pv_pool")
        at_ready = c.sem("ha_at_ready")
        at_turned = c.sem("ha_at_turned")
        aT_ready = c.sem("ha_aT_ready")
        out_done = c.sem("ha_out_done")
        own = c.sem("ha_own")
        added = c.sem("ha_added")
        OWN = 4
        AHEAD = 3

        def load_weights(sp):
            sp.dma_start(w[:], c.dram["ha_w"]).then_inc(w_loaded, 16)
            sp.dma_start(bias[:], c.dram["ha_bias"]).then_inc(w_loaded, 16)

        row_statistics(c, "ha_norm", c.x, meanwhile=load_weights)

        def turns(engine, body):
            body(0, 0)
            with engine.Fori(0, (NT - 1 - AHEAD) // 2) as i:
                for j in range(2):
                    body(i * 2 + (1 + j), (1 + j) % 2)
            for t in range(NT - AHEAD, NT):
                body(t, t % 2)

        def exists(t, ahead):
            return not isinstance(t, int) or t + ahead < NT

        def wait(engine, sem, count):
            if not (isinstance(count, int) and count <= 0):
                engine.wait_ge(sem, count)

        with nc.Block() as block:

            @block.sync
            def _(sp):
                def load(t, k):
                    wait(sp, qkv_done, t - 1)
                    sp.dma_start(cT[k][:], c.dram["ctx_tiles"][t]).then_inc(ctx_loaded[k], 16)

                in_pairs(sp, NT, load)

            @block.scalar
            def _(act):
                def norm(t, k):
                    nc.scalar.activation(xn[k][:], c.x[:, t, :], ACT.Identity, scale=c.column(c.rstd, t),
                                         bias=c.column(c.shift, t)).then_inc(normed, 1)

                def take_xT(t, k):
                    act.wait_ge(x_turned, t + 1)
                    nc.scalar.activation(xT[k][:].rearrange("p c t -> p (c t)"), psT[:],
                                         ACT.Copy).then_inc(xT_ready, 1)

                def take_qk(t, k):
                    act.wait_ge(qkv_done, t + 1)
                    nc.scalar.activation(q[k][:].rearrange("p h d -> p (h d)"), psQ[:], ACT.Copy)
                    nc.scalar.activation(kk[k][:].rearrange("p h d -> p (h d)"), psKV[:, 0:D],
                                         ACT.Copy).then_inc(qk_ready, 1)

                def take_v(t, k):
                    wait(act, pv_pool, t - 1)
                    wait(act, pv_dve, t - 1)
                    nc.scalar.activation(vT[k][:].rearrange("p d g -> p g d"),
                                         psKV[:, D:2 * D].rearrange("p (g d) -> p g d", g=H),
                                         ACT.Copy).then_inc(v_ready, 1)

                def exponential(t, k):
                    act.wait_ge(sub_done, t + 1)
                    wait(act, pv_pool, t - 1)
                    nc.scalar.activation(ex[k][:], sc[:], ACT.Exp).then_inc(exp_done, 1)

                def body(t, k):
                    if exists(t, 2):
                        take_qk(t + 2, k)
                    if exists(t, 3):
                        norm(t + 3, 1 - k)
                    if exists(t, 2):
                        take_v(t + 2, k)
                    if exists(t, 3):
                        take_xT(t + 3, 1 - k)
                    if exists(t, 1):
                        exponential(t + 1, 1 - k)
                    act.wait_ge(at_turned, t + 1)
                    nc.scalar.activation(aT[:].rearrange("p c t -> p (c t)"), psA[:],
                                         ACT.Copy).then_inc(aT_ready, 1)

                norm(0, 0)
                norm(1, 1)
                take_xT(0, 0)
                norm(2, 0)
                take_qk(0, 0)
                take_v(0, 0)
                take_xT(1, 1)
                take_qk(1, 1)
                take_v(1, 1)
                take_xT(2, 0)
                exponential(0, 0)
                turns(act, body)

            @block.tensor
            def _(pe):
                def front(t, k):
                    pe.wait_ge(normed, t + 1)
                    wait(pe, xT_ready, t)
                    for n in range(NC):
                        ins = nc.tensor.transpose(psT[:, n * P:(n + 1) * P], xn[k][:, n * P:(n + 1) * P], c.ident[:])
                    ins.then_inc(x_turned, 1)
                    pe.wait_ge(xT_ready, t + 1)
                    pe.wait_ge(ctx_loaded[k], loads_of_slot(t, k))
                    wait(pe, v_ready, t)
                    nc.tensor.matmul(psQ[:], c.ones[0:1, 0:P], bias[:, 0:D], start=True, stop=False)
                    for n in range(NC):
                        nc.tensor.matmul(psQ[:], xT[k][:, n, :], w[:, n, 0:D], start=False, stop=(n == NC - 1))
                    nc.tensor.matmul(psKV[:], c.ones[0:1, 0:P], bias[:, D:3 * D], start=True, stop=False)
                    for n in range(NC):
                        ins = nc.tensor.matmul(psKV[:], cT[k][:, n, :], w[:, n, D:3 * D], start=False,
                                               stop=(n == NC - 1))
                    ins.then_inc(qkv_done, 1)

                def body(t, k):
                    if exists(t, 3):
                        front(t + 3, 1 - k)
                    pe.wait_ge(at_ready, t + 1)
                    for n in range(NC):
                        ins = nc.tensor.transpose(psA[:, n * P:(n + 1) * P],
                                                  at[k][:, 8 * n:8 * n + 8, :].rearrange("p h d -> p (h d)"),
                                                  c.ident[:])
                    ins.then_inc(at_turned, 1)
                    wait(pe, added, t)
                    pe.wait_ge(aT_ready, t + 1)
                    nc.tensor.matmul(psO[:], c.ones[0:1, 0:P], bias[:, 3 * D:4 * D], start=True, stop=False)
                    for n in range(NC):
                        ins = nc.tensor.matmul(psO[:], aT[:, n, :], w[:, n, 3 * D:4 * D], start=False,
                                               stop=(n == NC - 1))
                    ins.then_inc(out_done, 1)

                pe.wait_ge(w_loaded, 32)
                for t in range(AHEAD):
                    front(t, t % 2)
                turns(pe, body)

            def qk_products(engine, h0, h1, k):
                n = h1 - h0
                return engine.tensor_tensor(qk_prod[:, h0:h1, :].rearrange("p h (g d) -> p h g d", d=HD),
                                            q[k][:, h0:h1, :].unsqueeze(2).to_broadcast([P, n, H, HD]),
                                            kk[k][:].unsqueeze(1).to_broadcast([P, n, H, HD]), ALU.mult)

            def pv_products(engine, h0, h1, k):
                n = h1 - h0
                return engine.tensor_tensor(pv_prod[:, h0:h1, :].rearrange("p h (d g) -> p h d g", g=H),
                                            ex[k][:, h0:h1, :].unsqueeze(2).to_broadcast([P, n, HD, H]),
                                            vT[k][:].unsqueeze(1).to_broadcast([P, n, HD, H]), ALU.mult)

            @block.gpsimd
            def _(pool):
                def qk(t, k):
                    pool.wait_ge(qk_ready, t + 1)
                    wait(pool, scored, t)
                    heads = FIRST_HEADS if isinstance(t, int) and t == 0 else POOL_HEADS
                    qk_products(nc.gpsimd, 0, heads, k).then_inc(qk_pool, 1)

                def body(t, k):
                    pool.wait_ge(prob_ready, t + 1)
                    wait(pool, at_ready, t)
                    pv_products(nc.gpsimd, 0, POOL_HEADS, k).then_inc(pv_pool, 1)
                    if exists(t, 2):
                        qk(t + 2, k)

                qk(0, 0)
                qk(1, 1)
                turns(pool, body)

            @block.vector
            def _(dve):
                def residual(t):
                    dve.wait_ge(out_done, t + 1)
                    nc.vector.tensor_tensor(c.x[:, t, :], c.x[:, t, :], psO[:], ALU.add).then_inc(added, 1)

                def products(t, k):
                    dve.wait_ge(qk_ready, t + 1)
                    heads = FIRST_HEADS if isinstance(t, int) and t == 0 else POOL_HEADS
                    qk_products(nc.vector, heads, H, k).then_inc(own, 1)

                def scores(t, k):
                    dve.wait_ge(own, t * OWN + 1)
                    dve.wait_ge(qk_pool, t + 1)
                    nc.vector.tensor_reduce(sc[:], qk_prod[:].rearrange("p h (g d) -> p h g d", g=H), AX.X,
                                            ALU.add).then_inc(scored, 1)

                def subtract_top(t):
                    dve.wait_ge(scored, t + 1)
                    nc.vector.tensor_reduce(red[:], sc[:], AX.X, ALU.max).then_inc(own, 1)
                    dve.wait_ge(own, t * OWN + 2)
                    nc.vector.tensor_tensor(sc[:], sc[:], red[:].unsqueeze(2).to_broadcast([P, H, H]),
                                            ALU.subtract).then_inc(sub_done, 1)

                def normalise(t, k):
                    dve.wait_ge(exp_done, t + 1)
                    nc.vector.tensor_reduce(red[:], ex[k][:], AX.X, ALU.add).then_inc(own, 1)
                    dve.wait_ge(own, t * OWN + 3)
                    nc.vector.reciprocal(red[:], red[:]).then_inc(own, 1)
                    dve.wait_ge(own, t * OWN + 4)
                    nc.vector.tensor_tensor(ex[k][:], ex[k][:], red[:].unsqueeze(2).to_broadcast([P, H, H]),
                                            ALU.mult).then_inc(prob_ready, 1)

                def body(t, k):
                    if exists(t, 1):
                        products(t + 1, 1 - k)
                    dve.wait_ge(v_ready, t + 1)
                    dve.wait_ge(prob_ready, t + 1)
                    pv_products(nc.vector, POOL_HEADS, H, k).then_inc(pv_dve, 1)
                    if exists(t, 1):
                        scores(t + 1, 1 - k)
                    if not (isinstance(t, int) and t == 0):
                        residual(t - 1)
                    if exists(t, 1):
                        subtract_top(t + 1)
                    dve.wait_ge(pv_dve, t + 1)
                    dve.wait_ge(pv_pool, t + 1)
                    nc.vector.tensor_reduce(at[k][:], pv_prod[:].rearrange("p h (d g) -> p h d g", d=HD), AX.X,
                                            ALU.add).then_inc(at_ready, 1)
                    if exists(t, 1):
                        normalise(t + 1, 1 - k)

                products(0, 0)
                scores(0, 0)
                subtract_top(0)
                normalise(0, 0)
                turns(dve, body)
                residual(NT - 1)



def causal_block(c):
    nc = c.nc
    row_statistics(c, "cb_norm", c.x, second_eps=1e-6)
    scaled, tile_step = c.sem("cb_scaled"), c.sem("cb_tile_step")
    with nc.Block() as block:

        @block.vector
        def _(dve):
            nc.vector.tensor_tensor(c.scale2[:], c.rstd[:], c.rms[:], ALU.mult).then_inc(scaled, 1)
            nc.vector.tensor_tensor(c.shift2[:], c.shift[:], c.rms[:], ALU.mult).then_inc(scaled, 1)
            dve.wait_ge(scaled, 2)

    def keep_normed(pool, t):
        nc.gpsimd.tensor_scalar(c.hid[:, t, :], c.x[:, t, :], c.column(c.rstd, t), c.column(c.shift, t),
                                ALU.mult, ALU.add).then_inc(tile_step, 1)

    norm_to_feature_major(c, "cb_turn", c.x, c.scale2, c.shift2, gain=0, tile_work=keep_normed)
    causal_attention(c)
    add_feature_major(c, "cb_out", c.out_t, c.hid)


PASSES = ((0, 0), (0, 1), (1, 0))


def in_pairs(engine, n, body, peel_last=False):
    straight = n % 2 or (2 if peel_last else 0)
    body(0, 0)
    body(1, 1)
    with engine.Fori(0, (n - 2 - straight) // 2) as i:
        for j in range(2):
            body(i * 2 + (2 + j), j)
    for t in range(n - straight, n):
        body(t, t % 2)


def loads_of_slot(t, k):
    return ((t - k) // 2 + 1) * 16 if isinstance(t, int) else (t - k) * 8 + 16


def norm_to_feature_major(c, name, src, scale, shift, gain=None, tile_work=None):
    nc = c.nc
    with ExitStack() as ctx:
        z = [c.sb(f"{name}_z{k}", [P, D], ctx=ctx) for k in range(2)]
        ps = [c.ps(f"{name}_ps{k}", [P, NC, P], ctx=ctx) for k in range(2)]
        (normed, turned, hi_done, lo_done), start = c.shared_sems("norm", ("normed", "turned", "hi", "lo"))

        def token(t):
            return slice(t * P, (t + 1) * P) if isinstance(t, int) else bass.ds(t * P, P)

        with nc.Block() as block:

            @block.scalar
            def _(act):
                def split_hi(t, k):
                    act.wait_ge(turned, start + t + 1)
                    for n in range(NC):
                        g = 1.0 if gain is None else c.vecs[:, gain + n:gain + n + 1]
                        ins = nc.scalar.activation(c.fT[0][:, n, token(t)], ps[k][:, n, :], ACT.Copy, scale=g)
                    ins.then_inc(hi_done, 1)

                def body(t, k):
                    nc.scalar.activation(z[k][:], src[:, t, :], ACT.Identity, scale=c.column(scale, t),
                                         bias=0.0 if shift is None else c.column(shift, t)).then_inc(normed, 1)
                    if not (isinstance(t, int) and t == 0):
                        split_hi(t - 1, 1 - k)

                in_pairs(act, NT, body)
                split_hi(NT - 1, 1)

            @block.tensor
            def _(pe):
                def body(t, k):
                    pe.wait_ge(normed, start + t + 1)
                    if not (isinstance(t, int) and t < 2):
                        pe.wait_ge(lo_done, start + t - 1)
                    for n in range(NC):
                        ins = nc.tensor.transpose(ps[k][:, n, :], z[k][:, n * P:(n + 1) * P], c.ident[:])
                    ins.then_inc(turned, 1)

                in_pairs(pe, NT, body)

            @block.vector
            def _(dve):
                def body(t, k):
                    dve.wait_ge(hi_done, start + t + 1)
                    for n in range(NC):
                        hi, lo = f32(c.fT[0][:, n, token(t)]), c.fT[1][:, n, token(t)]
                        if gain is None:
                            ins = nc.vector.tensor_tensor(lo, ps[k][:, n, :], hi, ALU.subtract)
                        else:
                            ins = nc.vector.scalar_tensor_tensor(
                                out=lo, in0=ps[k][:, n, :], scalar=c.vecs[:, gain + n:gain + n + 1], in1=hi,
                                op0=ALU.mult, op1=ALU.subtract)
                    ins.then_inc(lo_done, 1)

                in_pairs(dve, NT, body)

            if tile_work:

                @block.gpsimd
                def _(pool):
                    for t in range(NT):
                        tile_work(pool, t)


def add_feature_major(c, name, acc, dst, extra=None):
    nc = c.nc
    with ExitStack() as ctx:
        ps = [c.ps(f"{name}_ps{k}", [P, D], ctx=ctx) for k in range(4)]
        (turned, added), start = c.shared_sems("add", ("turned", "added"))
        base = c.sem(name + "_base") if extra is not None else None
        with nc.Block() as block:

            @block.tensor
            def _(pe):
                for t in range(NT):
                    if t >= 4:
                        pe.wait_ge(added, start + t - 3)
                    for n in range(NC):
                        ins = nc.tensor.transpose(ps[t % 4][:, n * P:(n + 1) * P], acc[:, n, t * P:(t + 1) * P],
                                                  c.ident[:])
                    ins.then_inc(turned, 1)

            if extra is not None:

                @block.gpsimd
                def _(pool):
                    for t in range(NT):
                        nc.gpsimd.tensor_tensor(dst[:, t, :], dst[:, t, :], extra[:, t, :], ALU.add).then_inc(base, 1)

            @block.vector
            def _(dve):
                for t in range(NT):
                    dve.wait_ge(turned, start + t + 1)
                    if extra is not None:
                        dve.wait_ge(base, t + 1)
                    nc.vector.tensor_tensor(dst[:, t, :], dst[:, t, :], ps[t % 4][:], ALU.add).then_inc(added, 1)



NH, DH, QHD = 16, 128, 192
PAIRS = NH // 2
QSCALE = float(QHD) ** -0.5


SPLITS = {2: (0,), 3: (1, 2)}
WO_SPLIT = 7


def causal_attention(c):
    nc = c.nc
    with ExitStack() as ctx:
        raw = c.sb("ca_raw", [P, 3, NC, 2 * DH], ctx=ctx)
        w = [c.sb(f"ca_w{x}", [P, 3, NC, 2 * DH], F32R, ctx=ctx) for x in range(2)]
        raw_o = c.sb("ca_raw_o", [DH, 2, D], ctx=ctx)
        wo = [c.sb(f"ca_wo{x}", [DH, 2, D], F32R, ctx=ctx) for x in range(2)]
        qk = [[c.sb(f"ca_{m}{x}", [DH, 2, T], F32R, ctx=ctx) for x in range(2)] for m in "qk"]
        v = [c.sb(f"ca_v{x}", [P, NT, 2 * DH], F32R, ctx=ctx) for x in range(2)]
        e = [c.sb(f"ca_e{k}", [P, 3 * P], ctx=ctx) for k in range(4)]
        pT = [[c.sb(f"ca_pT{k}{x}", [P, 3 * P], F32R, ctx=ctx) for x in range(2)] for k in range(2)]
        oT = [c.sb(f"ca_oT{x}", [DH, 2, T], F32R, ctx=ctx) for x in range(2)]
        top = c.sb("ca_top", [P, 4, 2], ctx=ctx)
        total = c.sb("ca_total", [P, 4, 2], ctx=ctx)
        inv = c.sb("ca_inv", [P, 4, 2], ctx=ctx)
        dummy = c.sb("ca_dummy", [P, 1], ctx=ctx)
        mask = c.sb("ca_mask", [P, P], BF16, ctx=ctx)
        mask_raw = c.sb("ca_mask_raw", [P, P], ctx=ctx)
        bank = [c.ps(f"ca_proj{k}", [P, HALF], ctx=ctx) for k in range(4)]
        ps_s = [c.ps(f"ca_s{k}", [P, 3 * P], ctx=ctx) for k in range(2)]
        ps_t = c.ps("ca_t", [P, 3 * P], ctx=ctx)
        ps_o = c.ps("ca_o", [DH, 2, S], ctx=ctx)

        mask_loaded = c.sem("ca_mask_loaded")
        mask_ready, zeroed = c.sem("ca_mask_ready"), c.sem("ca_zeroed")
        qkv_loaded, wo_loaded = c.sem("ca_qkv_loaded"), c.sem("ca_wo_loaded")
        w_hi, w_lo = c.sem("ca_w_hi"), c.sem("ca_w_lo")
        proj_done = c.sem("ca_proj_done")
        proj_hi = c.sem("ca_proj_hi")
        proj_lo = c.sem("ca_proj_lo")
        s_done = c.sem("ca_s_done")
        top_done = c.sem("ca_top_done")
        exp_done = c.sem("ca_exp_done")
        inv_done = c.sem("ca_inv_done")
        p_done = c.sem("ca_p_done")
        t_done = c.sem("ca_t_done")
        pT_hi, pT_lo = c.sem("ca_pT_hi"), c.sem("ca_pT_lo")
        pv_done = c.sem("ca_pv_done")
        oT_hi, oT_lo = c.sem("ca_oT_hi"), c.sem("ca_oT_lo")
        out_done = c.sem("ca_out_done")
        out_added = c.sem("ca_out_added")

        def bank_view(j):
            b = bank[j % 4]
            return b[:] if j < 8 else b[:].rearrange("p (t n) -> p t n", t=2)

        def projected(j, x):
            if j < 8:
                m, h, half = j // 4, j // 2 % 2, j % 2
                return qk[m][x][:, h, half * HALF:(half + 1) * HALF], QSCALE if m == 0 else 1.0
            t = 2 * (j - 8)
            return v[x][:, t:t + 2, :], 1.0

        def pairs(engine, body):
            body(0, True, False)
            with engine.Fori(0, PAIRS - 2) as i:
                body(i + 1, False, False)
            body(PAIRS - 1, False, True)

        def wait(engine, sem, count):
            if not (isinstance(count, int) and count <= 0):
                engine.wait_ge(sem, count)

        with nc.Block() as block:

            @block.sync
            def _(sp):
                sp.dma_start(mask_raw[:], c.dram["mask"]).then_inc(mask_loaded, 16)
                sp.dma_start(raw[:], c.dram["ca_w"][0]).then_inc(qkv_loaded, 16)
                sp.dma_start(raw_o[:], c.dram["ca_wo"][0]).then_inc(wo_loaded, 16)
                with sp.Fori(0, PAIRS - 1) as p:
                    sp.wait_ge(w_lo, p * 4 + 3)
                    sp.dma_start(raw[:], c.dram["ca_w"][p + 1]).then_inc(qkv_loaded, 16)
                    sp.wait_ge(w_lo, p * 4 + 7)
                    sp.dma_start(raw_o[:], c.dram["ca_wo"][p + 1]).then_inc(wo_loaded, 16)

            @block.gpsimd
            def _(pool):
                def split(part, count):
                    pool.wait_ge(w_hi, count)
                    if part == 3:
                        out, a, hi = wo[1][:], raw_o[:], f32(wo[0][:])
                    else:
                        out, a, hi = w[1][:, part], raw[:, part], f32(w[0][:, part])
                    nc.gpsimd.tensor_tensor(out, a, hi, ALU.subtract).then_inc(w_lo, 1)

                for part in range(3):
                    split(part, part + 1)

                def body(p, first, last):
                    for u in range(8):
                        k = u % 4
                        pool.wait_ge(inv_done, p * 8 + (u + 1))
                        nc.gpsimd.tensor_tensor(e[k][:, 0:P], e[k][:, 0:P], inv[:, k, 0:1].to_broadcast([P, P]),
                                                ALU.mult)
                        nc.gpsimd.tensor_tensor(e[k][:, P:], e[k][:, P:], inv[:, k, 1:2].to_broadcast([P, 2 * P]),
                                                ALU.mult).then_inc(p_done, 1)
                        for part in SPLITS.get(u, ()) if not last else ():
                            split(part, p * 4 + (4 + part))
                        if u == WO_SPLIT:
                            split(3, p * 4 + (4 if last else 7))

                pairs(pool, body)

            @block.scalar
            def _(act):
                nc.scalar.activation(dummy[:], c.ones[:, 0:1], ACT.Exp)

                def split(part, p):
                    if part == 3:
                        act.wait_ge(wo_loaded, p * 16 + 16)
                        wait(act, out_done, p * 4)
                        nc.scalar.activation(wo[0][:], raw_o[:], ACT.Copy).then_inc(w_hi, 1)
                    else:
                        act.wait_ge(qkv_loaded, p * 16 + 16)
                        wait(act, proj_done, p * 12)
                        nc.scalar.activation(w[0][:, part], raw[:, part], ACT.Copy).then_inc(w_hi, 1)

                def evacuate(p, j):
                    act.wait_ge(proj_done, p * 12 + (j + 1))
                    dst, scale = projected(j, 0)
                    nc.scalar.activation(dst, bank_view(j), ACT.Copy, scale=scale).then_inc(proj_hi, 1)

                for part in range(3):
                    split(part, 0)
                for j in range(8):
                    evacuate(0, j)

                def body(p, first, last):
                    for s in range(12):
                        if s == 0:
                            evacuate(p, 8)
                            evacuate(p, 9)
                        if s >= 8 and not last:
                            if s > 8:
                                evacuate(p + 1, 2 * (s - 9) + 1)
                            evacuate(p + 1, 2 * (s - 8))
                        if s >= 5 and s % 2 == 1:
                            b = (s - 5) // 2
                            act.wait_ge(pv_done, p * 8 + (2 * b + 2))
                            if b == 0:
                                wait(act, out_done, p * 4)
                            nc.scalar.activation(oT[0][:, :, b * S:(b + 1) * S], ps_o[:], ACT.Copy).then_inc(oT_hi, 1)
                        if 2 <= s < 10:
                            k = s % 2
                            act.wait_ge(t_done, p * 8 + (s - 1))
                            nc.scalar.activation(pT[k][0][:], ps_t[:], ACT.Copy).then_inc(pT_hi, 1)
                        if s < 8:
                            k, e_s = s % 4, ps_s[s % 2]
                            act.wait_ge(top_done, p * 8 + (s + 1))
                            nc.scalar.activation(e[k][:, 0:P], e_s[:, 0:P], ACT.Exp, bias=top[:, k, 0:1],
                                                 accum_out=total[:, k, 0:1])
                            nc.scalar.activation(e[k][:, P:], e_s[:, P:], ACT.Exp, bias=top[:, k, 1:2],
                                                 accum_out=total[:, k, 1:2]).then_inc(exp_done, 1)
                        if s == 1:
                            evacuate(p, 10)
                            evacuate(p, 11)
                        for part in SPLITS.get(s, ()) if not last else ():
                            split(part, p + 1)
                        if s == WO_SPLIT:
                            split(3, p)
                    if not last:
                        evacuate(p + 1, 7)

                pairs(act, body)

            @block.tensor
            def _(pe):
                def project(p, j):
                    if j >= 4:
                        pe.wait_ge(proj_lo, p * 12 + (j - 3))
                    else:
                        wait(pe, out_added, p * 4 - 4)
                    b, m = bank[j % 4], j // 4
                    if j < 8:
                        h, half = j // 2 % 2, j % 2
                        for n, (x, y) in enumerate(PASSES):
                            for ch in range(NC):
                                ins = nc.tensor.matmul(b[:], w[x][:, m, ch, h * DH:(h + 1) * DH],
                                                       c.fT[y][:, ch, half * HALF:(half + 1) * HALF],
                                                       start=(n + ch == 0), stop=(n == 2 and ch == NC - 1))
                    else:
                        for i in range(2):
                            t = 2 * (j - 8) + i
                            for n, (x, y) in enumerate(PASSES):
                                for ch in range(NC):
                                    ins = nc.tensor.matmul(b[:, i * 2 * DH:(i + 1) * 2 * DH],
                                                           c.fT[y][:, ch, t * P:(t + 1) * P], w[x][:, 2, ch, :],
                                                           start=(n + ch == 0), stop=(n == 2 and ch == NC - 1))
                    ins.then_inc(proj_done, 1)

                def scores(p, u):
                    b, h, k = u // 2, u % 2, u % 2
                    wait(pe, exp_done, p * 8 + (u - 1))
                    qh, kh = qk
                    for tile, c0, n_keys in ((0, 0, P), (1, P, 2 * P)):
                        q0 = b * S + tile * P
                        for n, (x, y) in enumerate(PASSES):
                            nc.tensor.matmul(ps_s[k][:, c0:c0 + n_keys], qh[x][:, h, q0:q0 + P],
                                             kh[y][:, h, b * S:b * S + n_keys], start=(n == 0), stop=False)
                        ins = nc.tensor.matmul(ps_s[k][:, c0 + n_keys - P:c0 + n_keys], c.ident_bf[:], mask[:],
                                               start=False, stop=True)
                    ins.then_inc(s_done, 1)

                def turn(p, u):
                    k = u % 4
                    pe.wait_ge(p_done, p * 8 + (u + 1))
                    wait(pe, pT_lo, p * 8 + u)
                    for n in range(3):
                        ins = nc.tensor.transpose(ps_t[:, n * P:(n + 1) * P], e[k][:, n * P:(n + 1) * P], c.ident[:])
                    ins.then_inc(t_done, 1)

                def weigh(p, u):
                    b, h, k = u // 2, u % 2, u % 2
                    pe.wait_ge(pT_lo, p * 8 + (u + 1))
                    if h == 0:
                        wait(pe, oT_lo, p * 4 + b)
                    for tile, q0, c0, n_q in ((0, 0, 0, 2 * P), (1, P, 2 * P, P)):
                        for n, (x, y) in enumerate(PASSES):
                            ins = nc.tensor.matmul(ps_o[:, h, q0:q0 + n_q], v[x][:, 2 * b + tile, h * DH:(h + 1) * DH],
                                                   pT[k][y][:, c0:c0 + n_q], start=(tile == 0 and n == 0),
                                                   stop=(tile == 1 and n == 2))
                    ins.then_inc(pv_done, 1)

                def output(j):
                    ch, half = j // 2, j % 2
                    for n, (x, y) in enumerate(PASSES):
                        for h in range(2):
                            ins = nc.tensor.matmul(bank[j][:], wo[x][:, h, ch * P:(ch + 1) * P],
                                                   oT[y][:, h, half * HALF:(half + 1) * HALF],
                                                   start=(n + h == 0), stop=(n == 2 and h == 1))
                    ins.then_inc(out_done, 1)

                pe.wait_ge(mask_ready, 1)
                for j in range(8):
                    if j % 4 == 0:
                        pe.wait_ge(w_lo, j // 4 + 1)
                    project(0, j)
                pe.wait_ge(w_lo, 3)

                def body(p, first, last):
                    for s in range(12):
                        if s == 0:
                            project(p, 8)
                            project(p, 9)
                            pe.wait_ge(proj_lo, p * 12 + 8)
                        if s >= 8 and not last:
                            if s == 8:
                                pe.wait_ge(w_lo, p * 4 + 6)
                            project(p + 1, 2 * (s - 8))
                        if s == 4:
                            pe.wait_ge(proj_lo, p * 12 + 12)
                        if s >= 4:
                            weigh(p, s - 4)
                        if s < 8:
                            scores(p, s)
                        if s == 1:
                            project(p, 10)
                            project(p, 11)
                        if 2 <= s < 10:
                            turn(p, s - 2)
                        if s in (2, 3) and not first:
                            if s == 2:
                                pe.wait_ge(oT_lo, p * 4)
                                pe.wait_ge(w_lo, p * 4 + 3)
                            for j in (2 * (s - 2), 2 * (s - 2) + 1):
                                pe.wait_ge(proj_lo, p * 12 + (9 + j))
                                output(j)
                        if s >= 8 and not last:
                            project(p + 1, 2 * (s - 8) + 1)

                pairs(pe, body)
                pe.wait_ge(oT_lo, PAIRS * 4)
                pe.wait_ge(w_lo, PAIRS * 4)
                pe.wait_ge(out_added, PAIRS * 4 - 4)
                for j in range(4):
                    output(j)

            @block.vector
            def _(dve):
                nc.vector.memset(c.out_t[:], 0.0).then_inc(zeroed, 1)
                dve.wait_ge(mask_loaded, 16)
                nc.vector.tensor_copy(mask[:], mask_raw[:]).then_inc(mask_ready, 1)
                dve.wait_ge(zeroed, 1)

                def evacuate(p, j):
                    dve.wait_ge(proj_hi, p * 12 + (j + 1))
                    hi, scale = projected(j, 0)
                    lo, _ = projected(j, 1)
                    if scale == 1.0:
                        ins = nc.vector.tensor_tensor(lo, bank_view(j), f32(hi), ALU.subtract)
                    else:
                        ins = nc.vector.scalar_tensor_tensor(out=lo, in0=bank_view(j), scalar=scale, in1=f32(hi),
                                                             op0=ALU.mult, op1=ALU.subtract)
                    ins.then_inc(proj_lo, 1)

                def add(p, j):
                    ch, half = j // 2, j % 2
                    dst = c.out_t[:, ch, half * HALF:(half + 1) * HALF]
                    dve.wait_ge(out_done, p * 4 + (j + 1))
                    wait(dve, out_added, p * 4)
                    nc.vector.tensor_tensor(dst, dst, bank[j][:], ALU.add).then_inc(out_added, 1)

                for j in range(8):
                    evacuate(0, j)

                def body(p, first, last):
                    for s in range(12):
                        if s == 0:
                            evacuate(p, 8)
                            evacuate(p, 9)
                        if s >= 8 and not last:
                            if s > 8:
                                evacuate(p + 1, 2 * (s - 9) + 1)
                            evacuate(p + 1, 2 * (s - 8))
                        if s >= 5 and s % 2 == 1:
                            b = (s - 5) // 2
                            dve.wait_ge(oT_hi, p * 4 + (b + 1))
                            nc.vector.tensor_tensor(oT[1][:, :, b * S:(b + 1) * S], ps_o[:],
                                                    f32(oT[0][:, :, b * S:(b + 1) * S]),
                                                    ALU.subtract).then_inc(oT_lo, 1)
                        if s < 8:
                            k, e_s = s % 4, ps_s[s % 2]
                            dve.wait_ge(s_done, p * 8 + (s + 1))
                            nc.vector.tensor_reduce(top[:, k, 0:1], e_s[:, 0:P], AX.X, ALU.max, negate=True)
                            nc.vector.tensor_reduce(top[:, k, 1:2], e_s[:, P:], AX.X, ALU.max,
                                                    negate=True).then_inc(top_done, 1)
                        if 2 <= s < 10:
                            k = s % 2
                            dve.wait_ge(pT_hi, p * 8 + (s - 1))
                            nc.vector.tensor_tensor(pT[k][1][:], ps_t[:], f32(pT[k][0][:]),
                                                    ALU.subtract).then_inc(pT_lo, 1)
                        if s < 8:
                            dve.wait_ge(exp_done, p * 8 + (s + 1))
                            nc.vector.reciprocal(inv[:, s % 4, :], total[:, s % 4, :]).then_inc(inv_done, 1)
                        if s == 1:
                            evacuate(p, 10)
                            evacuate(p, 11)
                        if s in (2, 3) and not first:
                            add(p - 1, 2 * (s - 2))
                            add(p - 1, 2 * (s - 2) + 1)
                    if not last:
                        evacuate(p + 1, 7)

                pairs(dve, body)
                for j in range(4):
                    add(PAIRS - 1, j)



ROWS = 32
WCOLS = 2 * NC * P + D + P


def top_k_mask(c, dve, step, probs, top, mask, n_experts):
    nc = c.nc
    for t in range(NT):
        ins = nc.vector.match_replace(mask[:, t, :], top[:, t, :], probs[:, t, :], -2.0)
    step.after(ins)
    step.after(nc.vector.tensor_tensor(mask[:], mask[:], probs[:], ALU.not_equal))


def route(c, name, n_experts, top_k, threshold=None, shared=False):
    nc = c.nc
    width = n_experts + 8
    with ExitStack() as ctx:
        gate = c.sb(name + "_gate", [P, NC, n_experts], ctx=ctx)
        g = [c.sb(f"{name}_g{x}", [P, NC, n_experts], F32R, ctx=ctx) for x in range(2)]
        probs = c.sb(name + "_probs", [P, NT, width], ctx=ctx)
        mask = c.sb(name + "_mask", [P, NT, width], ctx=ctx)
        top = c.sb(name + "_top", [P, NT, 8], ctx=ctx)
        kept = c.sb(name + "_kept", [P, NT, 8], ctx=ctx)
        share = c.sb(name + "_share", [P, NT, 8], ctx=ctx)
        red = c.sb(name + "_red", [P, NT], ctx=ctx)
        weights = c.sb(name + "_weights", [P, NT, ROWS], ctx=ctx)
        ps_l = c.ps(name + "_ps_l", [P, NT, n_experts], ctx=ctx)
        ps_w = [c.ps(f"{name}_ps_w{k}", [ROWS, HALF], ctx=ctx) for k in range(NHALF)]
        loaded, g_hi, g_lo = c.sem(name + "_loaded"), c.sem(name + "_g_hi"), c.sem(name + "_g_lo")
        logits, shifted, exped = c.sem(name + "_logits"), c.sem(name + "_shifted"), c.sem(name + "_exped")
        weighted, turned = c.sem(name + "_weighted"), c.sem(name + "_turned")
        hi_done, lo_done, own = c.sem(name + "_hi"), c.sem(name + "_lo"), c.sem(name + "_own")
        experts = probs[:, :, 0:n_experts]

        def spread(col, n):
            return col.unsqueeze(2).to_broadcast([P, NT, n])

        with nc.Block() as block:

            @block.sync
            def _(sp):
                sp.dma_start(gate[:], c.dram[name + "_gate"]).then_inc(loaded, 16)

            @block.scalar
            def _(act):
                act.wait_ge(loaded, 16)
                nc.scalar.activation(g[0][:], gate[:], ACT.Copy).then_inc(g_hi, 1)
                act.wait_ge(shifted, 1)
                nc.scalar.activation(experts, experts, ACT.Exp).then_inc(exped, 1)
                for k in range(NHALF):
                    act.wait_ge(turned, k + 1)
                    nc.scalar.activation(c.route_t[0:ROWS, k * HALF:(k + 1) * HALF], ps_w[k][:],
                                         ACT.Copy).then_inc(hi_done, 1)

            @block.tensor
            def _(pe):
                pe.wait_ge(g_lo, 1)
                for t in range(NT):
                    for n, (x, y) in enumerate(PASSES):
                        for ch in range(NC):
                            ins = nc.tensor.matmul(ps_l[:, t, :], c.fT[x][:, ch, t * P:(t + 1) * P], g[y][:, ch, :],
                                                   start=(n + ch == 0), stop=(n == 2 and ch == NC - 1))
                ins.then_inc(logits, 1)
                pe.wait_ge(weighted, 1)
                for t in range(NT):
                    k, c0 = t // 4, t % 4 * P
                    ins = nc.tensor.matmul(ps_w[k][:, c0:c0 + P], weights[:, t, :], c.ident[:], start=True, stop=True)
                    if t % 4 == 3:
                        ins.then_inc(turned, 1)

            @block.vector
            def _(dve):
                step = Counter(dve, own)
                dve.wait_ge(g_hi, 1)
                nc.vector.tensor_tensor(g[1][:], gate[:], f32(g[0][:]), ALU.subtract).then_inc(g_lo, 1)
                step.after(nc.vector.memset(probs[:], -1.0))
                step.after(nc.vector.memset(weights[:], 0.0))
                if shared:
                    step.after(nc.vector.memset(weights[:, :, n_experts:n_experts + 1], 1.0))
                step.after(nc.vector.memset(c.route_t[:].bitcast(F32), 0.0))
                dve.wait_ge(logits, 1)
                step.after(nc.vector.tensor_reduce(red[:], ps_l[:], AX.X, ALU.max))
                nc.vector.tensor_tensor(experts, ps_l[:], spread(red[:], n_experts), ALU.subtract).then_inc(shifted, 1)
                dve.wait_ge(exped, 1)
                step.after(nc.vector.tensor_reduce(red[:], experts, AX.X, ALU.add))
                step.after(nc.vector.reciprocal(red[:], red[:]))
                step.after(nc.vector.tensor_tensor(experts, experts, spread(red[:], n_experts), ALU.mult))
                for t in range(NT):
                    ins = nc.vector.max(out=top[:, t, :], in_=probs[:, t, :])
                step.after(ins)
                if threshold is None:
                    step.after(nc.vector.memset(top[:, :, top_k:8], -1.0))
                    step.after(nc.vector.tensor_reduce(red[:], top[:, :, 0:top_k], AX.X, ALU.add))
                else:
                    step.after(nc.vector.tensor_reduce(red[:], top[:], AX.X, ALU.add))
                    step.after(nc.vector.tensor_scalar(red[:], red[:], 1e-12, None, ALU.max))
                    step.after(nc.vector.reciprocal(red[:], red[:]))
                    step.after(nc.vector.tensor_tensor(share[:], top[:], spread(red[:], 8), ALU.mult))
                    for j in range(1, top_k):
                        step.after(nc.vector.tensor_tensor(share[:, :, j], share[:, :, j], share[:, :, j - 1], ALU.add))
                    step.after(nc.vector.memset(kept[:, :, 0:1], 1.0))
                    step.after(nc.vector.tensor_scalar(kept[:, :, 1:8], share[:, :, 0:7], threshold, None, ALU.is_lt))
                    step.after(nc.vector.tensor_tensor(top[:], top[:], kept[:], ALU.mult))
                    step.after(nc.vector.tensor_reduce(red[:], top[:], AX.X, ALU.add))
                    step.after(nc.vector.tensor_scalar(kept[:], kept[:], -1.0, None, ALU.add))
                    step.after(nc.vector.tensor_tensor(top[:], top[:], kept[:], ALU.add))
                    step.after(nc.vector.tensor_scalar(red[:], red[:], 1e-12, None, ALU.max))
                top_k_mask(c, dve, step, probs, top, mask, n_experts)
                step.after(nc.vector.reciprocal(red[:], red[:]))
                step.after(nc.vector.tensor_tensor(experts, experts, mask[:, :, 0:n_experts], ALU.mult))
                nc.vector.tensor_tensor(weights[:, :, 0:n_experts], experts, spread(red[:], n_experts),
                                        ALU.mult).then_inc(weighted, 1)
                for k in range(NHALF):
                    dve.wait_ge(hi_done, k + 1)
                    cols = slice(k * HALF, (k + 1) * HALF)
                    nc.vector.tensor_tensor(c.route_t[ROWS:2 * ROWS, cols], ps_w[k][:],
                                            f32(c.route_t[0:ROWS, cols]), ALU.subtract).then_inc(lo_done, 1)


def experts(c, name, n_chunks):
    nc = c.nc
    with ExitStack() as ctx:
        raw = [c.sb(f"{name}_raw{k}", [P, WCOLS], ctx=ctx) for k in range(2)]
        w = [[c.sb(f"{name}_w{k}{x}", [P, WCOLS], F32R, ctx=ctx) for x in range(2)] for k in range(2)]
        gated = [c.sb(f"{name}_gated{k}", [P, HALF], ctx=ctx) for k in range(2)]
        routed = [c.sb(f"{name}_routed{k}", [P, HALF], ctx=ctx) for k in range(2)]
        inner = [c.sb(f"{name}_inner{k}", [P, HALF], ctx=ctx) for k in range(2)]
        a = [[c.sb(f"{name}_a{k}{x}", [P, HALF], F32R, ctx=ctx) for x in range(2)] for k in range(2)]
        zeros = c.sb(name + "_zeros", [P, HALF], BF16, ctx=ctx)
        ps_g = [c.ps(f"{name}_ps_g{k}", [P, HALF], ctx=ctx) for k in range(2)]
        ps_u = c.ps(name + "_ps_u", [P, HALF], ctx=ctx)
        ps_r = c.ps(name + "_ps_r", [P, HALF], ctx=ctx)
        acc = [[c.ps(f"{name}_acc{ch}{h}", [P, HALF], ctx=ctx) for h in range(NHALF)] for ch in range(NC)]
        loaded = [c.sem(f"{name}_loaded{k}") for k in range(2)]
        zeroed = c.sem(name + "_zeroed")
        w_hi, w_lo = c.sem(name + "_w_hi"), c.sem(name + "_w_lo")
        gate_done = c.sem(name + "_gate_done")
        route_done = c.sem(name + "_route_done")
        up_done = c.sem(name + "_up_done")
        down_done = c.sem(name + "_down_done")
        silu_done = c.sem(name + "_silu_done")
        routed_done = c.sem(name + "_routed_done")
        inner_done = c.sem(name + "_inner_done")
        a_hi, a_lo = c.sem(name + "_a_hi"), c.sem(name + "_a_lo")
        taken = c.sem(name + "_taken")

        def gate_up(m, ch):
            c0 = (m * NC + ch) * P
            return slice(c0, c0 + P)

        def down(ch):
            c0 = 2 * NC * P + ch * P
            return slice(c0, c0 + P)

        select = slice(WCOLS - P, WCOLS)
        zero = lambda x: isinstance(x, int) and x == 0

        with nc.Block() as block:

            @block.sync
            def _(sp):
                def load(ck, k):
                    if not (isinstance(ck, int) and ck < 2):
                        sp.wait_ge(w_lo, ck - 1)
                    sp.dma_start(raw[k][:], c.dram[name + "_w"][ck]).then_inc(loaded[k], 16)

                in_pairs(sp, n_chunks, load)

            @block.gpsimd
            def _(pool):
                def split(ck, k):
                    pool.wait_ge(w_hi, ck + 1)
                    nc.gpsimd.tensor_tensor(w[k][1][:], raw[k][:], f32(w[k][0][:]), ALU.subtract).then_inc(w_lo, 1)

                in_pairs(pool, n_chunks, split)

            @block.scalar
            def _(act):
                def split(ck, k):
                    act.wait_ge(loaded[k], loads_of_slot(ck, k))
                    if not (isinstance(ck, int) and ck < 2):
                        act.wait_ge(down_done, ck * 2 - 2)
                    nc.scalar.activation(w[k][0][:], raw[k][:], ACT.Copy).then_inc(w_hi, 1)

                def take_hi(n, h):
                    act.wait_ge(inner_done, n + 1)
                    nc.scalar.activation(a[h][0][:], inner[h][:], ACT.Copy).then_inc(a_hi, 1)

                def body(ck, k):
                    for h in range(2):
                        n = ck * 2 + h
                        if not zero(n):
                            take_hi(n - 1, 1 - h)
                        if h == 1 and not (isinstance(ck, int) and ck == n_chunks - 1):
                            split(ck + 1, 1 - k)
                        act.wait_ge(gate_done, n + 1)
                        nc.scalar.activation(gated[h][:], ps_g[h][:], ACT.Silu).then_inc(silu_done, 1)

                split(0, 0)
                in_pairs(act, n_chunks, body, peel_last=True)
                take_hi(2 * n_chunks - 1, 1)
                act.wait_ge(down_done, 2 * n_chunks)
                for ch in range(NC):
                    for h in range(NHALF):
                        nc.scalar.activation(c.out_t[:, ch, h * HALF:(h + 1) * HALF], acc[ch][h][:],
                                             ACT.Copy).then_inc(taken, 1)

            @block.tensor
            def _(pe):
                def down_products(n, h, k):
                    pe.wait_ge(a_lo, n + 1)
                    for ch in range(NC):
                        for x, y in PASSES:
                            ins = nc.tensor.matmul(acc[ch][h][:], w[k][x][:, down(ch)], a[h][y][:], start=False,
                                                   stop=False, skip_group_check=True)
                    ins.then_inc(down_done, 1)

                def body(ck, k):
                    pe.wait_ge(w_lo, ck + 1)
                    for h in range(2):
                        n = ck * 2 + h
                        cols = slice(h * HALF, (h + 1) * HALF)
                        for i, (x, y) in enumerate(PASSES):
                            for ch in range(NC):
                                ins = nc.tensor.matmul(ps_g[h][:], w[k][x][:, gate_up(0, ch)], c.fT[y][:, ch, cols],
                                                       start=(i + ch == 0), stop=(i == 2 and ch == NC - 1))
                        ins.then_inc(gate_done, 1)
                        pe.wait_ge(routed_done, n)
                        nc.tensor.matmul(ps_r[:], w[k][0][0:2 * ROWS, select], c.route_t[:, cols], start=True,
                                         stop=True).then_inc(route_done, 1)
                        pe.wait_ge(inner_done, n)
                        for i, (x, y) in enumerate(PASSES):
                            for ch in range(NC):
                                ins = nc.tensor.matmul(ps_u[:], w[k][x][:, gate_up(1, ch)], c.fT[y][:, ch, cols],
                                                       start=(i + ch == 0), stop=(i == 2 and ch == NC - 1))
                        ins.then_inc(up_done, 1)
                        if not zero(n):
                            down_products(n - 1, 1 - h, k if h == 1 else 1 - k)

                pe.wait_ge(zeroed, 1)
                for ch in range(NC):
                    for h in range(NHALF):
                        nc.tensor.matmul(acc[ch][h][:], zeros[:, 0:P], zeros[:], start=True, stop=False,
                                         skip_group_check=True)
                in_pairs(pe, n_chunks, body)
                down_products(2 * n_chunks - 1, 1, (n_chunks - 1) % 2)

            @block.vector
            def _(dve):
                nc.vector.memset(zeros[:], 0.0).then_inc(zeroed, 1)

                def take_lo(n, h):
                    dve.wait_ge(a_hi, n + 1)
                    nc.vector.tensor_tensor(a[h][1][:], inner[h][:], f32(a[h][0][:]), ALU.subtract).then_inc(a_lo, 1)

                def body(ck, k):
                    for h in range(2):
                        n = ck * 2 + h
                        if not zero(n):
                            take_lo(n - 1, 1 - h)
                        dve.wait_ge(silu_done, n + 1)
                        dve.wait_ge(route_done, n + 1)
                        if not zero(n):
                            dve.wait_ge(inner_done, n)
                        nc.vector.tensor_tensor(routed[h][:], ps_r[:], gated[h][:], ALU.mult).then_inc(routed_done, 1)
                        dve.wait_ge(up_done, n + 1)
                        dve.wait_ge(routed_done, n + 1)
                        if not zero(n):
                            dve.wait_ge(a_lo, n - 1)
                        nc.vector.tensor_tensor(inner[h][:], ps_u[:], routed[h][:], ALU.mult).then_inc(inner_done, 1)

                in_pairs(dve, n_chunks, body)
                take_lo(2 * n_chunks - 1, 1)


def routed_block(c):
    nc = c.nc
    squared, root, own = c.sem("rb_squared"), c.sem("rb_root"), c.sem("rb_own")
    with ExitStack() as ctx:
        sq = c.sb("rb_sq", [P, NT, D], ctx=ctx)
        with nc.Block() as block:

            @block.vector
            def _(dve):
                step = Counter(dve, own)
                step.after(nc.vector.tensor_tensor(sq[:], c.hid[:], c.hid[:], ALU.mult))
                step.after(nc.vector.tensor_reduce(c.stat[:, 0, :], sq[:], AX.X, ALU.add))
                step.after(nc.vector.tensor_scalar(c.stat[:, 0, :], c.stat[:, 0, :], 1.0 / D, 1e-6, ALU.mult, ALU.add))
                inverse_root(c, dve, step, squared, root, 1, c.stat[:, 0, :], c.rms[:])

            @block.scalar
            def _(act):
                act.wait_ge(squared, 1)
                nc.scalar.activation(c.stat[:, 1, :], c.stat[:, 0, :], ACT.Sqrt).then_inc(root, 1)

    norm_to_feature_major(c, "rb_turn", c.hid, c.rms, None, gain=NC)
    route(c, "rb_route", 16, 4, shared=True)
    experts(c, "rb_moe", L0_CHUNKS)
    add_feature_major(c, "rb_out", c.out_t, c.x, extra=c.hid)



SLOT = 4 * HD
LN255 = float(np.log(255.0))
NPAIR = H // 2


def quantised_attention(c):
    row_statistics(c, "qa_norm", c.x)
    norm_to_feature_major(c, "qa_turn", c.x, c.rstd, c.shift)
    with ExitStack() as ctx:
        a = Core(c.nc, ctx, c.dram)
        a.sq = a.sb("qa_sq", [P, NT, H])
        a.sv = a.sb("qa_sv", [P, NC])
        a.q_parts = a.sb("qa_q_parts", [P, NPAIR, T], BF16)
        a.k_parts = a.sb("qa_k_parts", [P, NPAIR, T], BF16)
        a.v_int = a.sb("qa_v_int", [P, NT, D], BF16)
        a.wp = [a.sb(f"qa_wp{x}", [P, NC, D], F32R) for x in range(2)]
        quantise(c, a)
        a.aT = [a.sb(f"qa_aT{x}", [P, NC, T], F32R) for x in range(2)]
        attend(c, a)
        project_out(c, a)
    add_feature_major(c, "qa_out", c.out_t, c.x)


def quantise(c, a):
    nc = c.nc
    with ExitStack() as ctx:
        q_rows = c.sb("qa_q_rows", [P, NT, H, 4, HD], BF16, ctx=ctx)
        k_rows = c.sb("qa_k_rows", [P, NT, H, 4, HD], BF16, ctx=ctx)
        v_cols = c.sb("qa_v_cols", [P, NC, T], BF16, ctx=ctx)
        with ExitStack() as inner:
            project_in(c, a, inner, q_rows, k_rows, v_cols)
        slots = [c.ps(f"qa_ps_slot{k}", [P, T], BF16, ctx=ctx) for k in range(4)]
        turned, by_act, by_dve = c.sem("qa_turned"), c.sem("qa_turned_act"), c.sem("qa_turned_dve")
        groups = [("q", n) for n in range(NPAIR)] + [("k", n) for n in range(NPAIR)] + [("v", n) for n in range(NC)]

        def source(kind, n, t):
            if kind == "v":
                return v_cols[:, n, t * P:(t + 1) * P]
            rows = q_rows if kind == "q" else k_rows
            return rows[:, t, 2 * n:2 * n + 2].rearrange("p h s d -> p (h s d)")

        def target(kind, n):
            if kind == "v":
                return a.v_int[:, :, n * P:(n + 1) * P]
            return (a.q_parts if kind == "q" else a.k_parts)[:, n, :].rearrange("p (t n) -> p t n", t=NT)

        def slot(g):
            return slots[g % 4][:].rearrange("p (t n) -> p t n", t=NT)

        with nc.Block() as block:

            @block.tensor
            def _(pe):
                for g, (kind, n) in enumerate(groups):
                    if g >= 4:
                        pe.wait_ge(by_act if g % 2 else by_dve, (g - 4) // 2 + 1)
                    for t in range(NT):
                        ins = nc.tensor.transpose(slots[g % 4][:, t * P:(t + 1) * P], source(kind, n, t),
                                                  c.ident_bf[:])
                    ins.then_inc(turned, 1)

            @block.scalar
            def _(act):
                for g in range(1, len(groups), 2):
                    act.wait_ge(turned, g + 1)
                    nc.scalar.activation(target(*groups[g]), slot(g), ACT.Copy).then_inc(by_act, 1)

            @block.vector
            def _(dve):
                for g in range(0, len(groups), 2):
                    dve.wait_ge(turned, g + 1)
                    nc.vector.tensor_copy(target(*groups[g]), slot(g)).then_inc(by_dve, 1)


def project_in(c, a, ctx, q_rows, k_rows, v_cols):
    nc = c.nc
    w_raw = c.sb("qa_w_raw", [P, NC, 4 * D], ctx=ctx)
    w = [c.sb(f"qa_w{x}", [P, NC, 3 * D], F32R, ctx=ctx) for x in range(2)]
    ctx_raw = c.sb("qa_ctx_raw", [P, NC, T], ctx=ctx)
    cT = [c.sb(f"qa_cT{x}", [P, NC, T], F32R, ctx=ctx) for x in range(2)]
    bias = c.sb("qa_bias", [1, 2 * D], ctx=ctx)
    qf = c.sb("qa_qf", [P, NT * H, HD], ctx=ctx)
    kf = c.sb("qa_kf", [P, NT * H, HD], ctx=ctx)
    vf = c.out_t
    ints = c.sb("qa_ints", [P, NT * H, HD], I16, ctx=ctx)
    v_ints = c.sb("qa_v_ints", [P, T], I16, ctx=ctx)
    rest = c.hid[:].rearrange("p t (h d) -> p (t h) d", d=HD)
    sk = c.sb("qa_sk", [P, NT * H], ctx=ctx)
    inv = c.sb("qa_inv_scale", [P, NT * H], ctx=ctx)
    inv_v = c.sb("qa_inv_v", [P, NC], ctx=ctx)
    bank = [c.ps(f"qa_bank{k}", [P, HALF], ctx=ctx) for k in range(8)]
    loaded = c.sem("qa_loaded")
    hi_done, lo_done = c.sem("qa_hi"), c.sem("qa_lo")
    done = c.sem("qa_proj_done")
    out = c.sem("qa_proj_out")
    own = c.sem("qa_quant_own")
    sq = a.sq[:].rearrange("p t h -> p (t h)")

    with nc.Block() as block:

        @block.sync
        def _(sp):
            sp.dma_start(w_raw[:], c.dram["qa_w"]).then_inc(loaded, 16)
            sp.dma_start(ctx_raw[:], c.dram["ctx_t"]).then_inc(loaded, 16)
            sp.dma_start(bias[:], c.dram["qa_bias"]).then_inc(loaded, 16)

        @block.gpsimd
        def _(pool):
            pool.wait_ge(hi_done, 2)
            nc.gpsimd.tensor_tensor(w[1][:], w_raw[:, :, 0:3 * D], f32(w[0][:]), ALU.subtract).then_inc(lo_done, 1)
            nc.gpsimd.tensor_tensor(a.wp[1][:], w_raw[:, :, 3 * D:], f32(a.wp[0][:]), ALU.subtract).then_inc(lo_done, 1)
            pool.wait_ge(hi_done, 3)
            nc.gpsimd.tensor_tensor(cT[1][:], ctx_raw[:], f32(cT[0][:]), ALU.subtract).then_inc(lo_done, 1)

        @block.scalar
        def _(act):
            act.wait_ge(loaded, 48)
            nc.scalar.activation(w[0][:], w_raw[:, :, 0:3 * D], ACT.Copy).then_inc(hi_done, 1)
            nc.scalar.activation(a.wp[0][:], w_raw[:, :, 3 * D:], ACT.Copy).then_inc(hi_done, 1)
            nc.scalar.activation(cT[0][:], ctx_raw[:], ACT.Copy).then_inc(hi_done, 1)
            for j in range(8):
                act.wait_ge(done, j + 1)
                dst = (qf, kf)[j // 4][:, (j % 4) * 2 * H:(j % 4 + 1) * 2 * H, :]
                nc.scalar.activation(dst.rearrange("p h d -> p (h d)"), bank[j][:], ACT.Copy).then_inc(out, 1)
            for j in range(4):
                act.wait_ge(done, j + 9)
                ch, half = j // 2, j % 2
                nc.scalar.activation(vf[:, ch, half * HALF:(half + 1) * HALF], bank[j][:], ACT.Identity,
                                     bias=c.vecs[:, 4 + ch:5 + ch]).then_inc(out, 1)

        @block.tensor
        def _(pe):
            pe.wait_ge(lo_done, 1)
            for m in range(2):
                if m == 1:
                    pe.wait_ge(lo_done, 3)
                src = (c.fT, cT)[m]
                for t in range(NT):
                    dst = bank[4 * m + t // 2][:, (t % 2) * D:(t % 2 + 1) * D]
                    nc.tensor.matmul(dst, c.ones[0:1, 0:P], bias[:, m * D:(m + 1) * D], start=True, stop=False)
                    for n, (x, y) in enumerate(PASSES):
                        for ch in range(NC):
                            ins = nc.tensor.matmul(dst, src[x][:, ch, t * P:(t + 1) * P],
                                                   w[y][:, ch, m * D:(m + 1) * D], start=False,
                                                   stop=(n == 2 and ch == NC - 1))
                    if t % 2:
                        ins.then_inc(done, 1)
            for j in range(4):
                pe.wait_ge(out, j + 1)
                out_ch, half = j // 2, j % 2
                for n, (x, y) in enumerate(PASSES):
                    for ch in range(NC):
                        ins = nc.tensor.matmul(bank[j][:], w[x][:, ch, 2 * D + out_ch * P:2 * D + (out_ch + 1) * P],
                                               cT[y][:, ch, half * HALF:(half + 1) * HALF], start=(n + ch == 0),
                                               stop=(n == 2 and ch == NC - 1))
                ins.then_inc(done, 1)

        @block.vector
        def _(dve):
            step = Counter(dve, own)

            def spread(col):
                return col.unsqueeze(2).to_broadcast([P, NT * H, HD])

            def integers(values, scale, factor):
                step.after(nc.vector.tensor_reduce(scale, values[:], AX.X, ALU.max, apply_absolute_value=True))
                step.after(nc.vector.tensor_scalar(scale, scale, factor / 127.0, 1e-8, ALU.mult, ALU.max))
                step.after(nc.vector.reciprocal(inv[:], scale))
                if factor != 1.0:
                    step.after(nc.vector.tensor_scalar(inv[:], inv[:], factor, None, ALU.mult))
                step.after(nc.vector.tensor_tensor(ints[:], values[:], spread(inv[:]), ALU.mult))

            def rows(tensor, part):
                return tensor[:, :, :, part, :].rearrange("p t h d -> p (t h) d")

            step.after(nc.vector.memset(rows(q_rows, 3), 0.0))
            step.after(nc.vector.memset(rows(k_rows, 3), 0.0))
            dve.wait_ge(out, 4)
            integers(qf, sq, HD ** -0.5)
            for part in range(3):
                ins = nc.vector.tensor_scalar(rows(q_rows, part), ints[:], 127.0, -127.0, ALU.min, ALU.max)
            step.after(ins)
            dve.wait_ge(out, 8)
            integers(kf, sk[:], 1.0)
            step.after(nc.vector.tensor_scalar(kf[:], ints[:], 127.0, -127.0, ALU.min, ALU.max))
            step.after(nc.vector.tensor_tensor(rest, kf[:], spread(sk[:]), ALU.mult))
            for part in range(3):
                step.after(nc.vector.tensor_copy(rows(k_rows, part), rest))
                if part < 2:
                    step.after(nc.vector.tensor_tensor(rest, rest, rows(k_rows, part), ALU.subtract))
            dve.wait_ge(out, 12)
            step.after(nc.vector.tensor_reduce(a.sv[:], vf[:], AX.X, ALU.max, apply_absolute_value=True))
            step.after(nc.vector.tensor_scalar(a.sv[:], a.sv[:], 1.0 / 127.0, 1e-8, ALU.mult, ALU.max))
            step.after(nc.vector.reciprocal(inv_v[:], a.sv[:]))
            for ch in range(NC):
                step.after(nc.vector.tensor_scalar(v_ints[:], vf[:, ch, :], inv_v[:, ch:ch + 1], None, ALU.mult))
                step.after(nc.vector.tensor_scalar(v_cols[:, ch, :], v_ints[:], 127.0, -127.0, ALU.min, ALU.max))


def attend(c, a):
    nc = c.nc
    LAG_T, LAG_V = 2, 3
    with ExitStack() as ctx:
        q_now = c.sb("qa_q_now", [P, NPAIR, P], BF16, ctx=ctx)
        e = [c.sb(f"qa_e{k}", [P, T], I16, ctx=ctx) for k in range(4)]
        pT = [c.sb(f"qa_pT{k}", [P, T], BF16, ctx=ctx) for k in range(2)]
        top = c.sb("qa_top", [P, 4], ctx=ctx)
        shift = c.sb("qa_shift", [P, 4], ctx=ctx)
        total = c.sb("qa_total", [P, NT, H], ctx=ctx)
        inv = c.sb("qa_inv", [P, H], ctx=ctx)
        at = c.sb("qa_at", [P, H, HD], ctx=ctx)
        dummy = c.sb("qa_dummy", [P, 1], ctx=ctx)
        ps_s = [c.ps(f"qa_s{k}", [P, T], ctx=ctx) for k in range(2)]
        ps_t = [c.ps(f"qa_t{k}", [P, T], BF16, ctx=ctx) for k in range(2)]
        ps_o = c.ps("qa_o", [P, H, HD], ctx=ctx)
        ps_a = c.ps("qa_a", [P, NC, P], ctx=ctx)
        q_ready = c.sem("qa_q_ready")
        s_done = c.sem("qa_s_done")
        top_done = c.sem("qa_top_done")
        shift_done = c.sem("qa_shift_done")
        exp_done = c.sem("qa_exp_done")
        t_done = c.sem("qa_t_done")
        out_dve, out_act = c.sem("qa_out_dve"), c.sem("qa_out_act")
        pv_done = c.sem("qa_pv_done")
        inv_done = c.sem("qa_inv_done")
        at_done = c.sem("qa_at_done")
        a_turned = c.sem("qa_a_turned")
        a_hi, a_lo = c.sem("qa_a_hi"), c.sem("qa_a_lo")

        def tiles(engine, body):
            body(0, True)
            with engine.Fori(0, NT - 1) as i:
                body(i + 1, False)

        def tokens(t):
            return slice(t * P, (t + 1) * P) if isinstance(t, int) else bass.ds(t * P, P)

        with nc.Block() as block:

            @block.gpsimd
            def _(pool):
                def body(t, first):
                    for half in range(2):
                        if not first:
                            pool.wait_ge(s_done, t * H - (H // 2) * (1 - half))
                        heads = slice(half * NPAIR // 2, (half + 1) * NPAIR // 2)
                        nc.gpsimd.tensor_copy(q_now[:, heads], a.q_parts[:, heads, tokens(t)]).then_inc(q_ready, 1)

                tiles(pool, body)

            @block.tensor
            def _(pe):
                def scores(t, h):
                    pe.wait_ge(exp_done, t * H + h + 1)
                    r0 = (h % 2) * SLOT
                    for half in range(2):
                        ins = nc.tensor.matmul(ps_s[h % 2][:, half * HALF:(half + 1) * HALF],
                                               q_now[r0:r0 + 3 * HD, h // 2, :],
                                               a.k_parts[r0:r0 + 3 * HD, h // 2, half * HALF:(half + 1) * HALF],
                                               start=True, stop=True)
                    ins.then_inc(s_done, 1)

                def turn(t, h):
                    pe.wait_ge(exp_done, t * H + h + 3)
                    for n in range(NT):
                        ins = nc.tensor.transpose(ps_t[h % 2][:, n * P:(n + 1) * P],
                                                  e[h % 4][:, n * P:(n + 1) * P].bitcast(BF16), c.ident_bf[:])
                    ins.then_inc(t_done, 1)

                def weigh(t, h):
                    pe.wait_ge(out_act if h % 2 else out_dve, t * (H // 2) + (h // 2 + 1))
                    if h == 0:
                        pe.wait_ge(at_done, t)
                    for n in range(NT):
                        ins = nc.tensor.matmul(ps_o[:, h, :], pT[h % 2][:, n * P:(n + 1) * P],
                                               a.v_int[:, n, h * HD:(h + 1) * HD], start=(n == 0), stop=(n == NT - 1))
                    if h == H - 1:
                        ins.then_inc(pv_done, 1)

                def turn_output(t):
                    pe.wait_ge(at_done, t + 1)
                    pe.wait_ge(a_lo, t)
                    for ch in range(NC):
                        ins = nc.tensor.transpose(ps_a[:, ch, :], at[:, 8 * ch:8 * ch + 8, :].rearrange("p h d -> p (h d)"),
                                                  c.ident[:])
                    ins.then_inc(a_turned, 1)

                def lagging(t, s, lag, work):
                    if s >= lag:
                        work(t, s - lag)
                    elif not (isinstance(t, int) and t == 0):
                        work(t - 1, H + s - lag)

                def body(t, first):
                    for h in range(H):
                        if h % (H // 2) == 0:
                            pe.wait_ge(q_ready, t * 2 + (h // (H // 2) + 1))
                        scores(t, h)
                        lagging(t, h, LAG_T, turn)
                        lagging(t, h, LAG_V, weigh)
                        if h == 5 and not first:
                            turn_output(t - 1)

                tiles(pe, body)
                for s in range(H, H + LAG_V):
                    if s - LAG_T < H:
                        turn(NT - 1, s - LAG_T)
                    weigh(NT - 1, s - LAG_V)
                turn_output(NT - 1)

            @block.vector
            def _(dve):
                def invert(t):
                    dve.wait_ge(exp_done, t * H + (H + 2))
                    nc.vector.reciprocal(inv[:], total[:, t, :]).then_inc(inv_done, 1)

                def finish(t):
                    dve.wait_ge(inv_done, t + 1)
                    dve.wait_ge(pv_done, t + 1)
                    nc.vector.tensor_tensor(at[:], ps_o[:], inv[:].unsqueeze(2).to_broadcast([P, H, HD]),
                                            ALU.mult).then_inc(at_done, 1)

                def split_lo(t):
                    dve.wait_ge(a_hi, t + 1)
                    for ch in range(NC):
                        ins = nc.vector.scalar_tensor_tensor(out=a.aT[1][:, ch, tokens(t)], in0=ps_a[:, ch, :],
                                                             scalar=a.sv[:, ch:ch + 1],
                                                             in1=f32(a.aT[0][:, ch, tokens(t)]), op0=ALU.mult,
                                                             op1=ALU.subtract)
                    ins.then_inc(a_lo, 1)

                def take(t, h):
                    dve.wait_ge(t_done, t * H + (h + 1))
                    nc.vector.tensor_copy(pT[h % 2][:], ps_t[h % 2][:].bitcast(I16)).then_inc(out_dve, 1)

                def body(t, first):
                    for h in range(H):
                        if h == 3 and not first:
                            finish(t - 1)
                        dve.wait_ge(s_done, t * H + (h + 1))
                        nc.vector.tensor_reduce(top[:, h % 4:h % 4 + 1], ps_s[h % 2][:], AX.X, ALU.max,
                                                negate=True).then_inc(top_done, 1)
                        dve.wait_ge(top_done, t * H + (h + 1))
                        nc.vector.tensor_scalar(shift[:, h % 4:h % 4 + 1], top[:, h % 4:h % 4 + 1],
                                                a.sq[:, t, h:h + 1], LN255, ALU.mult, ALU.add).then_inc(shift_done, 1)
                        if not (first and h < 2) and h % 2 == 0:
                            if h >= 2:
                                take(t, h - 2)
                            else:
                                take(t - 1, H - 2)
                        if h == 2 and not first:
                            invert(t - 1)
                        if h == 7 and not first:
                            split_lo(t - 1)

                tiles(dve, body)
                take(NT - 1, H - 2)
                invert(NT - 1)
                finish(NT - 1)
                split_lo(NT - 1)

            @block.scalar
            def _(act):
                nc.scalar.activation(dummy[:], c.ones[:, 0:1], ACT.Exp).then_inc(exp_done, 2)

                def take(t, h):
                    act.wait_ge(t_done, t * H + (h + 1))
                    nc.scalar.activation(pT[h % 2][:], ps_t[h % 2][:].bitcast(I16), ACT.Copy).then_inc(out_act, 1)

                def split_hi(t):
                    act.wait_ge(a_turned, t + 1)
                    for ch in range(NC):
                        ins = nc.scalar.activation(a.aT[0][:, ch, tokens(t)], ps_a[:, ch, :], ACT.Copy,
                                                   scale=a.sv[:, ch:ch + 1])
                    ins.then_inc(a_hi, 1)

                def body(t, first):
                    for h in range(H):
                        if h % 2 == 1:
                            if h >= 2:
                                take(t, h - 2)
                            elif not first:
                                take(t - 1, H - 1)
                        act.wait_ge(shift_done, t * H + (h + 1))
                        nc.scalar.activation(e[h % 4][:], ps_s[h % 2][:], ACT.Exp, bias=shift[:, h % 4:h % 4 + 1],
                                             scale=a.sq[:, t, h:h + 1],
                                             accum_out=total[:, t, h:h + 1]).then_inc(exp_done, 1)
                        if h == 6 and not first:
                            split_hi(t - 1)

                tiles(act, body)
                take(NT - 1, H - 1)
                split_hi(NT - 1)


def project_out(c, a):
    nc = c.nc
    with ExitStack() as ctx:
        bank = [c.ps(f"qa_out{k}", [P, HALF], ctx=ctx) for k in range(4)]
        done, out = c.sem("qa_out_done"), c.sem("qa_out_out")
        with nc.Block() as block:

            @block.tensor
            def _(pe):
                for j in range(4):
                    out_ch, half = j // 2, j % 2
                    for n, (x, y) in enumerate(PASSES):
                        for ch in range(NC):
                            ins = nc.tensor.matmul(bank[j][:], a.wp[x][:, ch, out_ch * P:(out_ch + 1) * P],
                                                   a.aT[y][:, ch, half * HALF:(half + 1) * HALF],
                                                   start=(n + ch == 0), stop=(n == 2 and ch == NC - 1))
                    ins.then_inc(done, 1)

            @block.scalar
            def _(act):
                for j in range(4):
                    out_ch, half = j // 2, j % 2
                    act.wait_ge(done, j + 1)
                    nc.scalar.activation(c.out_t[:, out_ch, half * HALF:(half + 1) * HALF], bank[j][:],
                                         ACT.Identity, bias=c.vecs[:, 6 + out_ch:7 + out_ch]).then_inc(out, 1)


L0_CHUNKS = (18 * 176 + P - 1) // P
L1_CHUNKS = 32 * 96 // P


def threshold_block(c):
    row_statistics(c, "tb_norm", c.x)
    norm_to_feature_major(c, "tb_turn", c.x, c.rstd, c.shift)
    route(c, "tb_route", 32, 8, threshold=0.8)
    experts(c, "tb_moe", L1_CHUNKS)
    add_feature_major(c, "tb_out", c.out_t, c.x)


def build(nc, dram, out):
    with ExitStack() as ctx:
        c = Core(nc, ctx, dram)
        c.x = c.sb("x_res", [P, NT, D])
        c.ident = c.sb("ident_sb", [P, P])
        c.ident_bf = c.sb("ident_bf", [P, P], BF16)
        c.ones = c.sb("ones", [P, P])
        c.vecs = c.sb("vecs_sb", [P, 16])
        c.bn = c.sb("bn", [P, NT, 6])
        c.mean_var = c.sb("mean_var", [P, NT, 2])
        c.stat = c.sb("stat", [P, 4, NT])
        c.rstd = c.sb("rstd", [P, NT])
        c.shift = c.sb("shift", [P, NT])
        c.rms = c.sb("rms", [P, NT])
        c.out_t = c.sb("out_t", [P, NC, T])
        c.fT = [c.sb(f"fT{x}", [P, NC, T], F32R) for x in range(2)]
        c.hid = c.sb("hid", [P, NT, D])
        c.route_t = c.sb("route_t", [2 * ROWS, T], F32R)
        c.scale2 = c.sb("scale2", [P, NT])
        c.shift2 = c.sb("shift2", [P, NT])
        load_constants(c)
        head_attention(c)
        causal_block(c)
        routed_block(c)
        quantised_attention(c)
        threshold_block(c)
        store(c, out)


def store(c, out):
    nc = c.nc
    stored = c.sem("stored")
    with nc.Block() as block:

        @block.sync
        def _(sp):
            sp.dma_start(out, c.x[:]).then_inc(stored, 16)
            sp.wait_ge(stored, 16)



def chunks(gate, up, down, sizes, n_chunks):
    rows = n_chunks * P
    pad = lambda m: np.concatenate([m, np.zeros((rows - len(m), D), np.float32)])
    turned = lambda m: pad(m).reshape(n_chunks, P, NC, P).transpose(0, 3, 2, 1).reshape(n_chunks, P, NC * P)
    of_row = np.repeat(np.arange(len(sizes)), sizes)
    select = np.zeros((P, rows), np.float32)
    for part in range(2):
        select[ROWS * part + of_row, np.arange(len(of_row))] = 1.0
    select = select.reshape(P, n_chunks, P).transpose(1, 0, 2)
    return np.concatenate([turned(gate), turned(up), pad(down).reshape(n_chunks, P, D), select], axis=2)


def arrays_of(inputs):
    a = {k: np.asarray(v) for k, v in inputs.items()}
    out = {}
    out["x"] = a["x"].reshape(NT, P, D).transpose(1, 0, 2)
    ctx_t = a["ctx_2048"].reshape(T, D)
    out["ctx_tiles"] = ctx_t.reshape(NT, P, NC, P).transpose(0, 3, 2, 1)
    out["ident"] = np.eye(P, dtype=np.float32)
    feat = lambda m: m.reshape(NC, P, -1).transpose(1, 0, 2)
    out["ha_w"] = feat(np.concatenate([a["L0_xattn_Wq"].T, a["L0_xattn_Wk"].T, a["L0_xattn_Wv"].T,
                                       a["L0_xattn_Wo"].T], axis=1))
    out["ha_bias"] = np.concatenate([a["L0_xattn_bq"], a["L0_xattn_bk"], a["L0_xattn_bv"], a["L0_xattn_bo"]])[None]
    cols = np.concatenate([a["L0_ffn_ln1_w"].reshape(NC, P), a["L0_ffn_ln2_w"].reshape(NC, P)])
    out["vecs"] = np.concatenate([cols.T, a["L1_xattn_bkv"][D:].reshape(NC, P).T, a["L1_xattn_bp"].reshape(NC, P).T,
                                  np.zeros((P, 8), np.float32)], axis=1)
    out["ctx_t"] = feat(ctx_t.T)
    out["qa_w"] = feat(np.concatenate([a["L1_xattn_Wq"], a["L1_xattn_Wkv"], a["L1_xattn_Wp"]], axis=1))
    out["qa_bias"] = np.concatenate([a["L1_xattn_bq"], a["L1_xattn_bkv"][:D]])[None]
    head_rows = lambda m, step: m.reshape(NH, step, D)[:, :DH].reshape(PAIRS, 2 * DH, NC, P)
    kv = a["L0_ffn_kv_w"]
    qkv = np.stack([head_rows(a["L0_ffn_q_w"], QHD), head_rows(kv[:NH * DH], DH),
                    head_rows(kv[NH * DH:2 * NH * DH], DH)])
    out["ca_w"] = qkv.transpose(1, 4, 0, 3, 2)
    out["ca_wo"] = a["L0_ffn_o_w"].T.reshape(PAIRS, 2, DH, D).transpose(0, 2, 1, 3)
    out["mask"] = np.triu(np.full((P, P), -1e9, np.float32), 1)
    w1, w2, sh = a["L0_ffn_w1"], a["L0_ffn_w2"], a["L0_ffn_sh_gu_w"]
    out["rb_route_gate"] = feat(a["L0_ffn_gate_w"].T)
    out["rb_moe_w"] = chunks(np.concatenate([w1[:, :176].reshape(-1, D), sh[:352]]),
                             np.concatenate([w1[:, 176:].reshape(-1, D), sh[352:]]),
                             np.concatenate([w2.transpose(0, 2, 1).reshape(-1, D), a["L0_ffn_sh_down_w"].T]),
                             [176] * 16 + [352], L0_CHUNKS)
    gu, dn = a["L1_ffn_gate_up_proj"], a["L1_ffn_down_proj"]
    out["tb_route_gate"] = feat(a["L1_ffn_gate_weight"].T)
    out["tb_moe_w"] = chunks(gu[:, :96].reshape(-1, D), gu[:, 96:].reshape(-1, D),
                             dn.transpose(0, 2, 1).reshape(-1, D), [96] * 32, L1_CHUNKS)
    return {k: np.ascontiguousarray(v) for k, v in out.items()}


def kernel(**inputs):
    import concourse.bacc as bacc
    from concourse.bass_utils import run_bass_kernel_spmd

    nc = bacc.Bacc("TRN2", target_bir_lowering=False, num_devices=1)
    arrays = arrays_of(inputs)
    dram = {n: nc.dram_tensor("in_" + n, v.shape, mybir.dt.from_np(v.dtype), kind="ExternalInput").ap()
            for n, v in arrays.items()}
    out = nc.dram_tensor("out", (P, NT, D), F32, kind="ExternalOutput").ap()
    build(nc, dram, out)
    r = run_bass_kernel_spmd(nc, [{"in_" + n: v for n, v in arrays.items()}], core_ids=[0])
    y = r.results[0]["out"]
    return np.ascontiguousarray(y.transpose(1, 0, 2)).reshape(B, S, D)
```

```python
from contextlib import ExitStack

import numpy as np
import concourse.bass as bass
from concourse import mybir
from concourse.alu_op_type import AluOpType as ALU

F32 = mybir.dt.float32
F32R = mybir.dt.float32r
BF16 = mybir.dt.bfloat16
I16 = mybir.dt.int16
ACT = mybir.ActivationFunctionType
AX = mybir.AxisListType

P = 128
B, S, D = 4, 256, 256
T = B * S
NT = T // P
NC = D // P
H, HD = 16, 16
HALF = 512
NHALF = T // HALF


class Counter:

    def __init__(self, sem):
        self.engine, self.sem, self.n = None, sem, 0

    def on(self, engine):
        self.engine = engine
        return self

    def after(self, instruction):
        self.n += 1
        instruction.then_inc(self.sem, 1)
        self.engine.wait_ge(self.sem, self.n)


class Core:

    def __init__(self, nc, ctx, dram):
        self.nc, self.ctx, self.dram = nc, ctx, dram
        self.stages = {}
        self.steps = Counter(self.sem("vector_steps"))
        self.root_asked, self.root_done, self.roots = self.sem("root_asked"), self.sem("root_done"), 0

    def sb(self, name, shape, dtype=F32, ctx=None):
        return (ctx or self.ctx).enter_context(self.nc.sbuf_tensor(name, shape, dtype))

    def ps(self, name, shape, dtype=F32, ctx=None):
        return (ctx or self.ctx).enter_context(self.nc.psum_tensor(name, shape, dtype))

    def sem(self, name):
        return self.ctx.enter_context(self.nc.semaphore(name))

    def shared_sems(self, stage, names):
        if stage not in self.stages:
            self.stages[stage] = ([self.sem(f"{stage}_{n}") for n in names], 0)
        sems, runs = self.stages[stage]
        self.stages[stage] = (sems, runs + 1)
        return sems, runs

    def column(self, tensor, t):
        return tensor[:, t:t + 1] if isinstance(t, int) else tensor[:, bass.ds(t, 1)]


def f32(ap):
    return ap.bitcast(F32)


def load_constants(c, load_weights):
    nc = c.nc
    loaded = c.sem("const_loaded")
    prepared = c.sem("const_prepared")
    with nc.Block() as block:

        @block.sync
        def _(sp):
            sp.dma_start(c.x[:], c.dram["x"]).then_inc(loaded, 16)
            sp.dma_start(c.ident[:], c.dram["ident"]).then_inc(loaded, 16)
            sp.dma_start(c.vecs[:], c.dram["vecs"]).then_inc(loaded, 16)
            load_weights(sp)
            sp.wait_ge(loaded, 48)

        @block.vector
        def _(dve):
            dve.wait_ge(loaded, 48)
            nc.vector.tensor_copy(c.ident_bf[:], c.ident[:]).then_inc(prepared, 1)
            nc.vector.memset(c.ones[:], 1.0).then_inc(prepared, 1)
            dve.wait_ge(prepared, 2)


def row_statistics(c, src, eps=1e-5, second_eps=None, meanwhile=None, products=None, begun=False):
    nc = c.nc
    before = c.roots

    with nc.Block() as block:

        if meanwhile:
            block.sync(meanwhile)
        if products:
            block.tensor(products)

        @block.vector
        def _(dve):
            step = c.steps.on(dve)
            if not begun:
                for t in range(NT):
                    ins = nc.vector.bn_stats(c.bn[:, t, :], src[:, t, :])
                step.after(ins)
            for t in range(NT):
                ins = nc.vector.bn_aggr(c.mean_var[:, t, :], c.bn[:, t, :])
            step.after(ins)
            step.after(nc.vector.tensor_scalar(c.stat[:, 0, :], c.mean_var[:, :, 1], eps, None, ALU.add))
            inverse_root(c, dve, step, c.stat[:, 0, :], c.rstd[:])
            step.after(nc.vector.scalar_tensor_tensor(out=c.shift[:], in0=c.mean_var[:, :, 0], scalar=-1.0,
                                                      in1=c.rstd[:], op0=ALU.mult, op1=ALU.mult))
            if second_eps is not None:
                step.after(nc.vector.tensor_tensor(c.stat[:, 0, :], c.mean_var[:, :, 1], c.rstd[:], ALU.mult))
                step.after(nc.vector.tensor_tensor(c.stat[:, 0, :], c.stat[:, 0, :], c.rstd[:], ALU.mult))
                step.after(nc.vector.tensor_scalar(c.stat[:, 0, :], c.stat[:, 0, :], second_eps, None, ALU.add))
                inverse_root(c, dve, step, c.stat[:, 0, :], c.rms[:])
                nc.vector.tensor_tensor(c.scale2[:], c.rstd[:], c.rms[:], ALU.mult)
                step.after(nc.vector.tensor_tensor(c.shift2[:], c.shift[:], c.rms[:], ALU.mult))

        @block.scalar
        def _(act):
            for n in range(1 if second_eps is None else 2):
                act.wait_ge(c.root_asked, before + n + 1)
                nc.scalar.activation(c.stat[:, 1, :], c.stat[:, 0, :], ACT.Sqrt).then_inc(c.root_done, 1)


def inverse_root(c, dve, step, value, out):
    nc = c.nc
    c.roots += 1
    nc.vector.tensor_copy(c.stat[:, 2, :], value).then_inc(c.root_asked, 1)
    dve.wait_ge(c.root_asked, c.roots)
    dve.wait_ge(c.root_done, c.roots)
    r, u = c.stat[:, 1, :], c.stat[:, 3, :]
    step.after(nc.vector.reciprocal(r, r))
    step.after(nc.vector.tensor_tensor(u, r, r, ALU.mult))
    step.after(nc.vector.tensor_tensor(u, u, value, ALU.mult))
    step.after(nc.vector.tensor_scalar(u, u, -0.5, 1.5, ALU.mult, ALU.add))
    step.after(nc.vector.tensor_tensor(out, r, u, ALU.mult))



def pool_heads(product, t):
    if isinstance(t, int):
        return {("qk", 0): 5, ("qk", 1): 8, ("pv", NT - 1): 5}.get((product, t), 11)
    return 11


def head_attention(c):
    nc = c.nc
    with ExitStack() as ctx:
        w = c.sb("ha_w", [P, NC, 4 * D], ctx=ctx)
        bias = c.sb("ha_bias", [1, 4 * D], ctx=ctx)
        w1 = c.sb("ha_w1", [P, NC, 2 * D], ctx=ctx)
        bias_k1 = c.sb("ha_bias_k1", [1, D], ctx=ctx)
        xn = [c.sb(f"ha_xn{k}", [P, D], ctx=ctx) for k in range(2)]
        xT = [c.sb(f"ha_xT{k}", [P, NC, P], ctx=ctx) for k in range(2)]
        cT = [c.sb(f"ha_cT{k}", [P, NC, P], ctx=ctx) for k in range(2)]
        cT1 = [c.sb(f"ha_cT1{k}", [P, NC, P], ctx=ctx) for k in range(2)]
        q = [c.sb(f"ha_q{k}", [P, H, HD], ctx=ctx) for k in range(2)]
        kk = [c.sb(f"ha_k{k}", [P, H, HD], ctx=ctx) for k in range(2)]
        vT = [c.sb(f"ha_v{k}", [P, HD, H], ctx=ctx) for k in range(2)]
        ex = [c.sb(f"ha_ex{k}", [P, H, H], ctx=ctx) for k in range(2)]
        at = [c.sb(f"ha_at{k}", [P, H, HD], ctx=ctx) for k in range(2)]
        qk_prod = c.sb("ha_qk_prod", [P, H, H * HD], ctx=ctx)
        pv_prod = c.sb("ha_pv_prod", [P, H, HD * H], ctx=ctx)
        sc = c.sb("ha_sc", [P, H, H], ctx=ctx)
        red = c.sb("ha_red", [P, H], ctx=ctx)
        dummy = c.sb("ha_dummy", [P, 1], ctx=ctx)
        aT = c.sb("ha_aT", [P, NC, P], ctx=ctx)
        psT = c.ps("ha_psT", [P, NC * P], ctx=ctx)
        psQ = c.ps("ha_psQ", [P, D], ctx=ctx)
        psKV = c.ps("ha_psKV", [P, 2 * D], ctx=ctx)
        ps1 = c.ps("ha_ps1", [P, 2 * D], ctx=ctx)
        psA = c.ps("ha_psA", [P, NC * P], ctx=ctx)
        psO = c.ps("ha_psO", [P, D], ctx=ctx)
        w_loaded, w1_loaded = c.sem("ha_w_loaded"), c.sem("ha_w1_loaded")
        ctx_loaded = [c.sem(f"ha_ctx_loaded{k}") for k in range(2)]
        ctx1_loaded = [c.sem(f"ha_ctx1_loaded{k}") for k in range(2)]
        normed = c.sem("ha_normed")
        x_turned = c.sem("ha_x_turned")
        xT_ready = c.sem("ha_xT_ready")
        qkv_done = c.sem("ha_qkv_done")
        kv1_done = c.sem("ha_kv1_done")
        kv1_ready = c.sem("ha_kv1_ready")
        qk_ready = c.sem("ha_qk_ready")
        v_ready = c.sem("ha_v_ready")
        qk_pool = c.sem("ha_qk_pool")
        scored = c.sem("ha_scored")
        sub_done = c.sem("ha_sub_done")
        exp_done = c.sem("ha_exp_done")
        prob_ready = c.sem("ha_prob_ready")
        pv_dve = c.sem("ha_pv_dve")
        pv_pool = c.sem("ha_pv_pool")
        at_ready = c.sem("ha_at_ready")
        at_turned = c.sem("ha_at_turned")
        aT_ready = c.sem("ha_aT_ready")
        out_done = c.sem("ha_out_done")
        own = c.sem("ha_own")
        added = c.sem("ha_added")
        OWN = 4
        AHEAD = 3

        def load_weights(sp):
            sp.dma_start(w[:], c.dram["ha_w"]).then_inc(w_loaded, 16)
            sp.dma_start(bias[:], c.dram["ha_bias"]).then_inc(w_loaded, 16)
            for k in range(2):
                sp.dma_start(cT[k][:], c.dram["ctx_tiles"][k]).then_inc(ctx_loaded[k], 16)
            sp.dma_start(w1[:], c.dram["qa_wkv"]).then_inc(w1_loaded, 16)
            sp.dma_start(bias_k1[:], c.dram["qa_bias_k"]).then_inc(w1_loaded, 16)


        def turns(engine, body):
            body(0, 0)
            with engine.Fori(0, (NT - 1 - AHEAD) // 2) as i:
                for j in range(2):
                    body(i * 2 + (1 + j), (1 + j) % 2)
            for t in range(NT - AHEAD, NT):
                body(t, t % 2)

        def tokens(t):
            return slice(t * P, (t + 1) * P) if isinstance(t, int) else bass.ds(t * P, P)

        def exists(t, ahead):
            return not isinstance(t, int) or t + ahead < NT

        def wait(engine, sem, count):
            if not (isinstance(count, int) and count <= 0):
                engine.wait_ge(sem, count)

        def project_kv(pe, t, k):
            pe.wait_ge(ctx_loaded[k], loads_of_slot(t, k))
            wait(pe, v_ready, t)
            nc.tensor.matmul(psKV[:], c.ones[0:1, 0:P], bias[:, D:3 * D], start=True, stop=False)
            for n in range(NC):
                nc.tensor.matmul(psKV[:], cT[k][:, n, :], w[:, n, D:3 * D], start=False, stop=(n == NC - 1))

        def first_projection(pe):
            pe.wait_ge(w_loaded, 32)
            project_kv(pe, 0, 0)

        load_constants(c, load_weights)
        row_statistics(c, c.x, products=first_projection)

        with nc.Block() as block:

            @block.sync
            def _(sp):
                def load(t, k):
                    if not (isinstance(t, int) and t < 2):
                        sp.wait_ge(qkv_done, t - 1)
                        sp.dma_start(cT[k][:], c.dram["ctx_tiles"][t]).then_inc(ctx_loaded[k], 16)
                    wait(sp, kv1_done, t - 1)
                    sp.dma_start(cT1[k][:], c.dram["ctx_tiles"][t]).then_inc(ctx1_loaded[k], 16)

                in_pairs(sp, NT, load)

            @block.scalar
            def _(act):
                def norm(t, k):
                    nc.scalar.activation(xn[k][:], c.x[:, t, :], ACT.Identity, scale=c.column(c.rstd, t),
                                         bias=c.column(c.shift, t)).then_inc(normed, 1)

                def take_xT(t, k):
                    act.wait_ge(x_turned, t + 1)
                    nc.scalar.activation(xT[k][:].rearrange("p c t -> p (c t)"), psT[:],
                                         ACT.Copy).then_inc(xT_ready, 1)

                def take_qk(t, k):
                    act.wait_ge(qkv_done, t + 1)
                    nc.scalar.activation(q[k][:].rearrange("p h d -> p (h d)"), psQ[:], ACT.Copy)
                    nc.scalar.activation(kk[k][:].rearrange("p h d -> p (h d)"), psKV[:, 0:D],
                                         ACT.Copy).then_inc(qk_ready, 1)

                def take_v(t, k):
                    wait(act, pv_pool, t - 1)
                    wait(act, pv_dve, t - 1)
                    nc.scalar.activation(vT[k][:].rearrange("p d g -> p g d"),
                                         psKV[:, D:2 * D].rearrange("p (g d) -> p g d", g=H),
                                         ACT.Copy).then_inc(v_ready, 1)

                def take_kv1(t):
                    act.wait_ge(kv1_done, t + 1)
                    nc.scalar.activation(c.kf[:, t, :], ps1[:, 0:D], ACT.Copy)
                    for n in range(NC):
                        ins = nc.scalar.activation(c.vf[:, n, tokens(t)], ps1[:, D + n * P:D + (n + 1) * P],
                                                   ACT.Identity, bias=c.vecs[:, 4 + n:5 + n])
                    ins.then_inc(kv1_ready, 1)

                def exponential(t, k):
                    act.wait_ge(sub_done, t + 1)
                    wait(act, pv_pool, t - 1)
                    nc.scalar.activation(ex[k][:], sc[:], ACT.Exp).then_inc(exp_done, 1)

                def body(t, k):
                    if exists(t, 2):
                        take_qk(t + 2, k)
                    if exists(t, 3):
                        norm(t + 3, 1 - k)
                    if exists(t, 2):
                        take_v(t + 2, k)
                    take_kv1(t)
                    if exists(t, 3):
                        take_xT(t + 3, 1 - k)
                    if exists(t, 1):
                        exponential(t + 1, 1 - k)
                    act.wait_ge(at_turned, t + 1)
                    nc.scalar.activation(aT[:].rearrange("p c t -> p (c t)"), psA[:],
                                         ACT.Copy).then_inc(aT_ready, 1)

                norm(0, 0)
                norm(1, 1)
                take_xT(0, 0)
                norm(2, 0)
                nc.scalar.activation(dummy[:], c.ones[:, 0:1], ACT.Exp)
                take_qk(0, 0)
                take_v(0, 0)
                take_xT(1, 1)
                take_qk(1, 1)
                take_v(1, 1)
                take_xT(2, 0)
                exponential(0, 0)
                turns(act, body)

            @block.tensor
            def _(pe):
                def front(t, k):
                    pe.wait_ge(normed, t + 1)
                    wait(pe, xT_ready, t)
                    for n in range(NC):
                        ins = nc.tensor.transpose(psT[:, n * P:(n + 1) * P], xn[k][:, n * P:(n + 1) * P], c.ident[:])
                    ins.then_inc(x_turned, 1)
                    if not (isinstance(t, int) and t == 0):
                        project_kv(pe, t, k)
                    pe.wait_ge(xT_ready, t + 1)
                    nc.tensor.matmul(psQ[:], c.ones[0:1, 0:P], bias[:, 0:D], start=True, stop=False)
                    for n in range(NC):
                        ins = nc.tensor.matmul(psQ[:], xT[k][:, n, :], w[:, n, 0:D], start=False, stop=(n == NC - 1))
                    ins.then_inc(qkv_done, 1)

                def project_kv1(t, k):
                    if isinstance(t, int) and t == 0:
                        pe.wait_ge(w1_loaded, 32)
                    pe.wait_ge(ctx1_loaded[k], loads_of_slot(t, k))
                    wait(pe, kv1_ready, t)
                    nc.tensor.matmul(ps1[:, 0:D], c.ones[0:1, 0:P], bias_k1[:], start=True, stop=False)
                    for n in range(NC):
                        nc.tensor.matmul(ps1[:, 0:D], cT1[k][:, n, :], w1[:, n, 0:D], start=False, stop=(n == NC - 1))
                    for out in range(NC):
                        for n in range(NC):
                            ins = nc.tensor.matmul(ps1[:, D + out * P:D + (out + 1) * P],
                                                   w1[:, n, D + out * P:D + (out + 1) * P], cT1[k][:, n, :],
                                                   start=(n == 0), stop=(n == NC - 1))
                    ins.then_inc(kv1_done, 1)

                def body(t, k):
                    project_kv1(t, k)
                    if exists(t, 3):
                        front(t + 3, 1 - k)
                    pe.wait_ge(at_ready, t + 1)
                    for n in range(NC):
                        ins = nc.tensor.transpose(psA[:, n * P:(n + 1) * P],
                                                  at[k][:, 8 * n:8 * n + 8, :].rearrange("p h d -> p (h d)"),
                                                  c.ident[:])
                    ins.then_inc(at_turned, 1)
                    wait(pe, added, t)
                    pe.wait_ge(aT_ready, t + 1)
                    nc.tensor.matmul(psO[:], c.ones[0:1, 0:P], bias[:, 3 * D:4 * D], start=True, stop=False)
                    for n in range(NC):
                        ins = nc.tensor.matmul(psO[:], aT[:, n, :], w[:, n, 3 * D:4 * D], start=False,
                                               stop=(n == NC - 1))
                    ins.then_inc(out_done, 1)

                for t in range(AHEAD):
                    front(t, t % 2)
                turns(pe, body)

            def qk_products(engine, h0, h1, k):
                n = h1 - h0
                return engine.tensor_tensor(qk_prod[:, h0:h1, :].rearrange("p h (g d) -> p h g d", d=HD),
                                            q[k][:, h0:h1, :].unsqueeze(2).to_broadcast([P, n, H, HD]),
                                            kk[k][:].unsqueeze(1).to_broadcast([P, n, H, HD]), ALU.mult)

            def pv_products(engine, h0, h1, k):
                n = h1 - h0
                return engine.tensor_tensor(pv_prod[:, h0:h1, :].rearrange("p h (d g) -> p h d g", g=H),
                                            ex[k][:, h0:h1, :].unsqueeze(2).to_broadcast([P, n, HD, H]),
                                            vT[k][:].unsqueeze(1).to_broadcast([P, n, HD, H]), ALU.mult)

            @block.gpsimd
            def _(pool):
                def qk(t, k):
                    pool.wait_ge(qk_ready, t + 1)
                    wait(pool, scored, t)
                    qk_products(nc.gpsimd, 0, pool_heads("qk", t), k).then_inc(qk_pool, 1)

                def body(t, k):
                    pool.wait_ge(prob_ready, t + 1)
                    wait(pool, at_ready, t)
                    pv_products(nc.gpsimd, 0, pool_heads("pv", t), k).then_inc(pv_pool, 1)
                    if exists(t, 2):
                        qk(t + 2, k)

                qk(0, 0)
                qk(1, 1)
                turns(pool, body)

            @block.vector
            def _(dve):
                def residual(t):
                    dve.wait_ge(out_done, t + 1)
                    nc.vector.tensor_tensor(c.x[:, t, :], c.x[:, t, :], psO[:], ALU.add).then_inc(added, 1)

                def products(t, k):
                    dve.wait_ge(qk_ready, t + 1)
                    qk_products(nc.vector, pool_heads("qk", t), H, k).then_inc(own, 1)

                def scores(t, k):
                    dve.wait_ge(own, t * OWN + 1)
                    dve.wait_ge(qk_pool, t + 1)
                    nc.vector.tensor_reduce(sc[:], qk_prod[:].rearrange("p h (g d) -> p h g d", g=H), AX.X,
                                            ALU.add).then_inc(scored, 1)

                def subtract_top(t):
                    dve.wait_ge(scored, t + 1)
                    nc.vector.tensor_reduce(red[:], sc[:], AX.X, ALU.max).then_inc(own, 1)
                    dve.wait_ge(own, t * OWN + 2)
                    nc.vector.tensor_tensor(sc[:], sc[:], red[:].unsqueeze(2).to_broadcast([P, H, H]),
                                            ALU.subtract).then_inc(sub_done, 1)

                def normalise(t, k):
                    dve.wait_ge(exp_done, t + 1)
                    nc.vector.tensor_reduce(red[:], ex[k][:], AX.X, ALU.add).then_inc(own, 1)
                    dve.wait_ge(own, t * OWN + 3)
                    nc.vector.reciprocal(red[:], red[:]).then_inc(own, 1)
                    dve.wait_ge(own, t * OWN + 4)
                    nc.vector.tensor_tensor(ex[k][:], ex[k][:], red[:].unsqueeze(2).to_broadcast([P, H, H]),
                                            ALU.mult).then_inc(prob_ready, 1)

                def body(t, k):
                    if exists(t, 1):
                        products(t + 1, 1 - k)
                    dve.wait_ge(v_ready, t + 1)
                    dve.wait_ge(prob_ready, t + 1)
                    pv_products(nc.vector, pool_heads("pv", t), H, k).then_inc(pv_dve, 1)
                    if exists(t, 1):
                        scores(t + 1, 1 - k)
                    if not (isinstance(t, int) and t == 0):
                        residual(t - 1)
                    if exists(t, 1):
                        subtract_top(t + 1)
                    dve.wait_ge(pv_dve, t + 1)
                    dve.wait_ge(pv_pool, t + 1)
                    nc.vector.tensor_reduce(at[k][:], pv_prod[:].rearrange("p h (d g) -> p h d g", d=HD), AX.X,
                                            ALU.add).then_inc(at_ready, 1)
                    if exists(t, 1):
                        normalise(t + 1, 1 - k)

                products(0, 0)
                scores(0, 0)
                subtract_top(0)
                normalise(0, 0)
                turns(dve, body)
                residual(NT - 1)



def causal_block(c):
    nc = c.nc
    tile_step = c.sem("cb_tile_step")

    def keep_normed(pool, t):
        nc.gpsimd.tensor_scalar(c.hid[:, t, :], c.x[:, t, :], c.column(c.rstd, t), c.column(c.shift, t),
                                ALU.mult, ALU.add).then_inc(tile_step, 1)

    with ExitStack() as ctx:
        weights = CausalWeights(c, ctx)
        row_statistics(c, c.x, second_eps=1e-6, meanwhile=weights.load_first)
        norm_to_feature_major(c, "cb_turn", c.x, c.scale2, c.shift2, gain=0, tile_work=keep_normed)
        causal_attention(c, weights)
    add_feature_major(c, "cb_out", c.out_t, c.hid)


PASSES = ((0, 0), (0, 1), (1, 0))


def in_pairs(engine, n, body, tail=0, skip=0):
    straight = tail + (n - tail) % 2
    for t in range(skip, 2):
        body(t, t)
    with engine.Fori(0, (n - 2 - straight) // 2) as i:
        for j in range(2):
            body(i * 2 + (2 + j), j)
    for t in range(n - straight, n):
        body(t, t % 2)


def loads_of_slot(t, k):
    return ((t - k) // 2 + 1) * 16 if isinstance(t, int) else (t - k) * 8 + 16


def norm_to_feature_major(c, name, src, scale, shift, gain=None, tile_work=None):
    nc = c.nc
    with ExitStack() as ctx:
        z = c.sb(name + "_z", [P, NT, D], ctx=ctx)
        groups = [(half, n) for half in range(NHALF) for n in range(NC)]
        per_half = NT // NHALF
        ps = [c.ps(f"{name}_ps{k}", [P, HALF], ctx=ctx) for k in range(len(groups))]
        (normed_act, normed_dve, turned, hi_done, lo_done), runs = c.shared_sems(
            "norm", ("normed_act", "normed_dve", "turned", "hi", "lo"))
        start, half_tiles = runs * len(groups), runs * (NT // 2)

        def part(x, half, n):
            return c.fT[x][:, n, half * HALF:(half + 1) * HALF]

        with nc.Block() as block:

            @block.scalar
            def _(act):
                for t in range(0, NT, 2):
                    nc.scalar.activation(z[:, t, :], src[:, t, :], ACT.Identity, scale=scale[:, t:t + 1],
                                         bias=0.0 if shift is None else shift[:, t:t + 1]).then_inc(normed_act, 1)
                for g, (half, n) in enumerate(groups):
                    act.wait_ge(turned, start + g + 1)
                    nc.scalar.activation(part(0, half, n), ps[g][:], ACT.Copy,
                                         scale=1.0 if gain is None else c.vecs[:, gain + n:gain + n + 1]
                                         ).then_inc(hi_done, 1)

            @block.tensor
            def _(pe):
                for g, (half, n) in enumerate(groups):
                    if n == 0:
                        pe.wait_ge(normed_act, half_tiles + (half + 1) * per_half // 2)
                        pe.wait_ge(normed_dve, half_tiles + (half + 1) * per_half // 2)
                    for i in range(per_half):
                        ins = nc.tensor.transpose(ps[g][:, i * P:(i + 1) * P],
                                                  z[:, half * per_half + i, n * P:(n + 1) * P], c.ident[:])
                    ins.then_inc(turned, 1)

            @block.vector
            def _(dve):
                for t in range(1, NT, 2):
                    nc.vector.tensor_scalar(z[:, t, :], src[:, t, :], scale[:, t:t + 1],
                                            0.0 if shift is None else shift[:, t:t + 1],
                                            ALU.mult, ALU.add).then_inc(normed_dve, 1)
                for g, (half, n) in enumerate(groups):
                    dve.wait_ge(hi_done, start + g + 1)
                    hi, lo = f32(part(0, half, n)), part(1, half, n)
                    if gain is None:
                        ins = nc.vector.tensor_tensor(lo, ps[g][:], hi, ALU.subtract)
                    else:
                        ins = nc.vector.scalar_tensor_tensor(out=lo, in0=ps[g][:],
                                                             scalar=c.vecs[:, gain + n:gain + n + 1], in1=hi,
                                                             op0=ALU.mult, op1=ALU.subtract)
                    ins.then_inc(lo_done, 1)

            if tile_work:

                @block.gpsimd
                def _(pool):
                    for t in range(NT):
                        tile_work(pool, t)


def add_feature_major(c, name, acc, dst, out=None, statistics=False):
    nc = c.nc
    with ExitStack() as ctx:
        ps = [c.ps(f"{name}_ps{k}", [P, D], ctx=ctx) for k in range(NT)]
        (turned, added), runs = c.shared_sems("add", ("turned", "added"))
        start = runs * NT
        stored = c.sem("stored") if out is not None else None
        with nc.Block() as block:

            @block.tensor
            def _(pe):
                for t in range(NT):
                    for n in range(NC):
                        ins = nc.tensor.transpose(ps[t][:, n * P:(n + 1) * P], acc[:, n, t * P:(t + 1) * P],
                                                  c.ident[:])
                    ins.then_inc(turned, 1)

            if out is not None:

                @block.sync
                def _(sp):
                    step = NT // 4
                    for t in range(0, NT, step):
                        sp.wait_ge(added, start + t + step)
                        sp.dma_start(out[:, t:t + step, :], dst[:, t:t + step, :]).then_inc(stored, 16)
                    sp.wait_ge(stored, 4 * 16)

            @block.vector
            def _(dve):
                def bn_stats(t):
                    dve.wait_ge(added, start + t + 1)
                    nc.vector.bn_stats(c.bn[:, t, :], dst[:, t, :])

                for t in range(NT):
                    dve.wait_ge(turned, start + t + 1)
                    nc.vector.tensor_tensor(dst[:, t, :], dst[:, t, :], ps[t][:], ALU.add).then_inc(added, 1)
                    if statistics and t > 0:
                        bn_stats(t - 1)
                if statistics:
                    bn_stats(NT - 1)



NH, DH, QHD = 16, 128, 192
PAIRS = NH // 2
QSCALE = float(QHD) ** -0.5


SPLITS = {2: (0,), 3: (1, 2)}
WO_SPLIT = 7


class CausalWeights:

    def __init__(self, c, ctx):
        self.c = c
        self.raw = c.sb("ca_raw", [P, 3, NC, 2 * DH], ctx=ctx)
        self.raw_o = c.sb("ca_raw_o", [DH, 2, D], ctx=ctx)
        self.mask_raw = c.sb("ca_mask_raw", [P, P], ctx=ctx)
        self.mask_loaded = c.sem("ca_mask_loaded")
        self.qkv_loaded, self.wo_loaded = c.sem("ca_qkv_loaded"), c.sem("ca_wo_loaded")

    def load_qkv(self, sp, p):
        sp.dma_start(self.raw[:], self.c.dram["ca_w"][p]).then_inc(self.qkv_loaded, 16)

    def load_wo(self, sp, p):
        sp.dma_start(self.raw_o[:], self.c.dram["ca_wo"][p]).then_inc(self.wo_loaded, 16)

    def load_first(self, sp):
        self.load_qkv(sp, 0)
        self.load_wo(sp, 0)
        sp.dma_start(self.mask_raw[:], self.c.dram["mask"]).then_inc(self.mask_loaded, 16)


def causal_attention(c, weights):
    nc = c.nc
    with ExitStack() as ctx:
        raw, raw_o, mask_raw = weights.raw, weights.raw_o, weights.mask_raw
        w = [c.sb(f"ca_w{x}", [P, 3, NC, 2 * DH], F32R, ctx=ctx) for x in range(2)]
        wo = [c.sb(f"ca_wo{x}", [DH, 2, D], F32R, ctx=ctx) for x in range(2)]
        qk = [[c.sb(f"ca_{m}{x}", [DH, 2, T], F32R, ctx=ctx) for x in range(2)] for m in "qk"]
        v = [c.sb(f"ca_v{x}", [P, NT, 2 * DH], F32R, ctx=ctx) for x in range(2)]
        e = [c.sb(f"ca_e{k}", [P, 3 * P], ctx=ctx) for k in range(4)]
        pT = [[c.sb(f"ca_pT{k}{x}", [P, 3 * P], F32R, ctx=ctx) for x in range(2)] for k in range(2)]
        oT = [c.sb(f"ca_oT{x}", [DH, 2, T], F32R, ctx=ctx) for x in range(2)]
        top = c.sb("ca_top", [P, 4, 2], ctx=ctx)
        total = c.sb("ca_total", [P, 4, 2], ctx=ctx)
        inv = c.sb("ca_inv", [P, 4, 2], ctx=ctx)
        dummy = c.sb("ca_dummy", [P, 1], ctx=ctx)
        mask = c.sb("ca_mask", [P, P], BF16, ctx=ctx)
        bank = [c.ps(f"ca_proj{k}", [P, HALF], ctx=ctx) for k in range(4)]
        ps_s = [c.ps(f"ca_s{k}", [P, 3 * P], ctx=ctx) for k in range(2)]
        ps_t = c.ps("ca_t", [P, 3 * P], ctx=ctx)
        ps_o = c.ps("ca_o", [DH, 2, S], ctx=ctx)

        mask_ready = c.sem("ca_mask_ready")
        w_hi, w_lo = c.sem("ca_w_hi"), c.sem("ca_w_lo")
        first_lo = c.sem("ca_first_lo")
        proj_done = c.sem("ca_proj_done")
        proj_hi = c.sem("ca_proj_hi")
        proj_lo = c.sem("ca_proj_lo")
        s_done = c.sem("ca_s_done")
        top_done = c.sem("ca_top_done")
        exp_done = c.sem("ca_exp_done")
        inv_done = c.sem("ca_inv_done")
        p_done = c.sem("ca_p_done")
        t_done = c.sem("ca_t_done")
        pT_hi, pT_lo = c.sem("ca_pT_hi"), c.sem("ca_pT_lo")
        pv_done = c.sem("ca_pv_done")
        oT_hi, oT_lo = c.sem("ca_oT_hi"), c.sem("ca_oT_lo")
        out_done = c.sem("ca_out_done")
        out_added = c.sem("ca_out_added")

        def bank_view(j):
            b = bank[j % 4]
            return b[:] if j < 8 else b[:].rearrange("p (t n) -> p t n", t=2)

        def projected(j, x):
            if j < 8:
                m, h, half = j // 4, j // 2 % 2, j % 2
                return qk[m][x][:, h, half * HALF:(half + 1) * HALF], QSCALE if m == 0 else 1.0
            t = 2 * (j - 8)
            return v[x][:, t:t + 2, :], 1.0

        def pairs(engine, body):
            body(0, True, False)
            with engine.Fori(0, PAIRS - 2) as i:
                body(i + 1, False, False)
            body(PAIRS - 1, False, True)

        def wait(engine, sem, count):
            if not (isinstance(count, int) and count <= 0):
                engine.wait_ge(sem, count)

        with nc.Block() as block:

            @block.sync
            def _(sp):
                sp.wait_ge(first_lo, 3)
                weights.load_qkv(sp, 1)
                with sp.Fori(0, PAIRS - 2) as p:
                    sp.wait_ge(w_lo, p * 4 + 4)
                    weights.load_wo(sp, p + 1)
                    weights.load_qkv(sp, p + 2)
                sp.wait_ge(w_lo, PAIRS * 4 - 4)
                weights.load_wo(sp, PAIRS - 1)

            @block.gpsimd
            def _(pool):
                def split(part, count):
                    pool.wait_ge(w_hi, count)
                    if part == 3:
                        out, a, hi = wo[1][:], raw_o[:], f32(wo[0][:])
                    else:
                        out, a, hi = w[1][:, part], raw[:, part], f32(w[0][:, part])
                    nc.gpsimd.tensor_tensor(out, a, hi, ALU.subtract).then_inc(w_lo, 1)

                nc.gpsimd.memset(c.out_t[:], 0.0).then_inc(out_added, 4)

                def body(p, first, last):
                    for u in range(8):
                        k = u % 4
                        pool.wait_ge(inv_done, p * 8 + (u + 1))
                        nc.gpsimd.tensor_tensor(e[k][:, 0:P], e[k][:, 0:P], inv[:, k, 0:1].to_broadcast([P, P]),
                                                ALU.mult)
                        nc.gpsimd.tensor_tensor(e[k][:, P:], e[k][:, P:], inv[:, k, 1:2].to_broadcast([P, 2 * P]),
                                                ALU.mult).then_inc(p_done, 1)
                        for part in SPLITS.get(u, ()) if not last else ():
                            split(part, p * 4 + (4 + part))
                        if u == WO_SPLIT:
                            split(3, p * 4 + (4 if last else 7))

                pairs(pool, body)

            @block.scalar
            def _(act):
                def split(part, p):
                    if part == 3:
                        act.wait_ge(weights.wo_loaded, p * 16 + 16)
                        wait(act, out_done, p * 4)
                        nc.scalar.activation(wo[0][:], raw_o[:], ACT.Copy).then_inc(w_hi, 1)
                    else:
                        act.wait_ge(weights.qkv_loaded, p * 16 + 16)
                        wait(act, proj_done, p * 12)
                        nc.scalar.activation(w[0][:, part], raw[:, part], ACT.Copy).then_inc(w_hi, 1)

                def evacuate(p, j):
                    act.wait_ge(proj_done, p * 12 + (j + 1))
                    dst, scale = projected(j, 0)
                    nc.scalar.activation(dst, bank_view(j), ACT.Copy, scale=scale).then_inc(proj_hi, 1)

                for part in range(3):
                    split(part, 0)
                nc.scalar.activation(dummy[:], c.ones[:, 0:1], ACT.Exp)
                for j in range(8):
                    evacuate(0, j)

                def body(p, first, last):
                    for s in range(12):
                        if s == 0:
                            evacuate(p, 8)
                            evacuate(p, 9)
                        if s >= 8 and not last:
                            if s > 8:
                                evacuate(p + 1, 2 * (s - 9) + 1)
                            evacuate(p + 1, 2 * (s - 8))
                        if s >= 5 and s % 2 == 1:
                            b = (s - 5) // 2
                            act.wait_ge(pv_done, p * 8 + (2 * b + 2))
                            if b == 0:
                                wait(act, out_done, p * 4)
                            nc.scalar.activation(oT[0][:, :, b * S:(b + 1) * S], ps_o[:], ACT.Copy).then_inc(oT_hi, 1)
                        if 2 <= s < 10:
                            k = s % 2
                            act.wait_ge(t_done, p * 8 + (s - 1))
                            nc.scalar.activation(pT[k][0][:], ps_t[:], ACT.Copy).then_inc(pT_hi, 1)
                        if s < 8:
                            k, e_s = s % 4, ps_s[s % 2]
                            act.wait_ge(top_done, p * 8 + (s + 1))
                            nc.scalar.activation(e[k][:, 0:P], e_s[:, 0:P], ACT.Exp, bias=top[:, k, 0:1],
                                                 accum_out=total[:, k, 0:1])
                            nc.scalar.activation(e[k][:, P:], e_s[:, P:], ACT.Exp, bias=top[:, k, 1:2],
                                                 accum_out=total[:, k, 1:2]).then_inc(exp_done, 1)
                        if s == 1:
                            evacuate(p, 10)
                            evacuate(p, 11)
                        for part in SPLITS.get(s, ()) if not last else ():
                            split(part, p + 1)
                        if s == WO_SPLIT:
                            split(3, p)
                    if not last:
                        evacuate(p + 1, 7)

                pairs(act, body)

            @block.tensor
            def _(pe):
                def project(p, j):
                    if j >= 4:
                        pe.wait_ge(proj_lo, p * 12 + (j - 3))
                    else:
                        wait(pe, out_added, p * 4)
                    b, m = bank[j % 4], j // 4
                    if j < 8:
                        h, half = j // 2 % 2, j % 2
                        for n, (x, y) in enumerate(PASSES):
                            for ch in range(NC):
                                ins = nc.tensor.matmul(b[:], w[x][:, m, ch, h * DH:(h + 1) * DH],
                                                       c.fT[y][:, ch, half * HALF:(half + 1) * HALF],
                                                       start=(n + ch == 0), stop=(n == 2 and ch == NC - 1))
                    else:
                        for i in range(2):
                            t = 2 * (j - 8) + i
                            for n, (x, y) in enumerate(PASSES):
                                for ch in range(NC):
                                    ins = nc.tensor.matmul(b[:, i * 2 * DH:(i + 1) * 2 * DH],
                                                           c.fT[y][:, ch, t * P:(t + 1) * P], w[x][:, 2, ch, :],
                                                           start=(n + ch == 0), stop=(n == 2 and ch == NC - 1))
                    ins.then_inc(proj_done, 1)

                def scores(p, u):
                    b, h, k = u // 2, u % 2, u % 2
                    wait(pe, exp_done, p * 8 + (u - 1))
                    qh, kh = qk
                    nc.tensor.matmul(ps_s[k][:].rearrange("p (n k) -> p n k", n=3)[:, 0::2, :], c.ident_bf[:],
                                     mask[:].unsqueeze(1).to_broadcast([P, 2, P]), start=True, stop=False,
                                     skip_group_check=True)
                    for tile, c0, n_keys in ((0, 0, P), (1, P, 2 * P)):
                        q0 = b * S + tile * P
                        for n, (x, y) in enumerate(PASSES):
                            ins = nc.tensor.matmul(ps_s[k][:, c0:c0 + n_keys], qh[x][:, h, q0:q0 + P],
                                                   kh[y][:, h, b * S:b * S + n_keys], start=False,
                                                   stop=(tile == 1 and n == 2), skip_group_check=True)
                    ins.then_inc(s_done, 1)

                def turn(p, u):
                    k = u % 4
                    pe.wait_ge(p_done, p * 8 + (u + 1))
                    wait(pe, pT_lo, p * 8 + u)
                    for n in range(3):
                        ins = nc.tensor.transpose(ps_t[:, n * P:(n + 1) * P], e[k][:, n * P:(n + 1) * P], c.ident[:])
                    ins.then_inc(t_done, 1)

                def weigh(p, u):
                    b, h, k = u // 2, u % 2, u % 2
                    pe.wait_ge(pT_lo, p * 8 + (u + 1))
                    if h == 0:
                        wait(pe, oT_lo, p * 4 + b)
                    for tile, q0, c0, n_q in ((0, 0, 0, 2 * P), (1, P, 2 * P, P)):
                        for n, (x, y) in enumerate(PASSES):
                            ins = nc.tensor.matmul(ps_o[:, h, q0:q0 + n_q], v[x][:, 2 * b + tile, h * DH:(h + 1) * DH],
                                                   pT[k][y][:, c0:c0 + n_q], start=(tile == 0 and n == 0),
                                                   stop=(tile == 1 and n == 2))
                    ins.then_inc(pv_done, 1)

                def output(j):
                    ch, half = j // 2, j % 2
                    for n, (x, y) in enumerate(PASSES):
                        for h in range(2):
                            ins = nc.tensor.matmul(bank[j][:], wo[x][:, h, ch * P:(ch + 1) * P],
                                                   oT[y][:, h, half * HALF:(half + 1) * HALF],
                                                   start=(n + h == 0), stop=(n == 2 and h == 1))
                    ins.then_inc(out_done, 1)

                for j in range(8):
                    if j % 4 == 0:
                        pe.wait_ge(first_lo, j // 4 + 1)
                    project(0, j)
                pe.wait_ge(first_lo, 3)
                pe.wait_ge(mask_ready, 1)

                def body(p, first, last):
                    for s in range(12):
                        if s == 0:
                            project(p, 8)
                            project(p, 9)
                            pe.wait_ge(proj_lo, p * 12 + 8)
                        if s >= 8 and not last:
                            if s == 8:
                                pe.wait_ge(w_lo, p * 4 + 3)
                            project(p + 1, 2 * (s - 8))
                        if s == 4:
                            pe.wait_ge(proj_lo, p * 12 + 12)
                        if s >= 4:
                            weigh(p, s - 4)
                        if s < 8:
                            scores(p, s)
                        if s == 1:
                            project(p, 10)
                            project(p, 11)
                        if 2 <= s < 10:
                            turn(p, s - 2)
                        if s in (2, 3) and not first:
                            if s == 2:
                                pe.wait_ge(oT_lo, p * 4)
                                pe.wait_ge(w_lo, p * 4)
                            for j in (2 * (s - 2), 2 * (s - 2) + 1):
                                pe.wait_ge(proj_lo, p * 12 + (9 + j))
                                output(j)
                        if s >= 8 and not last:
                            project(p + 1, 2 * (s - 8) + 1)

                pairs(pe, body)
                pe.wait_ge(oT_lo, PAIRS * 4)
                pe.wait_ge(w_lo, PAIRS * 4 - 3)
                pe.wait_ge(out_added, PAIRS * 4)
                for j in range(4):
                    output(j)

            @block.vector
            def _(dve):
                for part in range(3):
                    dve.wait_ge(w_hi, part + 1)
                    nc.vector.tensor_tensor(w[1][:, part], raw[:, part], f32(w[0][:, part]),
                                            ALU.subtract).then_inc(first_lo, 1)
                dve.wait_ge(weights.mask_loaded, 16)
                nc.vector.tensor_copy(mask[:], mask_raw[:]).then_inc(mask_ready, 1)

                def evacuate(p, j):
                    dve.wait_ge(proj_hi, p * 12 + (j + 1))
                    hi, scale = projected(j, 0)
                    lo, _ = projected(j, 1)
                    if scale == 1.0:
                        ins = nc.vector.tensor_tensor(lo, bank_view(j), f32(hi), ALU.subtract)
                    else:
                        ins = nc.vector.scalar_tensor_tensor(out=lo, in0=bank_view(j), scalar=scale, in1=f32(hi),
                                                             op0=ALU.mult, op1=ALU.subtract)
                    ins.then_inc(proj_lo, 1)

                def add(p, j):
                    ch, half = j // 2, j % 2
                    dst = c.out_t[:, ch, half * HALF:(half + 1) * HALF]
                    dve.wait_ge(out_done, p * 4 + (j + 1))
                    dve.wait_ge(out_added, p * 4 + 4)
                    nc.vector.tensor_tensor(dst, dst, bank[j][:], ALU.add).then_inc(out_added, 1)

                for j in range(8):
                    evacuate(0, j)

                def body(p, first, last):
                    for s in range(12):
                        if s == 0:
                            evacuate(p, 8)
                            evacuate(p, 9)
                        if s >= 8 and not last:
                            if s > 8:
                                evacuate(p + 1, 2 * (s - 9) + 1)
                            evacuate(p + 1, 2 * (s - 8))
                        if s >= 5 and s % 2 == 1:
                            b = (s - 5) // 2
                            dve.wait_ge(oT_hi, p * 4 + (b + 1))
                            nc.vector.tensor_tensor(oT[1][:, :, b * S:(b + 1) * S], ps_o[:],
                                                    f32(oT[0][:, :, b * S:(b + 1) * S]),
                                                    ALU.subtract).then_inc(oT_lo, 1)
                        if s < 8:
                            k, e_s = s % 4, ps_s[s % 2]
                            dve.wait_ge(s_done, p * 8 + (s + 1))
                            nc.vector.tensor_reduce(top[:, k, 0:1], e_s[:, 0:P], AX.X, ALU.max, negate=True)
                            nc.vector.tensor_reduce(top[:, k, 1:2], e_s[:, P:], AX.X, ALU.max,
                                                    negate=True).then_inc(top_done, 1)
                        if 2 <= s < 10:
                            k = s % 2
                            dve.wait_ge(pT_hi, p * 8 + (s - 1))
                            nc.vector.tensor_tensor(pT[k][1][:], ps_t[:], f32(pT[k][0][:]),
                                                    ALU.subtract).then_inc(pT_lo, 1)
                        if s < 8:
                            dve.wait_ge(exp_done, p * 8 + (s + 1))
                            nc.vector.reciprocal(inv[:, s % 4, :], total[:, s % 4, :]).then_inc(inv_done, 1)
                        if s == 1:
                            evacuate(p, 10)
                            evacuate(p, 11)
                        if s in (2, 3) and not first:
                            add(p - 1, 2 * (s - 2))
                            add(p - 1, 2 * (s - 2) + 1)
                    if not last:
                        evacuate(p + 1, 7)

                pairs(dve, body)
                for j in range(4):
                    add(PAIRS - 1, j)



ROWS = 32
L0_CHUNKS = (18 * 176 + P - 1) // P
L1_CHUNKS = 32 * 96 // P
WCOLS = 2 * NC * P + D + P


def top_k_mask(c, step, probs, top, mask):
    nc = c.nc
    for t in range(NT):
        ins = nc.vector.match_replace(mask[:, t, :], top[:, t, :], probs[:, t, :], -2.0)
    step.after(ins)
    step.after(nc.vector.tensor_tensor(mask[:], mask[:], probs[:], ALU.not_equal))


def route(c, name, n_experts, top_k, expert_weights, threshold=None, shared=False):
    nc = c.nc
    width = n_experts + 8
    with ExitStack() as ctx:
        gate = expert_weights.gate
        g = [c.sb(f"{name}_g{x}", [P, NC, n_experts], F32R, ctx=ctx) for x in range(2)]
        probs = c.sb(name + "_probs", [P, NT, width], ctx=ctx)
        mask = c.sb(name + "_mask", [P, NT, width], ctx=ctx)
        top = c.sb(name + "_top", [P, NT, 8], ctx=ctx)
        kept = c.sb(name + "_kept", [P, NT, 8], ctx=ctx)
        share = [c.sb(f"{name}_share{k}", [P, NT, 16], ctx=ctx) for k in range(2)]
        dummy = c.sb(name + "_dummy", [P, 1], ctx=ctx)
        red = c.sb(name + "_red", [P, NT], ctx=ctx)
        weights = c.sb(name + "_weights", [P, NT, ROWS], ctx=ctx)
        ps_l = c.ps(name + "_ps_l", [P, NT, n_experts], ctx=ctx)
        by_expert = c.sb(name + "_by_expert", [n_experts, T], ctx=ctx)
        ps_e = [c.ps(f"{name}_ps_e{k}", [n_experts, HALF], ctx=ctx) for k in range(NHALF)]
        ps_w = [c.ps(f"{name}_ps_w{k}", [ROWS, HALF], ctx=ctx) for k in range(NHALF)]
        g_hi, g_lo = c.sem(name + "_g_hi"), c.sem(name + "_g_lo")
        logits, shifted, exped = c.sem(name + "_logits"), c.sem(name + "_shifted"), c.sem(name + "_exped")
        logits_out, logits_turned = c.sem(name + "_logits_out"), c.sem(name + "_logits_turned")
        weighted, turned = c.sem(name + "_weighted"), c.sem(name + "_turned")
        hi_done, lo_done = c.sem(name + "_hi"), c.sem(name + "_lo")
        experts = probs[:, :, 0:n_experts]

        def spread(col, n):
            return col.unsqueeze(2).to_broadcast([P, NT, n])

        with nc.Block() as block:

            @block.gpsimd
            def _(pool):
                expert_weights.split_lo(pool, 0, 0)

            @block.scalar
            def _(act):
                act.wait_ge(expert_weights.gate_loaded, 16)
                nc.scalar.activation(g[0][:], gate[:], ACT.Copy).then_inc(g_hi, 1)
                nc.scalar.activation(dummy[:], c.ones[:, 0:1], ACT.Exp)
                for k in range(NHALF):
                    act.wait_ge(logits, k + 1)
                    nc.scalar.activation(by_expert[:, k * HALF:(k + 1) * HALF], ps_e[k][:],
                                         ACT.Copy).then_inc(logits_out, 1)
                expert_weights.split_hi(act, 0, 0)
                act.wait_ge(shifted, 1)
                nc.scalar.activation(experts, experts, ACT.Exp).then_inc(exped, 1)
                for k in range(NHALF):
                    act.wait_ge(turned, k + 1)
                    nc.scalar.activation(c.route_t[0:ROWS, k * HALF:(k + 1) * HALF], ps_w[k][:],
                                         ACT.Copy).then_inc(hi_done, 1)

            @block.tensor
            def _(pe):
                pe.wait_ge(g_lo, 1)
                for k in range(NHALF):
                    for n, (x, y) in enumerate(PASSES):
                        for ch in range(NC):
                            ins = nc.tensor.matmul(ps_e[k][:], g[x][:, ch, :],
                                                   c.fT[y][:, ch, k * HALF:(k + 1) * HALF],
                                                   start=(n + ch == 0), stop=(n == 2 and ch == NC - 1))
                    ins.then_inc(logits, 1)
                for k in range(NHALF):
                    pe.wait_ge(logits_out, k + 1)
                    for t in range(k * NT // NHALF, (k + 1) * NT // NHALF):
                        ins = nc.tensor.transpose(ps_l[:, t, :], by_expert[:, t * P:(t + 1) * P],
                                                  c.ident[0:n_experts, 0:n_experts])
                ins.then_inc(logits_turned, 1)
                pe.wait_ge(weighted, 1)
                for t in range(NT):
                    k, c0 = t // 4, t % 4 * P
                    ins = nc.tensor.transpose(ps_w[k][:, c0:c0 + P], weights[:, t, :], c.ident[:])
                    if t % 4 == 3:
                        ins.then_inc(turned, 1)

            @block.vector
            def _(dve):
                step = c.steps.on(dve)
                dve.wait_ge(g_hi, 1)
                nc.vector.tensor_tensor(g[1][:], gate[:], f32(g[0][:]), ALU.subtract).then_inc(g_lo, 1)
                step.after(nc.vector.memset(probs[:], -1.0))
                step.after(nc.vector.memset(weights[:], 0.0))
                if shared:
                    step.after(nc.vector.memset(weights[:, :, n_experts:n_experts + 1], 1.0))
                step.after(nc.vector.memset(c.route_t[:].bitcast(F32), 0.0))
                if threshold is not None:
                    for k in range(2):
                        step.after(nc.vector.memset(share[k][:, :, 0:8], 0.0))
                dve.wait_ge(logits_turned, 1)
                step.after(nc.vector.tensor_reduce(red[:], ps_l[:], AX.X, ALU.max))
                nc.vector.tensor_tensor(experts, ps_l[:], spread(red[:], n_experts), ALU.subtract).then_inc(shifted, 1)
                dve.wait_ge(exped, 1)
                step.after(nc.vector.tensor_reduce(red[:], experts, AX.X, ALU.add))
                step.after(nc.vector.reciprocal(red[:], red[:]))
                step.after(nc.vector.tensor_tensor(experts, experts, spread(red[:], n_experts), ALU.mult))
                for t in range(NT):
                    ins = nc.vector.max(out=top[:, t, :], in_=probs[:, t, :])
                step.after(ins)
                if threshold is None:
                    step.after(nc.vector.memset(top[:, :, top_k:8], -1.0))
                    step.after(nc.vector.tensor_reduce(red[:], top[:, :, 0:top_k], AX.X, ALU.add))
                else:
                    step.after(nc.vector.tensor_reduce(red[:], top[:], AX.X, ALU.add))
                    step.after(nc.vector.tensor_scalar(red[:], red[:], 1e-12, None, ALU.max))
                    step.after(nc.vector.reciprocal(red[:], red[:]))
                    step.after(nc.vector.tensor_tensor(share[0][:, :, 8:], top[:], spread(red[:], 8), ALU.mult))
                    for n, places in enumerate((1, 2, 4)):
                        old, new = share[n % 2], share[(n + 1) % 2]
                        step.after(nc.vector.tensor_tensor(new[:, :, 8:], old[:, :, 8:],
                                                           old[:, :, 8 - places:16 - places], ALU.add))
                    step.after(nc.vector.memset(kept[:, :, 0:1], 1.0))
                    step.after(nc.vector.tensor_scalar(kept[:, :, 1:8], share[1][:, :, 8:15], threshold, None,
                                                       ALU.is_lt))
                    step.after(nc.vector.tensor_tensor(top[:], top[:], kept[:], ALU.mult))
                    step.after(nc.vector.tensor_reduce(red[:], top[:], AX.X, ALU.add))
                    step.after(nc.vector.tensor_scalar(kept[:], kept[:], -1.0, None, ALU.add))
                    step.after(nc.vector.tensor_tensor(top[:], top[:], kept[:], ALU.add))
                    step.after(nc.vector.tensor_scalar(red[:], red[:], 1e-12, None, ALU.max))
                top_k_mask(c, step, probs, top, mask)
                step.after(nc.vector.reciprocal(red[:], red[:]))
                step.after(nc.vector.tensor_tensor(experts, experts, mask[:, :, 0:n_experts], ALU.mult))
                nc.vector.tensor_tensor(weights[:, :, 0:n_experts], experts, spread(red[:], n_experts),
                                        ALU.mult).then_inc(weighted, 1)
                for k in range(NHALF):
                    dve.wait_ge(hi_done, k + 1)
                    cols = slice(k * HALF, (k + 1) * HALF)
                    nc.vector.tensor_tensor(c.route_t[ROWS:2 * ROWS, cols], ps_w[k][:],
                                            f32(c.route_t[0:ROWS, cols]), ALU.subtract).then_inc(lo_done, 1)


class ExpertWeights:

    def __init__(self, c, ctx, name, n_experts):
        self.c, self.name = c, name
        self.raw = [c.sb(f"{name}_raw{k}", [P, WCOLS], ctx=ctx) for k in range(2)]
        self.w = [[c.sb(f"{name}_w{k}{x}", [P, WCOLS], F32R, ctx=ctx) for x in range(2)] for k in range(2)]
        self.loaded = [c.sem(f"{name}_loaded{k}") for k in range(2)]
        self.w_hi, self.w_lo = c.sem(name + "_w_hi"), c.sem(name + "_w_lo")
        self.down_done = c.sem(name + "_down_done")
        self.gate = c.sb(name + "_gate", [P, NC, n_experts], ctx=ctx)
        self.gate_loaded = c.sem(name + "_gate_loaded")

    def load_first(self, sp):
        sp.dma_start(self.gate[:], self.c.dram[self.name + "_gate"]).then_inc(self.gate_loaded, 16)
        self.load(sp, 0, 0)
        self.load(sp, 1, 1)

    def load(self, sp, ck, k):
        if not (isinstance(ck, int) and ck < 2):
            sp.wait_ge(self.w_lo, ck - 1)
        sp.dma_start(self.raw[k][:], self.c.dram[self.name + "_w"][ck]).then_inc(self.loaded[k], 16)

    def split_hi(self, act, ck, k):
        act.wait_ge(self.loaded[k], loads_of_slot(ck, k))
        if not (isinstance(ck, int) and ck < 2):
            act.wait_ge(self.down_done, ck * 2 - 2)
        self.c.nc.scalar.activation(self.w[k][0][:], self.raw[k][:], ACT.Copy).then_inc(self.w_hi, 1)

    def split_lo(self, pool, ck, k):
        pool.wait_ge(self.w_hi, ck + 1)
        self.c.nc.gpsimd.tensor_tensor(self.w[k][1][:], self.raw[k][:], f32(self.w[k][0][:]),
                                       ALU.subtract).then_inc(self.w_lo, 1)


def experts(c, name, n_chunks, weights, meanwhile=None, pool_last=None):
    nc = c.nc
    with ExitStack() as ctx:
        w, w_lo, down_done = weights.w, weights.w_lo, weights.down_done
        gated = [c.sb(f"{name}_gated{k}", [P, HALF], ctx=ctx) for k in range(2)]
        routed = [c.sb(f"{name}_routed{k}", [P, HALF], ctx=ctx) for k in range(2)]
        inner = [c.sb(f"{name}_inner{k}", [P, HALF], ctx=ctx) for k in range(2)]
        a = [[c.sb(f"{name}_a{k}{x}", [P, HALF], F32R, ctx=ctx) for x in range(2)] for k in range(2)]
        ps_g = [c.ps(f"{name}_ps_g{k}", [P, HALF], ctx=ctx) for k in range(2)]
        ps_u = c.ps(name + "_ps_u", [P, HALF], ctx=ctx)
        ps_r = c.ps(name + "_ps_r", [P, HALF], ctx=ctx)
        acc = [[c.ps(f"{name}_acc{ch}{h}", [P, HALF], ctx=ctx) for h in range(NHALF)] for ch in range(NC)]
        gate_done = c.sem(name + "_gate_done")
        route_done = c.sem(name + "_route_done")
        up_done = c.sem(name + "_up_done")
        silu_done = c.sem(name + "_silu_done")
        routed_done = c.sem(name + "_routed_done")
        inner_done = c.sem(name + "_inner_done")
        a_hi, a_lo = c.sem(name + "_a_hi"), c.sem(name + "_a_lo")
        taken = c.sem(name + "_taken")

        def gate_up(m, ch):
            c0 = (m * NC + ch) * P
            return slice(c0, c0 + P)

        def down(ch):
            c0 = 2 * NC * P + ch * P
            return slice(c0, c0 + P)

        select = slice(WCOLS - P, WCOLS)
        tail = 1 if meanwhile is None else 3
        zero = lambda x: isinstance(x, int) and x == 0

        with nc.Block() as block:

            @block.sync
            def _(sp):
                in_pairs(sp, n_chunks, lambda ck, k: weights.load(sp, ck, k), skip=2)

            @block.gpsimd
            def _(pool):
                in_pairs(pool, n_chunks, lambda ck, k: weights.split_lo(pool, ck, k), skip=1)
                if pool_last:
                    pool_last(pool)

            @block.scalar
            def _(act):
                def take_hi(n, h):
                    act.wait_ge(inner_done, n + 1)
                    nc.scalar.activation(a[h][0][:], inner[h][:], ACT.Copy).then_inc(a_hi, 1)

                def body(ck, k):
                    for h in range(2):
                        n = ck * 2 + h
                        if not zero(n):
                            take_hi(n - 1, 1 - h)
                        if h == 1 and not (isinstance(ck, int) and ck == n_chunks - 1):
                            weights.split_hi(act, ck + 1, 1 - k)
                        act.wait_ge(gate_done, n + 1)
                        nc.scalar.activation(gated[h][:], ps_g[h][:], ACT.Silu).then_inc(silu_done, 1)
                        if meanwhile is not None and isinstance(n, int):
                            meanwhile.on_scalar(act, n)

                in_pairs(act, n_chunks, body, tail=tail)
                take_hi(2 * n_chunks - 1, 1)
                act.wait_ge(down_done, 2 * n_chunks)
                for ch in range(NC):
                    for h in range(NHALF):
                        nc.scalar.activation(c.out_t[:, ch, h * HALF:(h + 1) * HALF], acc[ch][h][:],
                                             ACT.Copy).then_inc(taken, 1)

            @block.tensor
            def _(pe):
                def down_products(n, h, k):
                    pe.wait_ge(a_lo, n + 1)
                    first = isinstance(n, int) and n < NHALF
                    for ch in range(NC):
                        for i, (x, y) in enumerate(PASSES):
                            ins = nc.tensor.matmul(acc[ch][h][:], w[k][x][:, down(ch)], a[h][y][:],
                                                   start=(first and i == 0), stop=False, skip_group_check=True)
                    ins.then_inc(down_done, 1)

                def body(ck, k):
                    pe.wait_ge(w_lo, ck + 1)
                    for h in range(2):
                        n = ck * 2 + h
                        cols = slice(h * HALF, (h + 1) * HALF)
                        for i, (x, y) in enumerate(PASSES):
                            for ch in range(NC):
                                ins = nc.tensor.matmul(ps_g[h][:], w[k][x][:, gate_up(0, ch)], c.fT[y][:, ch, cols],
                                                       start=(i + ch == 0), stop=(i == 2 and ch == NC - 1))
                        ins.then_inc(gate_done, 1)
                        if not zero(n):
                            pe.wait_ge(routed_done, n)
                        nc.tensor.matmul(ps_r[:], w[k][0][0:2 * ROWS, select], c.route_t[:, cols], start=True,
                                         stop=True).then_inc(route_done, 1)
                        if not zero(n):
                            pe.wait_ge(inner_done, n)
                        for i, (x, y) in enumerate(PASSES):
                            for ch in range(NC):
                                ins = nc.tensor.matmul(ps_u[:], w[k][x][:, gate_up(1, ch)], c.fT[y][:, ch, cols],
                                                       start=(i + ch == 0), stop=(i == 2 and ch == NC - 1))
                        ins.then_inc(up_done, 1)
                        if not zero(n):
                            down_products(n - 1, 1 - h, k if h == 1 else 1 - k)

                in_pairs(pe, n_chunks, body)
                down_products(2 * n_chunks - 1, 1, (n_chunks - 1) % 2)

            @block.vector
            def _(dve):
                def take_lo(n, h):
                    dve.wait_ge(a_hi, n + 1)
                    nc.vector.tensor_tensor(a[h][1][:], inner[h][:], f32(a[h][0][:]), ALU.subtract).then_inc(a_lo, 1)

                def body(ck, k):
                    for h in range(2):
                        n = ck * 2 + h
                        if not zero(n):
                            take_lo(n - 1, 1 - h)
                        dve.wait_ge(silu_done, n + 1)
                        dve.wait_ge(route_done, n + 1)
                        if not zero(n):
                            dve.wait_ge(inner_done, n)
                        nc.vector.tensor_tensor(routed[h][:], ps_r[:], gated[h][:], ALU.mult).then_inc(routed_done, 1)
                        dve.wait_ge(up_done, n + 1)
                        dve.wait_ge(routed_done, n + 1)
                        if not (isinstance(n, int) and n < 2):
                            dve.wait_ge(a_lo, n - 1)
                        nc.vector.tensor_tensor(inner[h][:], ps_u[:], routed[h][:], ALU.mult).then_inc(inner_done, 1)
                        if meanwhile is not None and isinstance(n, int):
                            meanwhile.on_vector(dve, n)

                in_pairs(dve, n_chunks, body, tail=tail)
                take_lo(2 * n_chunks - 1, 1)


def routed_block(c, keys_values):
    nc = c.nc
    before = c.roots

    def add_hid(pool):
        for t in range(NT):
            nc.gpsimd.tensor_tensor(c.x[:, t, :], c.x[:, t, :], c.hid[:, t, :], ALU.add)
        keys_values.on_pool(pool)

    with ExitStack() as ctx:
        weights = ExpertWeights(c, ctx, "rb_moe", 16)
        squared = c.sem("rb_squared")
        sq = c.sb("rb_sq", [P, NT, D], ctx=ctx)
        with nc.Block() as block:

            @block.sync
            def _(sp):
                weights.load_first(sp)
                keys_values.load_weights(sp)

            @block.vector
            def _(dve):
                step = c.steps.on(dve)
                half = slice(NT // 2, NT)
                step.after(nc.vector.tensor_tensor(sq[:, half], c.hid[:, half], c.hid[:, half], ALU.mult))
                step.after(nc.vector.tensor_reduce(c.stat[:, 0, half], sq[:, half], AX.X, ALU.add))
                dve.wait_ge(squared, NT // 2)
                step.after(nc.vector.tensor_scalar(c.stat[:, 0, :], c.stat[:, 0, :], 1.0 / D, 1e-6, ALU.mult, ALU.add))
                inverse_root(c, dve, step, c.stat[:, 0, :], c.rms[:])

            @block.scalar
            def _(act):
                for t in range(NT // 2):
                    nc.scalar.activation(sq[:, t, :], c.hid[:, t, :], ACT.Square,
                                         accum_out=c.stat[:, 0, t:t + 1]).then_inc(squared, 1)
                act.wait_ge(c.root_asked, before + 1)
                nc.scalar.activation(c.stat[:, 1, :], c.stat[:, 0, :], ACT.Sqrt).then_inc(c.root_done, 1)

        norm_to_feature_major(c, "rb_turn", c.hid, c.rms, None, gain=NC)
        route(c, "rb_route", 16, 4, weights, shared=True)
        experts(c, "rb_moe", L0_CHUNKS, weights, meanwhile=keys_values, pool_last=add_hid)
    add_feature_major(c, "rb_out", c.out_t, c.x, statistics=True)



SLOT = 4 * HD
LN255 = float(np.log(255.0))
NPAIR = H // 2
ACT_TAKES = [h for h in range(H) if h % 2 == 1]
DVE_TAKES = [h for h in range(H) if h not in ACT_TAKES]


def spread(col):
    return col.unsqueeze(2).to_broadcast([P, NT * H, HD])


def rows(tensor, part):
    return tensor[:, :, :, part, :].rearrange("p t h d -> p (t h) d")


class KeysValues:

    LATE = 2 * (L0_CHUNKS - 3)

    def __init__(self, c, ctx):
        self.c = c
        self.k_rows = c.sb("kv_k_rows", [P, NT, H, 4, HD], BF16, ctx=ctx)
        self.v_cols = c.sb("kv_v_cols", [P, NC, T], BF16, ctx=ctx)
        self.ints = c.sb("kv_ints", [P, NT * H, HD], I16, ctx=ctx)
        self.k_ints = c.sb("kv_k_ints", [P, NT * H, HD], BF16, ctx=ctx)
        self.v_ints = c.sb("kv_v_ints", [P, NC, T], I16, ctx=ctx)
        self.rest = c.sb("kv_rest", [P, NT * H, HD], ctx=ctx)
        self.sk = c.sb("kv_sk", [P, NT * H], ctx=ctx)
        self.sv = c.sb("kv_sv", [P, NC], ctx=ctx)
        self.inv = c.sb("kv_inv", [P, NT * H], ctx=ctx)
        self.inv_v = c.sb("kv_inv_v", [P, NC], ctx=ctx)
        self.rest_ready = c.sem("kv_rest_ready")
        self.part_done = c.sem("kv_part_done")
        self.inv_v_ready, self.v_rounded = c.sem("kv_inv_v_ready"), c.sem("kv_v_rounded")
        self.w_raw = c.sb("kv_w_raw", [P, NC, 2 * D], ctx=ctx)
        self.wq, self.wp = ([c.sb(f"kv_w{m}{x}", [P, NC, D], F32R, ctx=ctx) for x in range(2)] for m in "qp")
        self.bias_q, self.bias_p = (c.sb("kv_bias_" + m, [P, D], ctx=ctx) for m in "qp")
        self.loaded, self.w_hi = c.sem("kv_loaded"), c.sem("kv_w_hi")

    def load_weights(self, sp):
        sp.dma_start(self.w_raw[:], self.c.dram["qa_w"]).then_inc(self.loaded, 16)
        sp.dma_start(self.bias_q[:], self.c.dram["qa_bias_q"]).then_inc(self.loaded, 16)
        sp.dma_start(self.bias_p[:], self.c.dram["qa_bias_p"]).then_inc(self.loaded, 16)

    def on_pool(self, pool):
        for m, w in enumerate((self.wq, self.wp)):
            pool.wait_ge(self.w_hi, m + 1)
            self.c.nc.gpsimd.tensor_tensor(w[1][:], self.w_raw[:, :, m * D:(m + 1) * D], f32(w[0][:]), ALU.subtract)

    def part(self, part):
        self.c.nc.scalar.activation(rows(self.k_rows, part), self.rest[:], ACT.Copy).then_inc(self.part_done, 1)

    def on_vector(self, dve, n):
        nc, c = self.c.nc, self.c
        step = c.steps.on(dve)
        kf = c.kf[:].rearrange("p t (h d) -> p (t h) d", d=HD)
        if n == 0:
            step.after(nc.vector.tensor_reduce(self.sk[:], kf, AX.X, ALU.max, apply_absolute_value=True))
        elif n == 1:
            step.after(nc.vector.tensor_scalar(self.sk[:], self.sk[:], 1.0 / 127.0, 1e-8, ALU.mult, ALU.max))
            step.after(nc.vector.reciprocal(self.inv[:], self.sk[:]))
        elif n == 2:
            step.after(nc.vector.tensor_tensor(self.ints[:], kf, spread(self.inv[:]), ALU.mult))
        elif n == 3:
            step.after(nc.vector.tensor_scalar(self.k_ints[:], self.ints[:], 127.0, -127.0, ALU.min, ALU.max))
        elif n == self.LATE:
            nc.vector.tensor_tensor(self.rest[:], self.k_ints[:], spread(self.sk[:]), ALU.mult).then_inc(
                self.rest_ready, 1)
        elif n == self.LATE + 1:
            step.after(nc.vector.tensor_reduce(self.sv[:], c.vf[:], AX.X, ALU.max, apply_absolute_value=True))
        elif n == self.LATE + 2:
            dve.wait_ge(self.part_done, 1)
            nc.vector.tensor_tensor(self.rest[:], self.rest[:], rows(self.k_rows, 0), ALU.subtract).then_inc(
                self.rest_ready, 1)
        elif n == self.LATE + 3:
            step.after(nc.vector.tensor_scalar(self.sv[:], self.sv[:], 1.0 / 127.0, 1e-8, ALU.mult, ALU.max))
            nc.vector.reciprocal(self.inv_v[:], self.sv[:]).then_inc(self.inv_v_ready, 1)
        elif n == self.LATE + 4:
            dve.wait_ge(self.part_done, 2)
            nc.vector.tensor_tensor(self.rest[:], self.rest[:], rows(self.k_rows, 1), ALU.subtract).then_inc(
                self.rest_ready, 1)
        elif n == self.LATE + 5:
            dve.wait_ge(self.v_rounded, NC)
            step.after(nc.vector.tensor_scalar(self.v_cols[:], self.v_ints[:], 127.0, -127.0, ALU.min, ALU.max))

    def on_scalar(self, act, n):
        if n == 2:
            act.wait_ge(self.loaded, 48)
            for m, w in enumerate((self.wq, self.wp)):
                self.c.nc.scalar.activation(w[0][:], self.w_raw[:, :, m * D:(m + 1) * D],
                                            ACT.Copy).then_inc(self.w_hi, 1)
        elif n == self.LATE + 1:
            act.wait_ge(self.rest_ready, 1)
            self.part(0)
        elif n == self.LATE + 3:
            act.wait_ge(self.rest_ready, 2)
            self.part(1)
        elif n == self.LATE + 4:
            act.wait_ge(self.inv_v_ready, 1)
            for ch in range(NC):
                self.c.nc.scalar.activation(self.v_ints[:, ch, :], self.c.vf[:, ch, :], ACT.Copy,
                                            scale=self.inv_v[:, ch:ch + 1]).then_inc(self.v_rounded, 1)


class Operands:
    pass


def quantised_attention(c, keys_values):
    with ExitStack() as ctx:
        a = Operands()
        a.wp, a.bias_p = keys_values.wp, keys_values.bias_p
        row_statistics(c, c.x, begun=True)
        norm_to_feature_major(c, "qa_turn", c.x, c.rstd, c.shift)
        a.sq = c.sb("qa_sq", [P, NT, H], ctx=ctx)
        a.sv = keys_values.sv
        a.q_parts = c.sb("qa_q_parts", [P, NPAIR, T], BF16, ctx=ctx)
        a.k_parts = c.sb("qa_k_parts", [P, NPAIR, T], BF16, ctx=ctx)
        a.v_int = c.sb("qa_v_int", [P, NT, D], BF16, ctx=ctx)
        quantise(c, a, keys_values)
        a.aT = [c.sb(f"qa_aT{x}", [P, NC, T], F32R, ctx=ctx) for x in range(2)]
        attend(c, a)
        project_out(c, a)


def quantise(c, a, keys_values):
    nc = c.nc
    with ExitStack() as ctx:
        wq = keys_values.wq
        q_rows = c.sb("qa_q_rows", [P, NT, H, 4, HD], BF16, ctx=ctx)
        k_rows, v_cols = keys_values.k_rows, keys_values.v_cols
        qf = c.sb("qa_qf", [P, NT * H, HD], ctx=ctx)
        q_ints = c.sb("qa_q_ints", [P, NT * H, HD], I16, ctx=ctx)
        inv = c.sb("qa_inv_scale", [P, NT * H], ctx=ctx)
        bank = [c.ps(f"qa_bank{k}", [P, HALF], ctx=ctx) for k in range(4)]
        slots = [c.ps(f"qa_ps_slot{k}", [P, T], BF16, ctx=ctx) for k in range(4)]
        q_done = c.sem("qa_q_done")
        q_rows_ready = c.sem("qa_q_rows_ready")
        zeroed = c.sem("qa_zeroed")
        turned, by_act, by_dve = c.sem("qa_turned"), c.sem("qa_turned_act"), c.sem("qa_turned_dve")
        sq = a.sq[:].rearrange("p t h -> p (t h)")

        groups = [("v", n) for n in range(NC)] + [("k", n) for n in range(NPAIR)] + [("q", n) for n in range(NPAIR)]
        dve_groups = [g for g, (kind, n) in enumerate(groups) if kind == "q" and n % 4]
        act_groups = [g for g in range(len(groups)) if g not in dve_groups]

        def source(kind, n, t):
            if kind == "v":
                return v_cols[:, n, t * P:(t + 1) * P]
            return (q_rows if kind == "q" else k_rows)[:, t, 2 * n:2 * n + 2].rearrange("p h s d -> p (h s d)")

        def target(kind, n):
            if kind == "v":
                return a.v_int[:, :, n * P:(n + 1) * P]
            return (a.q_parts if kind == "q" else a.k_parts)[:, n, :].rearrange("p (t n) -> p t n", t=NT)

        def slot(g):
            return slots[g % 4][:].rearrange("p (t n) -> p t n", t=NT)

        with nc.Block() as block:

            @block.gpsimd
            def _(pool):
                nc.gpsimd.memset(rows(k_rows, 3), 0.0).then_inc(zeroed, 1)
                nc.gpsimd.memset(rows(q_rows, 3), 0.0).then_inc(zeroed, 1)

            @block.scalar
            def _(act):
                def evacuate(g):
                    act.wait_ge(turned, g + 1)
                    nc.scalar.activation(target(*groups[g]), slot(g), ACT.Copy).then_inc(by_act, 1)

                keys_values.part(2)
                for g in act_groups:
                    evacuate(g)

            @block.tensor
            def _(pe):
                for t in range(NT):
                    dst = bank[t // 2][:, (t % 2) * D:(t % 2 + 1) * D]
                    for n, (x, y) in enumerate(PASSES):
                        for ch in range(NC):
                            ins = nc.tensor.matmul(dst, c.fT[x][:, ch, t * P:(t + 1) * P], wq[y][:, ch, :],
                                                   start=(n + ch == 0), stop=(n == 2 and ch == NC - 1))
                    if t % 2:
                        ins.then_inc(q_done, 1)
                for g, (kind, n) in enumerate(groups):
                    if g >= 4:
                        if g - 4 in act_groups:
                            pe.wait_ge(by_act, act_groups.index(g - 4) + 1)
                        else:
                            pe.wait_ge(by_dve, dve_groups.index(g - 4) + 1)
                    if n == 0:
                        if kind == "k":
                            pe.wait_ge(zeroed, 1)
                            pe.wait_ge(keys_values.part_done, 3)
                        elif kind == "q":
                            pe.wait_ge(zeroed, 2)
                            pe.wait_ge(q_rows_ready, 3)
                    for t in range(NT):
                        ins = nc.tensor.transpose(slots[g % 4][:, t * P:(t + 1) * P], source(kind, n, t),
                                                  c.ident_bf[:])
                    ins.then_inc(turned, 1)

            @block.vector
            def _(dve):
                step = c.steps.on(dve)

                factor = HD ** -0.5
                for half in range(2):
                    some = slice(half * NT * H // 2, (half + 1) * NT * H // 2)
                    for j in range(2 * half, 2 * half + 2):
                        dve.wait_ge(q_done, j + 1)
                        dst = qf[:, j * 2 * H:(j + 1) * 2 * H, :].rearrange("p (t h) d -> p t (h d)", t=2)
                        ins = nc.vector.tensor_tensor(dst, bank[j][:].rearrange("p (t n) -> p t n", t=2),
                                                      keys_values.bias_q[:].unsqueeze(1).to_broadcast([P, 2, D]),
                                                      ALU.add)
                    step.after(ins)
                    step.after(nc.vector.tensor_reduce(sq[:, some], qf[:, some], AX.X, ALU.max,
                                                       apply_absolute_value=True))
                    step.after(nc.vector.tensor_scalar(sq[:, some], sq[:, some], factor / 127.0, 1e-8, ALU.mult,
                                                       ALU.max))
                    step.after(nc.vector.reciprocal(inv[:, some], sq[:, some]))
                    step.after(nc.vector.tensor_scalar(inv[:, some], inv[:, some], factor, None, ALU.mult))
                    step.after(nc.vector.tensor_tensor(q_ints[:, some], qf[:, some],
                                                       inv[:, some].unsqueeze(2).to_broadcast([P, NT * H // 2, HD]),
                                                       ALU.mult))
                for part in range(3):
                    nc.vector.tensor_scalar(rows(q_rows, part), q_ints[:], 127.0, -127.0, ALU.min,
                                            ALU.max).then_inc(q_rows_ready, 1)
                for g in dve_groups:
                    dve.wait_ge(turned, g + 1)
                    nc.vector.tensor_copy(target(*groups[g]), slot(g)).then_inc(by_dve, 1)


def attend(c, a):
    nc = c.nc
    LAG_T, LAG_V = 2, 4
    with ExitStack() as ctx:
        q_now = c.sb("qa_q_now", [P, NPAIR, P], BF16, ctx=ctx)
        e = [c.sb(f"qa_e{k}", [P, T], I16, ctx=ctx) for k in range(4)]
        pT = [c.sb(f"qa_pT{k}", [P, T], BF16, ctx=ctx) for k in range(4)]
        top = c.sb("qa_top", [P, 4], ctx=ctx)
        shift = c.sb("qa_shift", [P, 4], ctx=ctx)
        total = c.sb("qa_total", [P, NT, H], ctx=ctx)
        inv = c.sb("qa_inv", [P, H], ctx=ctx)
        at = c.sb("qa_at", [P, H, HD], ctx=ctx)
        dummy = c.sb("qa_dummy", [P, 1], ctx=ctx)
        started = c.sb("qa_started", [P, 1], ctx=ctx)
        ps_s = [c.ps(f"qa_s{k}", [P, T], ctx=ctx) for k in range(2)]
        ps_t = [c.ps(f"qa_t{k}", [P, T], BF16, ctx=ctx) for k in range(2)]
        ps_o = c.ps("qa_o", [P, H, HD], ctx=ctx)
        ps_a = c.ps("qa_a", [P, NC, P], ctx=ctx)
        q_ready = c.sem("qa_q_ready")
        q_first = c.sem("qa_q_first")
        s_done = c.sem("qa_s_done")
        top_done = c.sem("qa_top_done")
        shift_done = c.sem("qa_shift_done")
        exp_done = c.sem("qa_exp_done")
        t_done = c.sem("qa_t_done")
        out_dve, out_act = c.sem("qa_out_dve"), c.sem("qa_out_act")
        pv_done = c.sem("qa_pv_done")
        inv_done = c.sem("qa_inv_done")
        at_done = c.sem("qa_at_done")
        a_turned = c.sem("qa_a_turned")
        a_hi = c.sem("qa_a_hi")
        a_lo = c.sem("qa_a_lo")

        def tiles(engine, body):
            body(0, True)
            with engine.Fori(0, NT - 1) as i:
                body(i + 1, False)

        def tokens(t):
            return slice(t * P, (t + 1) * P) if isinstance(t, int) else bass.ds(t * P, P)

        with nc.Block() as block:

            @block.gpsimd
            def _(pool):
                def body(t, first):
                    for half in range(0 if first else 2):
                        pool.wait_ge(s_done, t * H - (H // 2) * (1 - half))
                        heads = slice(half * NPAIR // 2, (half + 1) * NPAIR // 2)
                        nc.gpsimd.tensor_copy(q_now[:, heads], a.q_parts[:, heads, tokens(t)]).then_inc(q_ready, 1)

                tiles(pool, body)

            @block.tensor
            def _(pe):
                def scores(t, h):
                    pe.wait_ge(exp_done, t * H + h + 1)
                    r0 = (h % 2) * SLOT
                    for half in range(2):
                        ins = nc.tensor.matmul(ps_s[h % 2][:, half * HALF:(half + 1) * HALF],
                                               q_now[r0:r0 + 3 * HD, h // 2, :],
                                               a.k_parts[r0:r0 + 3 * HD, h // 2, half * HALF:(half + 1) * HALF],
                                               start=True, stop=True)
                    ins.then_inc(s_done, 1)

                def turn(t, h):
                    pe.wait_ge(exp_done, t * H + h + 3)
                    for n in range(NT):
                        ins = nc.tensor.transpose(ps_t[h % 2][:, n * P:(n + 1) * P],
                                                  e[h % 4][:, n * P:(n + 1) * P].bitcast(BF16), c.ident_bf[:])
                    ins.then_inc(t_done, 1)

                def weigh(t, h):
                    takes = ACT_TAKES if h in ACT_TAKES else DVE_TAKES
                    pe.wait_ge(out_act if h in ACT_TAKES else out_dve, t * len(takes) + (takes.index(h) + 1))
                    if h == 0 and not (isinstance(t, int) and t == 0):
                        pe.wait_ge(at_done, t)
                    for n in range(NT):
                        ins = nc.tensor.matmul(ps_o[:, h, :], pT[h % 4][:, n * P:(n + 1) * P],
                                               a.v_int[:, n, h * HD:(h + 1) * HD], start=(n == 0), stop=(n == NT - 1))
                    if h == H - 1:
                        ins.then_inc(pv_done, 1)

                def turn_output(t):
                    pe.wait_ge(at_done, t + 1)
                    pe.wait_ge(a_lo, t + 1)
                    for ch in range(NC):
                        ins = nc.tensor.transpose(ps_a[:, ch, :],
                                                  at[:, 8 * ch:8 * ch + 8, :].rearrange("p h d -> p (h d)"),
                                                  c.ident[:])
                    ins.then_inc(a_turned, 1)

                def lagging(t, s, lag, work):
                    if s >= lag:
                        work(t, s - lag)
                    elif not (isinstance(t, int) and t == 0):
                        work(t - 1, H + s - lag)

                def body(t, first):
                    for h in range(H):
                        if h % (H // 2) == 0:
                            if first:
                                pe.wait_ge(q_first, 1)
                            else:
                                pe.wait_ge(q_ready, t * 2 + (h // (H // 2) - 1))
                        scores(t, h)
                        lagging(t, h, LAG_V, weigh)
                        lagging(t, h, LAG_T, turn)
                        if h == 5 and not first:
                            turn_output(t - 1)

                tiles(pe, body)
                for s in range(H, H + LAG_V):
                    weigh(NT - 1, s - LAG_V)
                    if s - LAG_T < H:
                        turn(NT - 1, s - LAG_T)
                turn_output(NT - 1)

            @block.vector
            def _(dve):
                def invert(t):
                    dve.wait_ge(exp_done, t * H + (H + 2))
                    nc.vector.reciprocal(inv[:], total[:, t, :]).then_inc(inv_done, 1)

                def finish(t):
                    dve.wait_ge(inv_done, t + 1)
                    dve.wait_ge(pv_done, t + 1)
                    nc.vector.tensor_tensor(at[:], ps_o[:], inv[:].unsqueeze(2).to_broadcast([P, H, HD]),
                                            ALU.mult).then_inc(at_done, 1)

                def split_lo(t):
                    dve.wait_ge(a_hi, t + 1)
                    for ch in range(NC):
                        ins = nc.vector.scalar_tensor_tensor(out=a.aT[1][:, ch, tokens(t)], in0=ps_a[:, ch, :],
                                                             scalar=a.sv[:, ch:ch + 1],
                                                             in1=f32(a.aT[0][:, ch, tokens(t)]), op0=ALU.mult,
                                                             op1=ALU.subtract)
                    ins.then_inc(a_lo, 1)

                def take(t, h):
                    dve.wait_ge(t_done, t * H + (h + 1))
                    nc.vector.tensor_copy(pT[h % 4][:], ps_t[h % 2][:].bitcast(I16)).then_inc(out_dve, 1)

                def body(t, first):
                    for h in range(H):
                        if h == 4 and not first:
                            finish(t - 1)
                        dve.wait_ge(s_done, t * H + (h + 1))
                        nc.vector.tensor_reduce(top[:, h % 4:h % 4 + 1], ps_s[h % 2][:], AX.X, ALU.max,
                                                negate=True).then_inc(top_done, 1)
                        dve.wait_ge(top_done, t * H + (h + 1))
                        nc.vector.tensor_scalar(shift[:, h % 4:h % 4 + 1], top[:, h % 4:h % 4 + 1],
                                                a.sq[:, t, h:h + 1], LN255, ALU.mult, ALU.add).then_inc(shift_done, 1)
                        if (h - 2) % H in DVE_TAKES and not (first and h < 2):
                            take(t if h >= 2 else t - 1, (h - 2) % H)
                        if h == 3 and not first:
                            invert(t - 1)
                        if h == 7 and not first:
                            split_lo(t - 1)

                nc.vector.memset(started[:], 0.0).then_inc(a_lo, 1)
                nc.vector.tensor_copy(q_now[:], a.q_parts[:, :, 0:P]).then_inc(q_first, 1)
                tiles(dve, body)
                for h in (H - 2, H - 1):
                    if h in DVE_TAKES:
                        take(NT - 1, h)
                invert(NT - 1)
                finish(NT - 1)
                split_lo(NT - 1)

            @block.scalar
            def _(act):
                nc.scalar.activation(dummy[:], c.ones[:, 0:1], ACT.Exp).then_inc(exp_done, 2)

                def take(t, h):
                    act.wait_ge(t_done, t * H + (h + 1))
                    nc.scalar.activation(pT[h % 4][:], ps_t[h % 2][:].bitcast(I16), ACT.Copy).then_inc(out_act, 1)

                def split_hi(t):
                    act.wait_ge(a_turned, t + 1)
                    for ch in range(NC):
                        ins = nc.scalar.activation(a.aT[0][:, ch, tokens(t)], ps_a[:, ch, :], ACT.Copy,
                                                   scale=a.sv[:, ch:ch + 1])
                    ins.then_inc(a_hi, 1)

                def body(t, first):
                    for h in range(H):
                        act.wait_ge(shift_done, t * H + (h + 1))
                        nc.scalar.activation(e[h % 4][:], ps_s[h % 2][:], ACT.Exp, bias=shift[:, h % 4:h % 4 + 1],
                                             scale=a.sq[:, t, h:h + 1],
                                             accum_out=total[:, t, h:h + 1]).then_inc(exp_done, 1)
                        if (h - 2) % H in ACT_TAKES and not (first and h < 2):
                            take(t if h >= 2 else t - 1, (h - 2) % H)
                        if h == 6 and not first:
                            split_hi(t - 1)

                tiles(act, body)
                for h in (H - 2, H - 1):
                    if h in ACT_TAKES:
                        take(NT - 1, h)
                split_hi(NT - 1)


def project_out(c, a):
    nc = c.nc
    with ExitStack() as ctx:
        bank = [c.ps(f"qa_out{k}", [P, D], ctx=ctx) for k in range(NT)]
        done, biased, added = c.sem("qa_out_done"), c.sem("qa_out_biased"), c.sem("qa_out_added")
        with nc.Block() as block:

            @block.gpsimd
            def _(pool):
                for t in range(NT):
                    nc.gpsimd.tensor_tensor(c.x[:, t, :], c.x[:, t, :], a.bias_p[:], ALU.add).then_inc(biased, 1)

            @block.tensor
            def _(pe):
                for t in range(NT):
                    for n, (x, y) in enumerate(PASSES):
                        for ch in range(NC):
                            ins = nc.tensor.matmul(bank[t][:], a.aT[x][:, ch, t * P:(t + 1) * P], a.wp[y][:, ch, :],
                                                   start=(n + ch == 0), stop=(n == 2 and ch == NC - 1))
                    ins.then_inc(done, 1)

            @block.vector
            def _(dve):
                def bn_stats(t):
                    dve.wait_ge(added, t + 1)
                    nc.vector.bn_stats(c.bn[:, t, :], c.x[:, t, :])

                for t in range(NT):
                    dve.wait_ge(done, t + 1)
                    dve.wait_ge(biased, t + 1)
                    nc.vector.tensor_tensor(c.x[:, t, :], c.x[:, t, :], bank[t][:], ALU.add).then_inc(added, 1)
                    if t > 0:
                        bn_stats(t - 1)
                bn_stats(NT - 1)




def threshold_block(c, out):
    with ExitStack() as ctx:
        weights = ExpertWeights(c, ctx, "tb_moe", 32)
        row_statistics(c, c.x, meanwhile=weights.load_first, begun=True)
        norm_to_feature_major(c, "tb_turn", c.x, c.rstd, c.shift)
        route(c, "tb_route", 32, 8, weights, threshold=0.8)
        experts(c, "tb_moe", L1_CHUNKS, weights)
    add_feature_major(c, "tb_out", c.out_t, c.x, out=out)


def build(nc, dram, out):
    with ExitStack() as ctx:
        c = Core(nc, ctx, dram)
        c.x = c.sb("x_res", [P, NT, D])
        c.ident = c.sb("ident_sb", [P, P])
        c.ident_bf = c.sb("ident_bf", [P, P], BF16)
        c.ones = c.sb("ones", [P, P])
        c.vecs = c.sb("vecs_sb", [P, 3 * NC])
        c.bn = c.sb("bn", [P, NT, 6])
        c.mean_var = c.sb("mean_var", [P, NT, 2])
        c.stat = c.sb("stat", [P, 4, NT])
        c.rstd = c.sb("rstd", [P, NT])
        c.shift = c.sb("shift", [P, NT])
        c.rms = c.sb("rms", [P, NT])
        c.out_t = c.sb("out_t", [P, NC, T])
        c.fT = [c.sb(f"fT{x}", [P, NC, T], F32R) for x in range(2)]
        c.hid = c.sb("hid", [P, NT, D])
        c.kf = c.sb("kf", [P, NT, D])
        c.vf = c.sb("vf", [P, NC, T])
        c.route_t = c.sb("route_t", [2 * ROWS, T], F32R)
        c.scale2 = c.sb("scale2", [P, NT])
        c.shift2 = c.sb("shift2", [P, NT])
        head_attention(c)
        causal_block(c)
        with ExitStack() as of_layer_1:
            keys_values = KeysValues(c, of_layer_1)
            routed_block(c, keys_values)
            quantised_attention(c, keys_values)
        threshold_block(c, out)



def chunks(gate, up, down, sizes, n_chunks):
    rows = n_chunks * P
    pad = lambda m: np.concatenate([m, np.zeros((rows - len(m), D), np.float32)])
    turned = lambda m: pad(m).reshape(n_chunks, P, NC, P).transpose(0, 3, 2, 1).reshape(n_chunks, P, NC * P)
    of_row = np.repeat(np.arange(len(sizes)), sizes)
    select = np.zeros((P, rows), np.float32)
    for part in range(2):
        select[ROWS * part + of_row, np.arange(len(of_row))] = 1.0
    select = select.reshape(P, n_chunks, P).transpose(1, 0, 2)
    return np.concatenate([turned(gate), turned(up), pad(down).reshape(n_chunks, P, D), select], axis=2)


def arrays_of(inputs):
    a = {k: np.asarray(v) for k, v in inputs.items()}
    out = {}
    out["x"] = a["x"].reshape(NT, P, D).transpose(1, 0, 2)
    ctx_t = a["ctx_2048"].reshape(T, D)
    out["ctx_tiles"] = ctx_t.reshape(NT, P, NC, P).transpose(0, 3, 2, 1)
    out["ident"] = np.eye(P, dtype=np.float32)
    feat = lambda m: m.reshape(NC, P, -1).transpose(1, 0, 2)
    out["ha_w"] = feat(np.concatenate([a["L0_xattn_Wq"].T, a["L0_xattn_Wk"].T, a["L0_xattn_Wv"].T,
                                       a["L0_xattn_Wo"].T], axis=1))
    out["ha_bias"] = np.concatenate([a["L0_xattn_bq"], a["L0_xattn_bk"], a["L0_xattn_bv"], a["L0_xattn_bo"]])[None]
    cols = np.concatenate([a["L0_ffn_ln1_w"].reshape(NC, P), a["L0_ffn_ln2_w"].reshape(NC, P)])
    out["vecs"] = np.concatenate([cols.T, a["L1_xattn_bkv"][D:].reshape(NC, P).T], axis=1)
    out["qa_wkv"] = feat(a["L1_xattn_Wkv"])
    out["qa_bias_k"] = a["L1_xattn_bkv"][None, :D]
    out["qa_w"] = feat(np.concatenate([a["L1_xattn_Wq"], a["L1_xattn_Wp"]], axis=1))
    out["qa_bias_q"] = np.broadcast_to(a["L1_xattn_bq"], (P, D))
    out["qa_bias_p"] = np.broadcast_to(a["L1_xattn_bp"], (P, D))
    head_rows = lambda m, step: m.reshape(NH, step, D)[:, :DH].reshape(PAIRS, 2 * DH, NC, P)
    kv = a["L0_ffn_kv_w"]
    qkv = np.stack([head_rows(a["L0_ffn_q_w"], QHD), head_rows(kv[:NH * DH], DH),
                    head_rows(kv[NH * DH:2 * NH * DH], DH)])
    out["ca_w"] = qkv.transpose(1, 4, 0, 3, 2)
    out["ca_wo"] = a["L0_ffn_o_w"].T.reshape(PAIRS, 2, DH, D).transpose(0, 2, 1, 3)
    out["mask"] = np.triu(np.full((P, P), -1e9, np.float32), 1)
    w1, w2, sh = a["L0_ffn_w1"], a["L0_ffn_w2"], a["L0_ffn_sh_gu_w"]
    out["rb_moe_gate"] = feat(a["L0_ffn_gate_w"].T)
    out["rb_moe_w"] = chunks(np.concatenate([w1[:, :176].reshape(-1, D), sh[:352]]),
                             np.concatenate([w1[:, 176:].reshape(-1, D), sh[352:]]),
                             np.concatenate([w2.transpose(0, 2, 1).reshape(-1, D), a["L0_ffn_sh_down_w"].T]),
                             [176] * 16 + [352], L0_CHUNKS)
    gu, dn = a["L1_ffn_gate_up_proj"], a["L1_ffn_down_proj"]
    out["tb_moe_gate"] = feat(a["L1_ffn_gate_weight"].T)
    out["tb_moe_w"] = chunks(gu[:, :96].reshape(-1, D), gu[:, 96:].reshape(-1, D),
                             dn.transpose(0, 2, 1).reshape(-1, D), [96] * 32, L1_CHUNKS)
    return {k: np.ascontiguousarray(v) for k, v in out.items()}


def kernel(**inputs):
    import concourse.bacc as bacc
    from concourse.bass_utils import run_bass_kernel_spmd

    nc = bacc.Bacc("TRN2", target_bir_lowering=False, num_devices=1)
    arrays = arrays_of(inputs)
    dram = {n: nc.dram_tensor("in_" + n, v.shape, mybir.dt.from_np(v.dtype), kind="ExternalInput").ap()
            for n, v in arrays.items()}
    out = nc.dram_tensor("out", (P, NT, D), F32, kind="ExternalOutput").ap()
    build(nc, dram, out)
    r = run_bass_kernel_spmd(nc, [{"in_" + n: v for n, v in arrays.items()}], core_ids=[0])
    y = r.results[0]["out"]
    return np.ascontiguousarray(y.transpose(1, 0, 2)).reshape(B, S, D)
```
